# Optimizing a Trainium2 kernel written in Bass

```python
import numpy as np
import jax
import jax.numpy as jnp

def _softmax(x, axis=-1):
    return jax.nn.softmax(x, axis=axis)
def _gelu(x):
    return jax.nn.gelu(x, approximate=True)
def _silu(x):
    return jax.nn.silu(x)
def _sigmoid(x):
    return jax.nn.sigmoid(x)
def _layernorm(x, axis=-1, eps=1e-5):
    m = jnp.mean(x, axis=axis, keepdims=True)
    v = jnp.var(x, axis=axis, keepdims=True)
    return (x - m) / jnp.sqrt(v + eps)
def _scatter_add(tgt, idx, src, axis=0):
    return tgt.at[idx].add(src)
def _segment_sum(src, seg, n):
    return jax.ops.segment_sum(src, seg, n)

kernel_name = 'mk_dlrm_tower_d1_rec_783abb'

def setup_inputs(seed: int = 0):
    np.random.seed(seed)
    _w = jnp.asarray
    def _rec_inputs():
        import jax
        import jax.numpy as jnp
        _tk = jax.random.key(seed)
        ids = jnp.stack([jax.random.randint(jax.random.fold_in(_tk, 200 + f), (1024,), 0, v, jnp.int32) for f, v in enumerate([10000, 100000, 10000, 100000])], axis=1)
        tbl_0 = 0.05 * jax.random.normal(jax.random.fold_in(_tk, 500 + 0), (10000, 4), jnp.float32)
        tbl_1 = 0.05 * jax.random.normal(jax.random.fold_in(_tk, 500 + 1), (100000, 4), jnp.float32)
        tbl_2 = 0.05 * jax.random.normal(jax.random.fold_in(_tk, 500 + 2), (10000, 4), jnp.float32)
        tbl_3 = 0.05 * jax.random.normal(jax.random.fold_in(_tk, 500 + 3), (100000, 4), jnp.float32)
        _rk = jax.random.fold_in(_tk, 7)
        r_x = 7.22013e-05 + 1.00017 * jax.random.normal(jax.random.fold_in(_rk, 101), (1024, 2048), jnp.float32)
        W_top1 = 0.0197642 * jax.random.normal(jax.random.fold_in(_tk, 801), (2560, 512), jnp.float32)
        W_top2 = 0.0441942 * jax.random.normal(jax.random.fold_in(_tk, 802), (512, 256), jnp.float32)
        W_top3 = 0.0625 * jax.random.normal(jax.random.fold_in(_tk, 803), (256, 1), jnp.float32)
        b_top1 = jnp.zeros((512,), jnp.float32)
        b_top2 = jnp.zeros((256,), jnp.float32)
        return r_x, ids, tbl_0, tbl_1, tbl_2, tbl_3, W_top1, b_top1, W_top2, b_top2, W_top3
    r_x, ids, tbl_0, tbl_1, tbl_2, tbl_3, W_top1, b_top1, W_top2, b_top2, W_top3 = _rec_inputs()
    def _L0_rec_setup():
        import jax, jax.numpy as jnp
        import numpy as np
        B, IN, HID, D, N, OUT = (4096, 2048, 2048, 512, 4, 512)
        H = 8
        HD = D // H

        def _ln(x, g, b):
            m = x.mean(-1, keepdims=True)
            v = ((x - m) ** 2).mean(-1, keepdims=True)
            return (x - m) / jnp.sqrt(v + 1e-05) * g + b
        key = jax.random.key(seed)
        ks = jax.random.split(key, 32)

        def nrm(k, shape, scale=0.02):
            return jax.random.normal(k, shape, jnp.float32) * scale
        inp = {}
        inp['x'] = jax.random.normal(ks[0], (B, IN), jnp.float32)
        inp['strength'] = jax.random.uniform(ks[1], (B, N, N), jnp.float32)
        for t, i in (('er', 2), ('ei', 4)):
            inp[t + '_W1'] = nrm(ks[i], (HID, IN))
            inp[t + '_b1'] = jnp.zeros((HID,), jnp.float32)
            inp[t + '_g1'] = jnp.ones((HID,), jnp.float32)
            inp[t + '_be1'] = jnp.zeros((HID,), jnp.float32)
            inp[t + '_W2'] = nrm(ks[i + 1], (N * D, HID))
            inp[t + '_b2'] = jnp.zeros((N * D,), jnp.float32)
        names = ['Wq_r', 'Wq_i', 'Wk_r', 'Wk_i', 'Wv_r', 'Wv_i', 'Wo_r', 'Wo_i']
        for j, nm in enumerate(names):
            inp[nm] = nrm(ks[6 + j], (D, D))
            inp['b' + nm[1:]] = jnp.zeros((D,), jnp.float32)
        inp['int_Wr'] = jnp.tile(jnp.eye(D, dtype=jnp.float32)[None], (N, 1, 1))
        inp['int_Wi'] = jnp.zeros((N, D, D), jnp.float32)
        inp['meas_Mr'] = nrm(ks[20], (OUT, D), 1.0 / np.sqrt(D))
        inp['meas_Mi'] = nrm(ks[21], (OUT, D), 1.0 / np.sqrt(D))
        inp['post_W'] = nrm(ks[22], (OUT, OUT))
        inp['post_b'] = jnp.zeros((OUT,), jnp.float32)
        inp['post_g'] = jnp.ones((OUT,), jnp.float32)
        inp['post_be'] = jnp.zeros((OUT,), jnp.float32)
        return inp
    _L0_rec_all = _L0_rec_setup()
    _L0_rec_in = {k: v for k, v in _L0_rec_all.items() if k in ('er_W1', 'er_b1', 'er_g1', 'er_be1', 'er_W2', 'er_b2', 'ei_W1', 'ei_b1', 'ei_g1', 'ei_be1', 'ei_W2', 'ei_b2', 'Wq_r', 'bq_r', 'Wq_i', 'bq_i', 'Wk_r', 'bk_r', 'Wk_i', 'bk_i', 'Wv_r', 'bv_r', 'Wv_i', 'bv_i', 'Wo_r', 'bo_r', 'Wo_i', 'bo_i', 'int_Wr', 'int_Wi', 'meas_Mr', 'meas_Mi', 'post_W', 'post_b', 'post_g', 'post_be', )}
    del _L0_rec_all

    return {
        "r_x": r_x,
        "ids": ids,
        "tbl_0": tbl_0,
        "tbl_1": tbl_1,
        "tbl_2": tbl_2,
        "tbl_3": tbl_3,
        "W_top1": W_top1,
        "b_top1": b_top1,
        "W_top2": W_top2,
        "b_top2": b_top2,
        "W_top3": W_top3,
        "L0_rec_er_W1": _L0_rec_in["er_W1"],
        "L0_rec_er_b1": _L0_rec_in["er_b1"],
        "L0_rec_er_g1": _L0_rec_in["er_g1"],
        "L0_rec_er_be1": _L0_rec_in["er_be1"],
        "L0_rec_er_W2": _L0_rec_in["er_W2"],
        "L0_rec_er_b2": _L0_rec_in["er_b2"],
        "L0_rec_ei_W1": _L0_rec_in["ei_W1"],
        "L0_rec_ei_b1": _L0_rec_in["ei_b1"],
        "L0_rec_ei_g1": _L0_rec_in["ei_g1"],
        "L0_rec_ei_be1": _L0_rec_in["ei_be1"],
        "L0_rec_ei_W2": _L0_rec_in["ei_W2"],
        "L0_rec_ei_b2": _L0_rec_in["ei_b2"],
        "L0_rec_Wq_r": _L0_rec_in["Wq_r"],
        "L0_rec_bq_r": _L0_rec_in["bq_r"],
        "L0_rec_Wq_i": _L0_rec_in["Wq_i"],
        "L0_rec_bq_i": _L0_rec_in["bq_i"],
        "L0_rec_Wk_r": _L0_rec_in["Wk_r"],
        "L0_rec_bk_r": _L0_rec_in["bk_r"],
        "L0_rec_Wk_i": _L0_rec_in["Wk_i"],
        "L0_rec_bk_i": _L0_rec_in["bk_i"],
        "L0_rec_Wv_r": _L0_rec_in["Wv_r"],
        "L0_rec_bv_r": _L0_rec_in["bv_r"],
        "L0_rec_Wv_i": _L0_rec_in["Wv_i"],
        "L0_rec_bv_i": _L0_rec_in["bv_i"],
        "L0_rec_Wo_r": _L0_rec_in["Wo_r"],
        "L0_rec_bo_r": _L0_rec_in["bo_r"],
        "L0_rec_Wo_i": _L0_rec_in["Wo_i"],
        "L0_rec_bo_i": _L0_rec_in["bo_i"],
        "L0_rec_int_Wr": _L0_rec_in["int_Wr"],
        "L0_rec_int_Wi": _L0_rec_in["int_Wi"],
        "L0_rec_meas_Mr": _L0_rec_in["meas_Mr"],
        "L0_rec_meas_Mi": _L0_rec_in["meas_Mi"],
        "L0_rec_post_W": _L0_rec_in["post_W"],
        "L0_rec_post_b": _L0_rec_in["post_b"],
        "L0_rec_post_g": _L0_rec_in["post_g"],
        "L0_rec_post_be": _L0_rec_in["post_be"],
    }

def reference(r_x, ids, tbl_0, tbl_1, tbl_2, tbl_3, W_top1, b_top1, W_top2, b_top2, W_top3, L0_rec_er_W1, L0_rec_er_b1, L0_rec_er_g1, L0_rec_er_be1, L0_rec_er_W2, L0_rec_er_b2, L0_rec_ei_W1, L0_rec_ei_b1, L0_rec_ei_g1, L0_rec_ei_be1, L0_rec_ei_W2, L0_rec_ei_b2, L0_rec_Wq_r, L0_rec_bq_r, L0_rec_Wq_i, L0_rec_bq_i, L0_rec_Wk_r, L0_rec_bk_r, L0_rec_Wk_i, L0_rec_bk_i, L0_rec_Wv_r, L0_rec_bv_r, L0_rec_Wv_i, L0_rec_bv_i, L0_rec_Wo_r, L0_rec_bo_r, L0_rec_Wo_i, L0_rec_bo_i, L0_rec_int_Wr, L0_rec_int_Wi, L0_rec_meas_Mr, L0_rec_meas_Mi, L0_rec_post_W, L0_rec_post_b, L0_rec_post_g, L0_rec_post_be):
    import jax
    import jax.numpy as jnp
    def _L0_rec_ref(x, strength, er_W1, er_b1, er_g1, er_be1, er_W2, er_b2, ei_W1, ei_b1, ei_g1, ei_be1, ei_W2, ei_b2, Wq_r, bq_r, Wq_i, bq_i, Wk_r, bk_r, Wk_i, bk_i, Wv_r, bv_r, Wv_i, bv_i, Wo_r, bo_r, Wo_i, bo_i, int_Wr, int_Wi, meas_Mr, meas_Mi, post_W, post_b, post_g, post_be):
        import jax, jax.numpy as jnp
        import numpy as np
        B, IN, HID, D, N, OUT = (4096, 2048, 2048, 512, 4, 512)
        H = 8
        HD = D // H

        def _ln(x, g, b):
            m = x.mean(-1, keepdims=True)
            v = ((x - m) ** 2).mean(-1, keepdims=True)
            return (x - m) / jnp.sqrt(v + 1e-05) * g + b
        Bsz = x.shape[0]

        def enc(W1, b1, g, be, W2, b2):
            h = jax.nn.gelu(_ln(x @ W1.T + b1, g, be), approximate=False)
            return (h @ W2.T + b2).reshape(Bsz, N, D)
        sr = enc(er_W1, er_b1, er_g1, er_be1, er_W2, er_b2)
        si = enc(ei_W1, ei_b1, ei_g1, ei_be1, ei_W2, ei_b2)

        def heads(t):
            return t.reshape(Bsz, N, H, HD).transpose(0, 2, 1, 3)
        qr = heads(sr @ Wq_r.T + bq_r)
        qi = heads(si @ Wq_i.T + bq_i)
        kr = heads(sr @ Wk_r.T + bk_r)
        ki = heads(si @ Wk_i.T + bk_i)
        vr = heads(sr @ Wv_r.T + bv_r)
        vi = heads(si @ Wv_i.T + bv_i)
        ar = jnp.einsum('bhnd,bhmd->bhnm', qr, kr) + jnp.einsum('bhnd,bhmd->bhnm', qi, ki)
        ai = jnp.einsum('bhnd,bhmd->bhnm', qi, kr) - jnp.einsum('bhnd,bhmd->bhnm', qr, ki)
        mag = jnp.sqrt(ar ** 2 + ai ** 2 + 1e-08) * HD ** (-0.5)
        w = jax.nn.softmax(mag, axis=-1)
        out_r = jnp.einsum('bhnm,bhmd->bhnd', w, vr).transpose(0, 2, 1, 3).reshape(Bsz, N, D)
        out_i = jnp.einsum('bhnm,bhmd->bhnd', w, vi).transpose(0, 2, 1, 3).reshape(Bsz, N, D)
        attn_r = out_r @ Wo_r.T + bo_r
        attn_i = out_i @ Wo_i.T + bo_i
        R = jnp.einsum('bnd,ned->bne', attn_r, int_Wr) - jnp.einsum('bnd,ned->bne', attn_i, int_Wi)
        I = jnp.einsum('bnd,ned->bne', attn_r, int_Wi) + jnp.einsum('bnd,ned->bne', attn_i, int_Wr)
        Ri, Ii = (R[:, :, None, :], I[:, :, None, :])
        Rj, Ij = (R[:, None, :, :], I[:, None, :, :])
        phase = jnp.arctan2(Ii * Rj - Ri * Ij, Ri * Rj + Ii * Ij)
        f = jnp.cos(phase) * strength[..., None]
        sup_r = jnp.einsum('bijd,bjd->bd', f, R)
        sup_i = jnp.einsum('bijd,bjd->bd', f, I)
        norm = jnp.sqrt(jnp.sum(sup_r ** 2 + sup_i ** 2, axis=-1, keepdims=True) + 1e-08)
        sup_r = sup_r / norm
        sup_i = sup_i / norm
        mr = sup_r @ meas_Mr.T - sup_i @ meas_Mi.T
        mi = sup_r @ meas_Mi.T + sup_i @ meas_Mr.T
        amp = jnp.sqrt(mr ** 2 + mi ** 2)
        out = jax.nn.gelu(_ln(amp @ post_W.T + post_b, post_g, post_be), approximate=False)
        return out

    e = jnp.stack([tbl_0[ids[:, 0]], tbl_1[ids[:, 1]], tbl_2[ids[:, 2]], tbl_3[ids[:, 3]]], axis=1)
    z = _L0_rec_ref(r_x, e, L0_rec_er_W1, L0_rec_er_b1, L0_rec_er_g1, L0_rec_er_be1, L0_rec_er_W2, L0_rec_er_b2, L0_rec_ei_W1, L0_rec_ei_b1, L0_rec_ei_g1, L0_rec_ei_be1, L0_rec_ei_W2, L0_rec_ei_b2, L0_rec_Wq_r, L0_rec_bq_r, L0_rec_Wq_i, L0_rec_bq_i, L0_rec_Wk_r, L0_rec_bk_r, L0_rec_Wk_i, L0_rec_bk_i, L0_rec_Wv_r, L0_rec_bv_r, L0_rec_Wv_i, L0_rec_bv_i, L0_rec_Wo_r, L0_rec_bo_r, L0_rec_Wo_i, L0_rec_bo_i, L0_rec_int_Wr, L0_rec_int_Wi, L0_rec_meas_Mr, L0_rec_meas_Mi, L0_rec_post_W, L0_rec_post_b, L0_rec_post_g, L0_rec_post_be)
    z = z.reshape(z.shape[0], -1)
    h = jnp.concatenate([z, r_x], axis=1)
    h = jnp.maximum(h @ W_top1 + b_top1, 0.0)
    h = jnp.maximum(h @ W_top2 + b_top2, 0.0)
    y = h @ W_top3
    return y


_drawn_inputs = setup_inputs


def setup_inputs(seed=0):
    import zlib

    import numpy as np

    out = dict(_drawn_inputs(seed))
    spreads = {'b_top1': (0.0, 0.1),
     'b_top2': (0.0, 0.1),
     'L0_rec_er_b1': (0.0, 0.8),
     'L0_rec_er_g1': (1.0, 0.6),
     'L0_rec_er_be1': (0.0, 0.8),
     'L0_rec_er_b2': (0.0, 0.8),
     'L0_rec_ei_b1': (0.0, 0.8),
     'L0_rec_ei_g1': (1.0, 0.6),
     'L0_rec_ei_be1': (0.0, 0.8),
     'L0_rec_ei_b2': (0.0, 0.8),
     'L0_rec_bq_r': (0.0, 0.8),
     'L0_rec_bq_i': (0.0, 0.8),
     'L0_rec_bk_r': (0.0, 0.8),
     'L0_rec_bk_i': (0.0, 0.8),
     'L0_rec_bv_r': (0.0, 0.1),
     'L0_rec_bv_i': (0.0, 0.1),
     'L0_rec_bo_r': (0.0, 0.1),
     'L0_rec_bo_i': (0.0, 0.1),
     'L0_rec_int_Wi': (0.0, 0.1),
     'L0_rec_post_b': (0.0, 0.1),
     'L0_rec_post_g': (1.0, 0.2),
     'L0_rec_post_be': (0.0, 0.1)}
    factors = {'L0_rec_Wq_r': 8.0, 'L0_rec_Wq_i': 8.0, 'L0_rec_Wk_r': 8.0, 'L0_rec_Wk_i': 8.0}
    for name, (base, spread) in spreads.items():
        noise = np.random.default_rng([zlib.crc32(name.encode()), seed]).standard_normal(out[name].shape)
        drawn = base * np.exp(spread * noise) if base else spread * noise
        out[name] = jnp.asarray(drawn.astype(out[name].dtype))
    for name, factor in factors.items():
        out[name] = (out[name] * factor).astype(out[name].dtype)
    return out
```

```python
from contextlib import ExitStack

import concourse.bass as bass
from concourse import mybir

F32 = mybir.dt.float32
F32R = mybir.dt.float32r
I32 = mybir.dt.int32
U32 = mybir.dt.uint32
ALU = mybir.AluOpType
ACT = mybir.ActivationFunctionType
AX_X = mybir.AxisListType.X

P = 128
BATCH, IN, HID, D, N, OUT, HEADS, TOP2 = 1024, 2048, 2048, 512, 4, 512, 8, 256
HD = D // HEADS
CK = D // P
TILES = BATCH // P
EPS = 1e-5



def encoders(nc, sem, dram, w_stream, x_t, enc_cols):
    KT = IN // P
    SLOTS = KT // 2
    HALVES, BH = 2, BATCH // 2
    CH = 4
    G_S1R, G_TOP, G_S1I, G_S2R, G_S2I, GROUPS = 0, 4, 5, 9, 13, 17
    PAIRS = GROUPS * SLOTS

    with ExitStack() as ctx:
        def sb(name, shape, dt=F32):
            return ctx.enter_context(nc.sbuf_tensor(name, shape, dt))

        x_hi, x_lo = sb("x_hi", [P, KT, BH], F32R), sb("x_lo", [P, KT, BH], F32R)
        h_hi, h_lo = sb("h_hi", [P, KT, BH], F32R), sb("h_lo", [P, KT, BH], F32R)
        z = sb("z", [P, KT, BH])
        w_raw = sb("w_raw", [P, 2, 2, 512])
        w_hi, w_lo = sb("w_hi", [P, 2, 2, 512], F32R), sb("w_lo", [P, 2, 2, 512], F32R)
        staged = sb("staged", [P, 2, 2, BH])
        scratch = sb("scratch", [P, 2, BH])
        colsum, rstd = sb("colsum", [P, BH]), sb("rstd", [P, BH])
        cols = sb("enc_columns", [P, 2, 4, KT])
        mean_w, eps = sb("mean_w", [P, P]), sb("eps", [P, 1])
        zeros = sb("zeros", [P, BH])
        acc = ctx.enter_context(nc.psum_tensor("acc", [P, CH, 512], F32))
        stat = ctx.enter_context(nc.psum_tensor("stat", [P, 512], F32))

        raw_landed = [sem("raw_landed0"), sem("raw_landed1")]
        x_landed, cols_landed, consts = sem("x_landed"), sem("cols_landed"), sem("p1_consts")
        hi_ready, lo_ready = sem("w_hi_ready"), sem("w_lo_ready")
        pairs_used = sem("pairs_used")
        xhi_ready, xlo_ready = sem("xhi_ready"), sem("xlo_ready")
        acc_done, drained = sem("acc_done"), sem("drained")
        summed, stats_made = sem("summed"), sem("stats_made")
        centred, squared = sem("centred"), sem("squared")
        std_made, rstd_made = sem("std_made"), sem("rstd_made")
        scaled, gelued = sem("scaled"), sem("gelued")
        hhi_ready, hlo_ready = sem("hhi_ready"), sem("hlo_ready")
        shi_ready = sem("shi_ready")
        sent = [sem("sent0"), sem("sent1")]
        block = ctx.enter_context(nc.Block())

        SUMS = 4 * (1 + KT)

        def pair(half, g, s):
            return half * PAIRS + g * SLOTS + s

        def unit(half, g, c):
            return half * (GROUPS * CH) + g * CH + c

        def sends(half, g, c):
            j = 0 if isinstance(g, int) and g == G_TOP else (g - G_S2R) * 2 + 2
            return half * 18 + j + c // 2

        def schedule(run):
            for first, last in ((0, 0), (1, 3), (4, 4), (5, 5), (6, 6), (7, 8), (9, 9), (10, 11),
                                (12, 12), (13, 13), (14, 16)):
                run(first, last)

        def kind(g):
            return "top" if g == G_TOP else ("s1" if g < G_S2R else "s2")

        def norm1(g, s):
            if g not in (G_TOP, G_S2R) or s < 2:
                return 0, ()
            cut = (0, 3, 6, 9, 12, 14, 16)
            return int(g == G_S2R), range(cut[s - 2], cut[s - 1])

        def norm2(g, s):
            e = int(g in (G_S2R + 3, G_S2I))
            if g in (G_S1I, G_S2R + 3) and s >= 2:
                return e, range(2 * s - 4, 2 * s - 2)
            if g in (G_S1I + 1, G_S2I) and s < 2:
                return e, range(12 + 2 * s, 14 + 2 * s)
            return e, ()

        @block.sync
        def _(sp):
            sp.sem_inc(sent[0], 16)
            sp.sem_inc(sent[1], 16)
            sp.dma_start(cols[:, :, :, :], enc_cols).then_inc(cols_landed, 16)

            def out(half, g):
                for c in range(CH):
                    sp.wait_ge(drained, unit(half, g, c) + 5)
                    u = c % 2
                    if isinstance(g, int) and g == G_TOP:
                        dst = dram["top_x"][c, :, bass.ts(half, BH)]
                        sp.dma_start(dst, staged[:, u, 0, :]).then_inc(sent[u], 16)
                    else:
                        dst = dram["s"][(g - G_S2R) * CH + c][:, :, bass.ts(half, BH)]
                        sp.dma_start(dst.rearrange("a p b -> p a b"), staged[:, u, :, :]).then_inc(sent[u], 16)

            def group(half, g, before):
                for s in range(SLOTS):
                    sp.wait_ge(lo_ready, pair(half, g, s) + 1)
                    sp.dma_start(w_raw[:, s % 2, :, :], w_stream[g * SLOTS + s, :, :, :]).then_inc(raw_landed[s % 2], 16)
                    if isinstance(g, int) and g == 0:
                        sp.wait_ge(xlo_ready, half * SLOTS + s + 1)
                        sp.dma_start(scratch[:, :, :],
                                     x_t[2 * s:2 * s + 2, :, bass.ts(half, BH)].rearrange("k p b -> p k b")
                                     ).then_inc(x_landed, 16)
                    if s == 2 and before in ("top", "s2"):
                        out(half, g - 1)

            with nc.sync.Fori(0, HALVES) as half:
                def run(first, last):
                    before = kind(first - 1) if first else None
                    if first == last:
                        group(half, first, before)
                    else:
                        with nc.sync.Fori(first, last + 1) as g:
                            group(half, g, before)
                schedule(run)
                out(half, GROUPS - 1)
            for u in range(2):
                sp.wait_ge(sent[u], 16 * (18 * HALVES + 1))

        @block.scalar
        def _(act):
            act.wait_ge(cols_landed, 16)
            act.wait_ge(consts, 3)

            def drain(half, g, what):
                for c in range(CH):
                    if c < CH - 1:
                        act.wait_ge(acc_done, (half * GROUPS + g) * (CH - 1) + c + 1)
                    else:
                        act.wait_ge(pairs_used, pair(half, g, SLOTS - 1) + 3)
                    if what == "top":
                        act.wait_ge(sent[c % 2], 16 * (sends(half, g, c) + 1))
                        nc.scalar.activation(staged[:, c % 2, 0, :], acc[:, c, :], ACT.Copy).then_inc(drained, 1)
                    elif what == "s2r" or what == "s2i":
                        e = int(what == "s2i")
                        col = (g - (G_S2I if e else G_S2R)) * CH + c
                        act.wait_ge(sent[c % 2], 16 * (sends(half, g, c) + 1))
                        nc.scalar.activation(staged[:, c % 2, 0, :].bitcast(F32R), acc[:, c, :], ACT.Identity,
                                             bias=cols[:, e, 3, bass.ds(col, 1)]).then_inc(shi_ready, 1)
                    else:
                        e = int(what == "s1i")
                        col = (g - (G_S1I if e else G_S1R)) * CH + c
                        if e:
                            act.wait_ge(hlo_ready, half * 32 + col + 1)
                        nc.scalar.activation(z[:, bass.ds(col, 1), :], acc[:, c:c + 1, :], ACT.Identity,
                                             bias=cols[:, e, 0, bass.ds(col, 1)]).then_inc(drained, 1)

            def group(half, g, before):
                for s in range(SLOTS):
                    u = s % 2
                    act.wait_ge(raw_landed[u], 16 * (half * (PAIRS // 2) + g * (SLOTS // 2) + s // 2 + 1))
                    act.wait_ge(pairs_used, pair(half, g, s) + 1)
                    nc.scalar.activation(w_hi[:, u, :, :], w_raw[:, u, :, :], ACT.Copy).then_inc(hi_ready, 1)
                    if isinstance(g, int) and g == 0:
                        act.wait_ge(x_landed, 16 * (half * SLOTS + s + 1))
                        nc.scalar.activation(x_hi[:, 2 * s:2 * s + 2, :], scratch[:, :, :], ACT.Copy).then_inc(xhi_ready, 1)
                    if s == 0 and before:
                        drain(half, g - 1, before)
                    if not isinstance(g, int):
                        continue
                    e, chunks = norm1(g, s)
                    for i in chunks:
                        act.wait_ge(centred, half * 32 + e * KT + i + 1)
                        if i >= 2:
                            act.wait_ge(summed, half * SUMS + (2 * e + 1) * (1 + KT) + i)
                        nc.scalar.activation(scratch[:, i % 2, :], z[:, i, :], ACT.Square).then_inc(squared, 1)
                    if g in (G_S1I, G_S2R + 3) and s == 1:
                        e = int(g != G_S1I)
                        act.wait_ge(stats_made, half * 4 + 2 * e + 3)
                        nc.scalar.activation(rstd[:, :], stat[:, :], ACT.Sqrt, bias=eps[:, :]).then_inc(std_made, 1)
                    e, chunks = norm2(g, s)
                    for i in chunks:
                        act.wait_ge(scaled, half * 32 + e * KT + i + 1)
                        nc.scalar.activation(z[:, i, :], z[:, i, :], ACT.Gelu, bias=cols[:, e, 2, i:i + 1],
                                             scale=cols[:, e, 1, i:i + 1]).then_inc(gelued, 1)
                    for i in chunks:
                        act.wait_ge(gelued, half * 32 + e * KT + i + 1)
                        nc.scalar.activation(h_hi[:, i, :], z[:, i, :], ACT.Copy).then_inc(hhi_ready, 1)

            def what(g):
                return {0: "s1r", 4: "top", 5: "s1i", 9: "s2r", 13: "s2i"}[max(b for b in (0, 4, 5, 9, 13) if b <= g)]

            with nc.scalar.Fori(0, HALVES) as half:
                def run(first, last):
                    before = what(first - 1) if first else None
                    if first == last:
                        group(half, first, before)
                    else:
                        with nc.scalar.Fori(first, last + 1) as g:
                            group(half, g, before)
                schedule(run)
                drain(half, GROUPS - 1, "s2i")

        @block.vector
        def _(dve):
            dve.wait_ge(cols_landed, 16)
            dve.sem_inc(lo_ready, 2)
            dve.sem_inc(xlo_ready, 1)
            dve.sem_inc(drained, CH)
            nc.vector.memset(mean_w[:, :], 1.0 / HID).then_inc(consts, 1)
            nc.vector.memset(eps[:, :], EPS).then_inc(consts, 1)
            nc.vector.memset(zeros[:, :], 0.0).then_inc(consts, 1)

            def group(half, g, before):
                for s in range(SLOTS):
                    u = s % 2
                    dve.wait_ge(hi_ready, pair(half, g, s) + 1)
                    nc.vector.tensor_tensor(w_lo[:, u, :, :], w_raw[:, u, :, :], w_hi[:, u, :, :].bitcast(F32),
                                            ALU.subtract).then_inc(lo_ready, 1)
                    if isinstance(g, int) and g == 0:
                        dve.wait_ge(xhi_ready, half * SLOTS + s + 1)
                        nc.vector.tensor_tensor(x_lo[:, 2 * s:2 * s + 2, :], scratch[:, :, :],
                                                x_hi[:, 2 * s:2 * s + 2, :].bitcast(F32),
                                                ALU.subtract).then_inc(xlo_ready, 1)
                    if s == 0 and before:
                        drain(half, g - 1, before)
                    if not isinstance(g, int):
                        continue
                    e, chunks = norm1(g, s)
                    if chunks and s == 2:
                        dve.wait_ge(stats_made, half * 4 + 2 * e + 2)
                    for i in chunks:
                        nc.vector.tensor_tensor(z[:, i, :], z[:, i, :], stat[:, :], ALU.subtract).then_inc(centred, 1)
                    if g in (G_S1I, G_S2R + 3) and s == 1:
                        e = int(g != G_S1I)
                        dve.wait_ge(std_made, half * 2 + e + 1)
                        nc.vector.reciprocal(rstd[:, :], rstd[:, :]).then_inc(rstd_made, 1)
                    e, chunks = norm2(g, s)
                    for i in chunks:
                        dve.wait_ge(hhi_ready, half * 32 + e * KT + i + 1)
                        nc.vector.tensor_tensor(h_lo[:, i, :], z[:, i, :], h_hi[:, i, :].bitcast(F32),
                                                ALU.subtract).then_inc(hlo_ready, 1)

            def drain(half, g, what):
                if what != "s2r" and what != "s2i":
                    return
                e = int(what == "s2i")
                for c in range(CH):
                    col = (g - (G_S2I if e else G_S2R)) * CH + c
                    dve.wait_ge(shi_ready, half * 32 + (g - G_S2R) * CH + c + 1)
                    nc.vector.scalar_tensor_tensor(
                        staged[:, c % 2, 1, :].bitcast(F32R), acc[:, c, :], cols[:, e, 3, bass.ds(col, 1)],
                        staged[:, c % 2, 0, :], ALU.add, ALU.subtract).then_inc(drained, 1)

            def what(g):
                return {0: "s1", 9: "s2r", 13: "s2i"}[max(b for b in (0, 9, 13) if b <= g)]

            with nc.vector.Fori(0, HALVES) as half:
                def run(first, last):
                    before = what(first - 1) if first else None
                    if first == last:
                        group(half, first, before)
                    else:
                        with nc.vector.Fori(first, last + 1) as g:
                            group(half, g, before)
                schedule(run)
                drain(half, GROUPS - 1, "s2i")

        @block.gpsimd
        def _(pool):
            def clear(half, n):
                pool.wait_ge(stats_made, half * 4 + n + 1)
                nc.gpsimd.tensor_tensor(colsum[:, :], zeros[:, :], zeros[:, :], ALU.add).then_inc(summed, 1)

            def add(half, n, i, src, sq=None):
                pool.wait_ge(summed, half * SUMS + n * (1 + KT) + i + 1)
                nc.gpsimd.tensor_tensor(colsum[:, :], colsum[:, :], src, ALU.add).then_inc(summed, 1)

            pool.wait_ge(consts, 3)
            with nc.gpsimd.Fori(0, HALVES) as half:
                for e, g0 in ((0, G_S1R), (1, G_S1I)):
                    clear(half, 2 * e)
                    with nc.gpsimd.Fori(0, 4) as q:
                        for c in range(CH):
                            pool.wait_ge(drained, half * (GROUPS * CH) + g0 * CH + q * CH + c + 5)
                            add(half, 2 * e, q * CH + c, z[:, bass.ds(q * CH + c, 1), :])
                    clear(half, 2 * e + 1)
                    with nc.gpsimd.Fori(0, KT // 2) as q:
                        for u in range(2):
                            pool.wait_ge(squared, half * 32 + e * KT + q * 2 + u + 1)
                            add(half, 2 * e + 1, q * 2 + u, scratch[:, u, :])
                    with nc.gpsimd.Fori(0, KT) as i:
                        pool.wait_ge(rstd_made, half * 2 + e + 1)
                        nc.gpsimd.tensor_tensor(z[:, bass.ds(i, 1), :], z[:, bass.ds(i, 1), :],
                                                rstd[:, :].unsqueeze(1), ALU.mult).then_inc(scaled, 1)

        @block.tensor
        def _(pe):
            pe.sem_inc(pairs_used, 2)
            pe.sem_inc(stats_made, 1)
            pe.wait_ge(consts, 3)

            def statistic(half, n):
                pe.wait_ge(summed, half * SUMS + (n + 1) * (1 + KT))
                nc.tensor.matmul(stat[:, :], mean_w[:, :], colsum[:, :], start=True, stop=True).then_inc(stats_made, 1)

            sums_at = {(G_TOP, 1): 0, (G_S1I, 0): 1, (G_S2R, 1): 2, (G_S2R + 3, 0): 3}

            def group(half, g, moving):
                a_hi, a_lo = moving
                for s in range(SLOTS):
                    pe.wait_ge(lo_ready, pair(half, g, s) + 3)
                    if isinstance(g, int) and g == G_S1R:
                        pe.wait_ge(xlo_ready, half * SLOTS + s + 2)
                    if isinstance(g, int) and g == G_S2R and s == 0:
                        pe.wait_ge(hlo_ready, half * 32 + KT)
                    if isinstance(g, int) and g == G_S2I:
                        pe.wait_ge(hlo_ready, half * 32 + KT + 2 * s + 2)
                    for c in range(CH):
                        if s == 0:
                            pe.wait_ge(drained, unit(half, g, c) + 1)
                        for kk in range(2):
                            k = 2 * s + kk
                            for n, (a, b) in enumerate(((w_hi, a_hi), (w_hi, a_lo), (w_lo, a_hi))):
                                last = nc.tensor.matmul(acc[:, c, :], a[:, s % 2, kk, c * P:(c + 1) * P], b[:, k, :],
                                                        start=(k == 0 and n == 0), stop=(k == KT - 1 and n == 2))
                        if s == SLOTS - 1 and c < CH - 1:
                            last.then_inc(acc_done, 1)
                    last.then_inc(pairs_used, 1)
                    if isinstance(g, int) and (g, s) in sums_at:
                        statistic(half, sums_at[g, s])

            with nc.tensor.Fori(0, HALVES) as half:
                def run(first, last):
                    moving = (x_hi, x_lo) if first < G_S2R else (h_hi, h_lo)
                    if first == last:
                        group(half, first, moving)
                    else:
                        with nc.tensor.Fori(first, last + 1) as g:
                            group(half, g, moving)
                schedule(run)



def scores(nc, sem, dram, w_proj, bias_rows):
    with ExitStack() as ctx:
        def sb(name, shape, dt=F32):
            return ctx.enter_context(nc.sbuf_tensor(name, shape, dt))

        MATS = 4
        UNITS = 2 * N * 2
        RING = 4
        w_hi = sb("qk_w_hi", [P, MATS, CK, D], F32R)
        w_lo = sb("qk_w_lo", [P, MATS, CK, D], F32R)
        bias = sb("qk_bias", [P, MATS, D])
        s_in = sb("qk_s", [P, RING, CK, 2, P], F32R)
        qk = sb("qk", [P, 2, 2, 2, N, D])
        mixed = sb("qk_mixed", [P, 2, N, D])
        prod = sb("qk_prod", [P, 3, N, D])
        dots = sb("qk_dots", [P, 3, TILES, N * N * HEADS])
        tiny = sb("qk_tiny", [P, 1])
        ps = ctx.enter_context(nc.psum_tensor("qk_ps", [P, 8, D], F32))
        w_landed, bias_landed = [sem("qk_w_landed0"), sem("qk_w_landed1")], sem("qk_bias_landed")
        w_hi_made, w_lo_made = sem("qk_w_hi_made"), sem("qk_w_lo_made")
        s_landed = [sem(f"qk_s_landed{i}") for i in range(RING)]
        s_used = sem("qk_s_used")
        made, evicted = sem("qk_made"), sem("qk_evicted")
        mixes = sem("qk_mixes")
        pooled, reduced = sem("qk_pooled"), sem("qk_reduced")
        own_product, own_reduced = sem("qk_own_product"), sem("qk_own_reduced")
        soft, acted = sem("qk_soft"), sem("qk_acted")
        kept = sem("qk_kept")
        block = ctx.enter_context(nc.Block())

        def stages(fori, run):
            run(0, None, 0)
            with fori(0, TILES // 2 - 1) as q:
                run(2 * q + 1, 2 * q, 1)
                run(2 * q + 2, 2 * q + 1, 0)
            run(TILES - 1, TILES - 2, 1)
            run(None, TILES - 1, 0)

        def mat(j, e):
            return 2 * j + e

        @block.sync
        def _(sp):
            sp.dma_start(bias[:, :, :], bias_rows[0:MATS, :].unsqueeze(0).broadcast_to([P, MATS, D])).then_inc(bias_landed, 16)
            for m in range(MATS):
                if m >= 2:
                    sp.wait_ge(w_lo_made, m - 1)
                sp.dma_start(prod[:, m % 2, :, :], w_proj[m, :, :, :].rearrange("c p o -> p c o")).then_inc(w_landed[m % 2], 16)
            with nc.sync.Fori(0, TILES) as t:
                for n in range(N):
                    for e in range(2):
                        i = 2 * n + e
                        sp.wait_ge(s_used, t * 2 * N + i + 1)
                        src = dram["s"][(e * N + n) * CK:(e * N + n + 1) * CK, :, :, bass.ts(t, P)]
                        for c in range(CK):
                            sp.dma_start(s_in[:, i % RING, c, :, :].bitcast(F32),
                                         src[c].rearrange("a p b -> p a b")).then_inc(s_landed[i % RING], 16)
            sp.wait_ge(soft, 13)
            sp.dma_start(dram["w"], dots[:, 0, :, :]).then_inc(kept, 16)
            sp.wait_ge(kept, 16)

        @block.scalar
        def _(act):
            for m in range(MATS):
                act.wait_ge(w_landed[m % 2], 16 * (m // 2 + 1))
                nc.scalar.activation(w_hi[:, m, :, :], prod[:, m % 2, :, :], ACT.Copy).then_inc(w_hi_made, 1)
            act.wait_ge(soft, 7)
            nc.scalar.activation(dots[:, 0, :, :], dots[:, 0, :, :], ACT.Sqrt, bias=tiny[:, :],
                                 scale=1.0 / HD).then_inc(acted, 1)
            act.wait_ge(soft, 9)
            nc.scalar.activation(dots[:, 0, :, :], dots[:, 0, :, :], ACT.Exp).then_inc(acted, 1)

        @block.tensor
        def _(pe):
            pe.sem_inc(s_used, RING)
            with nc.tensor.Fori(0, TILES) as t:
                for n in range(N):
                    for e in range(2):
                        i = 2 * n + e
                        pe.wait_ge(s_landed[i % RING], 16 * CK * (t * 2 + i // RING + 1))
                        for j in range(2):
                            u = 2 * i + j
                            pe.wait_ge(w_lo_made, mat(j, e) + 1)
                            pe.wait_ge(evicted, t * UNITS + u + 1)
                            k = 0
                            for c in range(CK):
                                for a, b in ((0, w_hi), (1, w_hi), (0, w_lo)):
                                    last = nc.tensor.matmul(ps[:, u % 8, :], s_in[:, i % RING, c, a, :],
                                                            b[:, mat(j, e), c, :], start=(k == 0), stop=(k == 3 * CK - 1))
                                    k += 1
                            last.then_inc(s_used if j else made, 1)

        @block.vector
        def _(dve):
            dve.sem_inc(evicted, 8)
            dve.sem_inc(reduced, 2)
            dve.sem_inc(own_reduced, 1)
            nc.vector.memset(tiny[:, :], 1e-8 / HD)
            for m in range(MATS):
                dve.wait_ge(w_hi_made, m + 1)
                nc.vector.tensor_tensor(w_lo[:, m, :, :], prod[:, m % 2, :, :], w_hi[:, m, :, :].bitcast(F32),
                                        ALU.subtract).then_inc(w_lo_made, 1)
            dve.wait_ge(bias_landed, 16)

            def stage(t_in, t, par):
                for u in range(UNITS):
                    if t_in is not None:
                        i, j = u // 2, u % 2
                        n, e = i // 2, i % 2
                        if j:
                            dve.wait_ge(s_used, t_in * 2 * N + i + 1 + RING)
                        else:
                            dve.wait_ge(made, t_in * 2 * N + i + 1)
                        nc.vector.tensor_tensor(qk[:, par, j, e, n, :], ps[:, u % 8, :], bias[:, mat(j, e), :],
                                                ALU.add).then_inc(evicted, 1)
                    if t is not None:
                        n, what = u // 4, u % 4
                        if what < 2:
                            dve.wait_ge(pooled, t * 8 + n * 2 + what + 1)
                            done = reduced
                        elif what == 2:
                            if n == 0:
                                dve.wait_ge(mixes, t * 2 + 2)
                            dve.wait_ge(own_reduced, t * N + n + 1)
                            nc.vector.tensor_tensor(prod[:, 2, :, :],
                                                    mixed[:, 0, n:n + 1, :].broadcast_to([P, N, D]),
                                                    mixed[:, 1, :, :], ALU.mult).then_inc(own_product, 1)
                            continue
                        else:
                            dve.wait_ge(own_product, t * N + n + 1)
                            done = own_reduced
                        kind = min(what, 2)
                        W = N * HEADS
                        nc.vector.tensor_reduce(
                            dots[:, kind, bass.ds(t, 1), n * W:(n + 1) * W].rearrange("p t w -> p (t w)"),
                            prod[:, kind, :, :].rearrange("p m (h d) -> p (m h) d", d=HD), AX_X, ALU.add).then_inc(done, 1)

            stages(nc.vector.Fori, stage)

            steps = [0]

            def link(ins):
                steps[0] += 1
                ins.then_inc(soft, 1)
                dve.wait_ge(soft, steps[0])

            a, b, c = (dots[:, i, :, :] for i in range(3))
            most = qk[:, 0, 0, 0, 0, 0:TILES * N * HEADS]
            dve.wait_ge(own_reduced, TILES * N + 1)
            dve.wait_ge(reduced, TILES * 2 * N + 2)
            link(nc.vector.tensor_tensor(c, c, a, ALU.subtract))
            link(nc.vector.tensor_tensor(c, c, b, ALU.add))
            link(nc.vector.tensor_tensor(a, a, b, ALU.add))
            link(nc.vector.tensor_tensor(c, c, c, ALU.mult))
            link(nc.vector.tensor_tensor(a, a, a, ALU.mult))
            link(nc.vector.tensor_tensor(a, a, c, ALU.add))
            nc.vector.tensor_copy(tiny[:, :], tiny[:, :]).then_inc(soft, 1)
            steps[0] += 1
            dve.wait_ge(acted, 1)
            flat = a.rearrange("p t (n m h) -> p (t n) m h", m=N, h=HEADS)
            by_m = flat.rearrange("p x m h -> p x h m")
            m3 = most.rearrange("p (x h) -> p x h", h=HEADS)
            link(nc.vector.tensor_reduce(m3, by_m, AX_X, ALU.max))
            spread = m3.unsqueeze(2).broadcast_to([P, TILES * N, N, HEADS])
            nc.vector.tensor_tensor(flat, flat, spread, ALU.subtract).then_inc(soft, 1)
            steps[0] += 1
            dve.wait_ge(acted, 2)
            link(nc.vector.tensor_reduce(m3, by_m, AX_X, ALU.add))
            link(nc.vector.reciprocal(most, most))
            link(nc.vector.tensor_tensor(flat, flat, spread, ALU.mult))
            nc.vector.tensor_copy(tiny[:, :], tiny[:, :]).then_inc(soft, 1)

        @block.gpsimd
        def _(pool):
            def work(t, par):
                pool.wait_ge(evicted, t * UNITS + UNITS + 8)
                for j, op in ((0, ALU.add), (1, ALU.subtract)):
                    if not isinstance(t, int):
                        pool.wait_ge(own_product, t * N)
                    nc.gpsimd.tensor_tensor(mixed[:, j, :, :], qk[:, par, j, 0, :, :], qk[:, par, j, 1, :, :], op).then_inc(mixes, 1)
                for n in range(N):
                    for e in range(2):
                        pool.wait_ge(reduced, t * 8 + n * 2 + e + 1)
                        nc.gpsimd.tensor_tensor(prod[:, e, :, :],
                                                qk[:, par, 0, e, n:n + 1, :].broadcast_to([P, N, D]),
                                                qk[:, par, 1, e, :, :], ALU.mult).then_inc(pooled, 1)
            pool.wait_ge(w_lo_made, MATS)
            work(0, 0)
            with nc.gpsimd.Fori(0, TILES // 2 - 1) as q:
                work(2 * q + 1, 1)
                work(2 * q + 2, 0)
            pool.wait_ge(own_product, (TILES - 1) * N)
            work(TILES - 1, 1)


def attend(nc, sem, dram, w_proj, bias_rows, out_cols, identity):
    with ExitStack() as ctx:
        def sb(name, shape, dt=F32):
            return ctx.enter_context(nc.sbuf_tensor(name, shape, dt))

        MATS = 4
        UNITS = 2 * N
        RING = 4
        w_hi = sb("vo_w_hi", [P, MATS, CK, D], F32R)
        w_lo = sb("vo_w_lo", [P, MATS, CK, D], F32R)
        bias = sb("v_bias", [P, 2, D])
        o_bias = sb("o_bias", [P, 2, CK])
        ident = sb("ident", [P, P])
        s_in = sb("v_s", [P, RING, CK, 2, P], F32R)
        v = sb("v", [P, 2, 2, N, D])
        w_soft = sb("w_soft", [P, TILES, N * N * HEADS])
        w_tile = sb("w_tile", [P, 2, N * N * HEADS])
        prod = sb("v_prod", [P, 2, N, D])
        mixed = sb("v_mixed", [P, 2, D])
        m_hi = sb("m_hi", [P, 2, CK, N, P], F32R)
        m_lo = sb("m_lo", [P, 2, CK, N, P], F32R)
        staged = sb("attn_staged", [P, 2, 2, N, P])
        ps_v = ctx.enter_context(nc.psum_tensor("ps_v", [P, 4, D], F32))
        ps_t = ctx.enter_context(nc.psum_tensor("ps_t", [P, 2, CK, P], F32))
        ps_o = ctx.enter_context(nc.psum_tensor("ps_o", [P, 2, N, P], F32))
        w_landed, consts_landed = [sem("vo_w_landed0"), sem("vo_w_landed1")], sem("v_consts_landed")
        w_hi_made, w_lo_made = sem("vo_w_hi_made"), sem("vo_w_lo_made")
        s_landed = [sem(f"v_s_landed{i}") for i in range(RING)]
        v_made, evicted = sem("v_made"), sem("v_evicted")
        pooled, halved, mixes = sem("v_pooled"), sem("v_halved"), sem("v_mixes")
        turned, t_hi, t_lo = sem("turned"), sem("t_hi"), sem("t_lo")
        w_picked = sem("w_picked")
        o_made, o_hi, o_lo = sem("o_made"), sem("o_hi"), sem("o_lo")
        sent = [sem("attn_sent0"), sem("attn_sent1")]
        block = ctx.enter_context(nc.Block())

        def stages(fori, run):
            run(0, 0, "v")
            run(1, 1, "vm")
            with fori(1, TILES // 2) as q:
                run(2 * q, 0, "vmo")
                run(2 * q + 1, 1, "vmo")
            run(TILES, 0, "mo")
            run(TILES + 1, 1, "o")

        def pieces(t, u, has):
            c = u % N
            if u < N:
                return ((t - 2) * 8 + 4 + c, (t - 2) * 4 + 2 + c // 2, 1, c) if "o" in has else None
            return ((t - 1) * 8 + c, (t - 1) * 4 + c // 2, 0, c) if "m" in has else None

        @block.sync
        def _(sp):
            for u in range(2):
                sp.sem_inc(sent[u], 16)
            sp.dma_start(bias[:, :, :], bias_rows[4:6, :].unsqueeze(0).broadcast_to([P, 2, D])).then_inc(consts_landed, 16)
            sp.dma_start(o_bias[:, :, :], out_cols).then_inc(consts_landed, 16)
            sp.dma_start(ident[:, :], identity).then_inc(consts_landed, 16)
            sp.dma_start(w_soft[:, :, :], dram["w"]).then_inc(consts_landed, 16)
            for m in range(MATS):
                if m >= 2:
                    sp.wait_ge(w_lo_made, m - 1)
                sp.dma_start(prod[:, m % 2, :, :], w_proj[4 + m, :, :, :].rearrange("c p o -> p c o")).then_inc(w_landed[m % 2], 16)

            def stage(t, par, has):
                for u in range(UNITS):
                    if "v" in has:
                        sp.wait_ge(v_made, t * UNITS + u + 1)
                        for c in range(CK):
                            src = dram["s"][u * CK + c][:, :, bass.ts(t, P)]
                            sp.dma_start(s_in[:, u % RING, c, :, :].bitcast(F32),
                                         src.rearrange("a p b -> p a b")).then_inc(s_landed[u % RING], 16)

            with nc.sync.Fori(0, TILES) as t:
                stage(t, 0, "v")

        @block.scalar
        def _(act):
            for m in range(MATS):
                act.wait_ge(w_landed[m % 2], 16 * (m // 2 + 1))
                nc.scalar.activation(w_hi[:, m, :, :], prod[:, m % 2, :, :], ACT.Copy).then_inc(w_hi_made, 1)
            act.wait_ge(consts_landed, 64)

            def send(piece, t, e, c):
                act.wait_ge(o_lo, piece + 3)
                for a in range(2):
                    dst = dram["attn"][e, c, a][:, :, bass.ts(t, P)]
                    act.dma_start(dst, staged[:, c % 2, a, :, :]).then_inc(sent[c % 2], 16)

            def stage(t, par, has):
                for u in range(UNITS):
                    it = pieces(t, u, has)
                    if it:
                        piece, before, e, c = it
                        act.wait_ge(o_made, piece + 1)
                        act.wait_ge(sent[c % 2], before * 32 + 16)
                        nc.scalar.activation(staged[:, c % 2, 0, :, :].bitcast(F32R), ps_o[:, c % 2, :, :], ACT.Identity,
                                             bias=o_bias[:, e, c:c + 1]).then_inc(o_hi, 1)
                        send(piece, t - 2 if u < N else t - 1, e, c)
                    if "m" in has:
                        act.wait_ge(turned, (t - 1) * UNITS + u + 3)
                        nc.scalar.activation(m_hi[:, u // N, :, u % N, :], ps_t[:, u % 2, :, :],
                                             ACT.Copy).then_inc(t_hi, 1)

            stages(nc.scalar.Fori, stage)
            for u in range(2):
                act.wait_ge(sent[u], 16 + 32 * 4 * TILES)

        @block.tensor
        def _(pe):
            pe.sem_inc(v_made, RING)
            pe.sem_inc(turned, 2)
            pe.wait_ge(consts_landed, 64)

            def stage(t, par, has):
                for u in range(UNITS):
                    e, n = u // N, u % N
                    if "v" in has:
                        pe.wait_ge(s_landed[u % RING], 16 * CK * (t * 2 + u // RING + 1))
                        pe.wait_ge(w_lo_made, e + 1)
                        pe.wait_ge(evicted, t * UNITS + u + 1)
                        k = 0
                        for c in range(CK):
                            for a, b in ((0, w_hi), (1, w_hi), (0, w_lo)):
                                last = nc.tensor.matmul(ps_v[:, u % 4, :], s_in[:, u % RING, c, a, :], b[:, e, c, :],
                                                        start=(k == 0), stop=(k == 3 * CK - 1))
                                k += 1
                        last.then_inc(v_made, 1)
                    it = pieces(t, u, has)
                    if it:
                        piece, before, e, c = it
                        pe.wait_ge(t_lo, ((t - 1) * UNITS if u < N else (t - 1) * UNITS + N) + 2)
                        pe.wait_ge(o_lo, piece + 1)
                        k = 0
                        for j in range(CK):
                            for a, b in ((w_hi, m_hi), (w_hi, m_lo), (w_lo, m_hi)):
                                last = nc.tensor.matmul(ps_o[:, c % 2, :, :], a[:, 2 + e, j, c * P:(c + 1) * P], b[:, e, j, :, :],
                                                        start=(k == 0), stop=(k == 3 * CK - 1))
                                k += 1
                        last.then_inc(o_made, 1)
                    if "m" in has:
                        pe.wait_ge(mixes, (t - 1) * UNITS + u + 3)
                        pe.wait_ge(t_lo, (t - 1) * UNITS + u + 1)
                        for c in range(CK):
                            last = nc.tensor.transpose(ps_t[:, u % 2, c, :], mixed[:, u % 2, c * P:(c + 1) * P], ident[:, :])
                        last.then_inc(turned, 1)

            stages(nc.tensor.Fori, stage)

        @block.vector
        def _(dve):
            dve.sem_inc(evicted, 4)
            dve.sem_inc(mixes, 2)
            dve.sem_inc(t_lo, 2)
            dve.sem_inc(o_lo, 2)
            for m in range(MATS):
                dve.wait_ge(w_hi_made, m + 1)
                nc.vector.tensor_tensor(w_lo[:, m, :, :], prod[:, m % 2, :, :], w_hi[:, m, :, :].bitcast(F32),
                                        ALU.subtract).then_inc(w_lo_made, 1)
            dve.wait_ge(consts_landed, 64)

            def stage(t, par, has):
                for u in range(UNITS):
                    e, n = u // N, u % N
                    if "v" in has and u == 0:
                        nc.vector.tensor_copy(w_tile[:, par:par + 1, :], w_soft[:, bass.ds(t, 1), :]).then_inc(w_picked, 1)
                    if "v" in has:
                        dve.wait_ge(v_made, t * UNITS + u + 1 + RING)
                        nc.vector.tensor_tensor(v[:, par, e, n, :], ps_v[:, u % 4, :], bias[:, e, :],
                                                ALU.add).then_inc(evicted, 1)
                    if "m" in has:
                        dve.wait_ge(pooled, (t - 1) * UNITS + u + 1)
                        nc.vector.tensor_tensor(prod[:, u % 2, 0:2, :], prod[:, u % 2, 0:2, :], prod[:, u % 2, 2:4, :],
                                                ALU.add).then_inc(halved, 1)
                        dve.wait_ge(turned, (t - 1) * UNITS + u + 1)
                    it = pieces(t, u, has)
                    if it:
                        piece, before, e, c = it
                        dve.wait_ge(o_hi, piece + 1)
                        nc.vector.scalar_tensor_tensor(
                            staged[:, c % 2, 1, :, :].bitcast(F32R), ps_o[:, c % 2, :, :], o_bias[:, e, c:c + 1],
                            staged[:, c % 2, 0, :, :], ALU.add, ALU.subtract).then_inc(o_lo, 1)
                    if "m" in has:
                        dve.wait_ge(halved, (t - 1) * UNITS + u + 1)
                        nc.vector.tensor_tensor(mixed[:, u % 2, :], prod[:, u % 2, 0, :], prod[:, u % 2, 1, :],
                                                ALU.add).then_inc(mixes, 1)
                        dve.wait_ge(t_hi, (t - 1) * UNITS + u + 1)
                        nc.vector.tensor_tensor(m_lo[:, u // N, :, u % N, :], ps_t[:, u % 2, :, :],
                                                m_hi[:, u // N, :, u % N, :].bitcast(F32),
                                                ALU.subtract).then_inc(t_lo, 1)

            stages(nc.vector.Fori, stage)

        @block.gpsimd
        def _(pool):
            pool.wait_ge(w_lo_made, MATS)

            def work(t, par):
                pool.wait_ge(w_picked, t + 1)
                for u in range(UNITS):
                    e, n = u // N, u % N
                    if n == 0:
                        pool.wait_ge(evicted, t * UNITS + (e + 1) * N + 4)
                    pool.wait_ge(mixes, t * UNITS + u + 1)
                    w = w_tile[:, par, n * N * HEADS:(n + 1) * N * HEADS]
                    nc.gpsimd.tensor_tensor(prod[:, u % 2, :, :].rearrange("p m (h d) -> p (m h) d", d=HD),
                                            v[:, par, e, :, :].rearrange("p m (h d) -> p (m h) d", d=HD),
                                            w.unsqueeze(2).broadcast_to([P, N * HEADS, HD]), ALU.mult).then_inc(pooled, 1)

            with nc.gpsimd.Fori(0, TILES // 2) as q:
                work(2 * q, 0)
                work(2 * q + 1, 1)



def superpose(nc, sem, dram, w_int, ids_t, tables, identity):
    with ExitStack() as ctx:
        def sb(name, shape, dt=F32):
            return ctx.enter_context(nc.sbuf_tensor(name, shape, dt))

        MATS, RING, Q = 2 * N, 4, 4
        w_hi = sb("int_w_hi", [P, MATS, CK, D], F32R)
        w_lo = sb("int_w_lo", [P, MATS, CK, D], F32R)
        a_in = sb("a_in", [P, RING, 2, 2, P], F32R)
        ri = sb("ri", [P, 2, 2, N, D])
        raw = ri[:, :, :, :, :].rearrange("p x e n d -> p (x e) n d")
        sq = sb("sq", [P, 2, 2, N, P])
        zero = sb("zero", [P, 2, N, P])
        unit = sb("unit", [P, 2, 2, N, P])
        v = sb("mix", [P, 2, N, P])
        vz = sb("mix_zero", [P, N, P])
        sup = sb("sup_rows", [P, 2, D])
        turned = sb("sup_turned", [P, 2, CK, P])
        strength = sb("strength", [P, TILES, N, N])
        st = sb("strength_tile", [P, 2, N, N])
        ids = sb("ids_sb", [P, TILES, N], I32)
        ident = sb("ident3", [P, P])
        tiny = sb("tiny3", [P, 1])
        norm = sb("norm", [P, 2])
        ps = ctx.enter_context(nc.psum_tensor("ri_ps", [P, 2, 3, D], F32))
        ps_t = ctx.enter_context(nc.psum_tensor("sup_ps", [P, 2, CK, P], F32))
        w_landed = [sem(f"int_w_landed{i}") for i in range(4)]
        w_hi_made, w_lo_made = sem("int_w_hi_made"), sem("int_w_lo_made")
        consts_landed, gathered = sem("p3_consts_landed"), sem("gathered")
        a_landed = [sem(f"a_landed{i}") for i in range(RING)]
        a_used = sem("a_used")
        copied, ri_ready = sem("ri_copied"), sem("ri_ready")
        squares, mags, zeros = sem("sup_squares"), sem("mags"), sem("zeros")
        roots, guarded, inverted, units = sem("roots"), sem("guarded"), sem("inverted"), sem("units")
        mixing, c_made, products = sem("mixing"), sem("c_made"), sem("sup_products")
        folded, quarters = sem("folded"), sem("quarters")
        power, normed, sup_ready = sem("power"), sem("normed"), sem("sup_ready")
        sup_turned, sent = sem("sup_turned"), sem("sup_sent")
        out_copied = sem("sup_copied")
        picked, inv_norm = sem("picked"), sem("inv_norm")
        block = ctx.enter_context(nc.Block())

        def stages(fori, run):
            run(0, 0, "m")
            run(1, 1, "ms")
            with fori(1, TILES // 2) as q:
                run(2 * q, 0, "ms")
                run(2 * q + 1, 1, "ms")
            run(TILES, 0, "s")

        @block.sync
        def _(sp):
            sp.sem_inc(sent, 16)
            for m in range(MATS):
                if m >= 4:
                    sp.wait_ge(w_lo_made, m - 3)
                sp.dma_start(raw[:, m % 4, :, :], w_int[m, :, :, :].rearrange("c p o -> p c o")).then_inc(w_landed[m % 4], 16)
                if m == 1:
                    sp.dma_start(ident[:, :], identity).then_inc(consts_landed, 16)
            with nc.sync.Fori(0, TILES) as t:
                for i in range(4 * N):
                    n, e, cp = i // 4, i // 2 % 2, i % 2
                    sp.wait_ge(a_used, t * 4 * N + i + 1)
                    for cc in range(2):
                        src = dram["attn"][e, 2 * cp + cc][:, :, n, bass.ts(t, P)]
                        sp.dma_start(a_in[:, i % RING, cc, :, :].bitcast(F32),
                                     src.rearrange("a p b -> p a b")).then_inc(a_landed[i % RING], 16)

        @block.gpsimd
        def _(pool):
            nc.gpsimd.dma_start(ids[:, :, :], ids_t).then_inc(gathered, 16)
            pool.wait_ge(gathered, 16)
            for t in range(TILES):
                for i in range(N):
                    nc.gpsimd.indirect_dma_start(
                        strength[:, t, i, :], None, tables[i],
                        bass.IndirectOffsetOnAxis(ap=ids[:, t, i:i + 1].bitcast(U32), axis=0)).then_inc(gathered, 16)

            def magnitude(t, par, q):
                k, b = t * Q + q, q % 2
                pool.wait_ge(squares, k + 1)
                nc.gpsimd.tensor_tensor(sq[:, b, 0, :, :], sq[:, b, 0, :, :], sq[:, b, 1, :, :], ALU.add).then_inc(mags, 1)

            def units_of(t, par, q):
                k, b = t * Q + q, q % 2
                pool.wait_ge(inverted, k + 1)
                for e in range(2):
                    nc.gpsimd.tensor_tensor(unit[:, b, e, :, :], ri[:, par, e, :, q * P:(q + 1) * P], sq[:, b, 1, :, :],
                                            ALU.mult).then_inc(units, 1)

            def product(t, par, q):
                k, b = t * Q + q, q % 2
                pool.wait_ge(c_made, k + 1)
                for e in range(2):
                    nc.gpsimd.tensor_tensor(sq[:, b, e, :, :], ri[:, par, e, :, q * P:(q + 1) * P], zero[:, b, :, :],
                                            ALU.mult).then_inc(products, 1)

            def tile(t, par):
                for step, q in ((magnitude, 0), (magnitude, 1), (units_of, 0), (units_of, 1), (product, 0),
                                (magnitude, 2), (units_of, 2), (product, 1), (magnitude, 3), (units_of, 3),
                                (product, 2), (product, 3)):
                    step(t, par, q)

            with nc.gpsimd.Fori(0, TILES // 2) as h:
                tile(2 * h, 0)
                tile(2 * h + 1, 1)

        @block.scalar
        def _(act):
            for m in range(MATS):
                act.wait_ge(w_landed[m % 4], 16 * (m // 4 + 1))
                nc.scalar.activation(w_hi[:, m, :, :], raw[:, m % 4, :, :], ACT.Copy).then_inc(w_hi_made, 1)

            def stage(t, par, has):
                def copy(n):
                    if "m" not in has:
                        return
                    if isinstance(t, int) and t < 2 and n == 0:
                        act.wait_ge(w_lo_made, MATS)
                    act.wait_ge(a_used, t * 4 * N + 4 * n + 4 + RING)
                    for e in range(2):
                        nc.scalar.activation(ri[:, par, e, n, :], ps[:, n % 2, 2 * e, :], ACT.Copy).then_inc(copied, 1)

                def square(q):
                    k, b = (t - 1) * Q + q, q % 2
                    act.wait_ge(ri_ready, t * N + 2)
                    act.wait_ge(quarters, k + 1)
                    nc.scalar.activation(sq[:, b, :, :, :].rearrange("p e n d -> p (e n) d"),
                                         ri[:, 1 - par, :, :, q * P:(q + 1) * P].rearrange("p e n d -> p (e n) d"),
                                         ACT.Square).then_inc(squares, 1)

                def root(q):
                    k, b = (t - 1) * Q + q, q % 2
                    act.wait_ge(mags, k + 1)
                    nc.scalar.activation(sq[:, b, 1, :, :], sq[:, b, 0, :, :], ACT.Sqrt).then_inc(roots, 1)

                copy(0)
                if "s" in has:
                    square(0), square(1), root(0), root(1)
                copy(1)
                if "s" in has:
                    square(2), root(2)
                copy(2)
                if "s" in has:
                    square(3), root(3)
                copy(3)
                if "s" in has:
                    act.wait_ge(power, t)
                    nc.scalar.activation(norm[:, 1:2], norm[:, 0:1], ACT.Sqrt, bias=tiny[:, :]).then_inc(normed, 1)
                    act.wait_ge(sup_turned, t + 1)
                    act.wait_ge(sent, 16 * t)
                    nc.scalar.activation(turned[:, :, :, :], ps_t[:, :, :, :], ACT.Copy).then_inc(out_copied, 1)
                    act.wait_ge(out_copied, t)
                    act.dma_start(dram["sup"][:, :, bass.ts(t - 1, P)].rearrange("c p b -> p c b"),
                                  turned[:, :, :, :].rearrange("p e c b -> p (e c) b")).then_inc(sent, 16)

            stages(nc.scalar.Fori, stage)
            act.wait_ge(sent, 16 * (TILES + 1))

        @block.tensor
        def _(pe):
            pe.sem_inc(a_used, RING)
            pe.sem_inc(sup_turned, 1)
            pe.wait_ge(consts_landed, 16)

            def turn(t):
                pe.wait_ge(sup_ready, t + 1)
                for i in range(2 * CK):
                    last = nc.tensor.transpose(ps_t[:, i // CK, i % CK, :], sup[:, i // CK, i % CK * P:(i % CK + 1) * P], ident[:, :])
                last.then_inc(sup_turned, 1)

            def maps(t):
                for i in range(4 * N):
                    n, e, cp = i // 4, i // 2 % 2, i % 2
                    pe.wait_ge(a_landed[i % RING], 32 * (t * N + i // RING + 1))
                    pe.wait_ge(w_lo_made, 2 * n + 2)
                    if e == 0 and cp == 0:
                        pe.wait_ge(ri_ready, t * N + n + 1)
                    for to, m in ((e, e), (2, 1 - e)):
                        k = 0
                        for cc in range(2):
                            for a, b in ((0, w_hi), (1, w_hi), (0, w_lo)):
                                first = cp == 0 and k == 0 and (to < 2 or e == 0)
                                final = cp == 1 and k == 5 and (to < 2 or e == 1)
                                last = nc.tensor.matmul(ps[:, n % 2, (0, 1, 2)[to], :], a_in[:, i % RING, cc, a, :],
                                                        b[:, 2 * n + m, 2 * cp + cc, :], start=first, stop=final)
                                k += 1
                    last.then_inc(a_used, 1)

            maps(0)
            maps(1)
            with nc.tensor.Fori(2, TILES) as t:
                turn(t - 2)
                maps(t)
            turn(TILES - 2)
            turn(TILES - 1)

        @block.vector
        def _(dve):
            dve.sem_inc(ri_ready, 2)
            dve.sem_inc(quarters, 2)
            nc.vector.memset(tiny[:, :], 1e-8)
            for m in range(MATS):
                dve.wait_ge(w_hi_made, m + 1)
                nc.vector.tensor_tensor(w_lo[:, m, :, :], raw[:, m % 4, :, :], w_hi[:, m, :, :].bitcast(F32),
                                        ALU.subtract).then_inc(w_lo_made, 1)
            dve.wait_ge(gathered, 16 * (1 + TILES * N))
            MIX = 2 * N * N + 1

            def stage(t, par, has):
                def finish(n):
                    if "m" in has:
                        dve.wait_ge(copied, 2 * (t * N + n) + 2)
                        nc.vector.tensor_tensor(ri[:, par, 0, n, :], ri[:, par, 0, n, :], ps[:, n % 2, 1, :],
                                                ALU.subtract).then_inc(ri_ready, 1)

                def invert(q):
                    k, b = (t - 1) * Q + q, q % 2
                    dve.wait_ge(mags, k + 1)
                    nc.vector.tensor_scalar(zero[:, b, :, :], sq[:, b, 0, :, :], 0.0, None, ALU.is_equal).then_inc(zeros, 1)
                    dve.wait_ge(zeros, k + 1)
                    dve.wait_ge(roots, k + 1)
                    nc.vector.tensor_tensor(sq[:, b, 1, :, :], sq[:, b, 1, :, :], zero[:, b, :, :], ALU.add).then_inc(guarded, 1)
                    dve.wait_ge(guarded, k + 1)
                    nc.vector.reciprocal(sq[:, b, 1, :, :], sq[:, b, 1, :, :]).then_inc(inverted, 1)

                def mix(q):
                    k, b = (t - 1) * Q + q, q % 2
                    dve.wait_ge(units, 2 * k + 2)
                    dve.wait_ge(c_made, k) if not (isinstance(k, int) and k == 0) else None
                    step = 0
                    for i in range(N):
                        for j in range(N):
                            s = st[:, 0, i, j:j + 1]
                            for out, src in ((v[:, :, j, :], unit[:, b, :, i, :]), (vz[:, j, :], zero[:, b, i, :])):
                                if i == 0:
                                    ins = nc.vector.tensor_scalar(out, src, s, None, ALU.mult)
                                else:
                                    dve.wait_ge(mixing, k * MIX + step - 2 * N + 1)
                                    ins = nc.vector.scalar_tensor_tensor(out, src, s, out, ALU.mult, ALU.add)
                                ins.then_inc(mixing, 1)
                                step += 1
                    dve.wait_ge(mixing, k * MIX + MIX - 1)
                    nc.vector.tensor_tensor(v[:, :, :, :], v[:, :, :, :], unit[:, b, :, :, :], ALU.mult).then_inc(mixing, 1)
                    dve.wait_ge(mixing, k * MIX + MIX)
                    nc.vector.tensor_tensor(zero[:, b, :, :], v[:, 0, :, :], v[:, 1, :, :], ALU.add).then_inc(folded, 1)
                    dve.wait_ge(folded, (t - 1) * Q * 2 + (1, 2, 4, 6)[q])
                    nc.vector.tensor_tensor(zero[:, b, :, :], zero[:, b, :, :], vz[:, :, :], ALU.add).then_inc(c_made, 1)

                def total(q):
                    k, b = (t - 1) * Q + q, q % 2
                    dve.wait_ge(products, 2 * k + 2)
                    if q == 0:
                        dve.wait_ge(sup_turned, t)
                    nc.vector.tensor_tensor(sq[:, b, :, 0:2, :], sq[:, b, :, 0:2, :], sq[:, b, :, 2:4, :], ALU.add).then_inc(folded, 1)
                    dve.wait_ge(folded, (t - 1) * Q * 2 + order[q])
                    nc.vector.tensor_tensor(sup[:, :, q * P:(q + 1) * P], sq[:, b, :, 0, :], sq[:, b, :, 1, :],
                                            ALU.add).then_inc(quarters, 1)

                order = {0: 3, 1: 5, 2: 7, 3: 8}
                if "s" in has:
                    nc.vector.tensor_copy(st[:, 0:1, :, :], strength[:, bass.ds(t - 1, 1), :, :]).then_inc(picked, 1)
                    dve.wait_ge(picked, t)
                finish(0)
                if "s" in has:
                    invert(0)
                    invert(1)
                    mix(0)
                finish(1)
                if "s" in has:
                    mix(1)
                    total(0)
                    invert(2)
                finish(2)
                if "s" in has:
                    mix(2)
                    total(1)
                    invert(3)
                finish(3)
                if "s" in has:
                    mix(3)
                    total(2)
                    total(3)
                    dve.wait_ge(quarters, t * Q + 2)
                    flat = sup[:, :, :].rearrange("p e d -> p (e d)")
                    vf = v[:, :, :, :].rearrange("p e n d -> p (e n d)")
                    nc.vector.tensor_tensor_reduce(out=vf, in0=flat, in1=flat, scale=1.0, scalar=0.0, op0=ALU.mult,
                                                   op1=ALU.add, accum_out=norm[:, 0:1]).then_inc(power, 1)
                    dve.wait_ge(normed, t)
                    nc.vector.reciprocal(norm[:, 1:2], norm[:, 1:2]).then_inc(inv_norm, 1)
                    dve.wait_ge(inv_norm, t)
                    nc.vector.tensor_scalar(flat, flat, norm[:, 1:2], None, ALU.mult).then_inc(sup_ready, 1)

            stages(nc.vector.Fori, stage)



def towers(nc, sem, dram, w_tail, w_top2, w_top3, tail_cols, y):
    with ExitStack() as ctx:
        def sb(name, shape, dt=F32):
            return ctx.enter_context(nc.sbuf_tensor(name, shape, dt))

        HALVES, BH = 2, BATCH // 2
        UNITS = HALVES * CK
        PLACE = (0, 1, 2, 0, 1)
        w_raw = sb("tail_w_raw", [P, 2, CK, D])
        w_hi, w_lo = sb("tail_w_hi", [P, 3, CK, D], F32R), sb("tail_w_lo", [P, 3, CK, D], F32R)
        w3 = sb("w_top3", [P, 2])
        cols = sb("tail_columns", [P, 5, CK])
        rows = sb("rows", [P, 2 * CK, BH])
        x_hi = sb("tail_x_hi", [P, HALVES, 2 * CK, BH], F32R)
        x_lo = sb("tail_x_lo", [P, HALVES, 2 * CK, BH], F32R)
        amp_hi, amp_lo = sb("amp_hi", [P, HALVES, CK, BH], F32R), sb("amp_lo", [P, HALVES, CK, BH], F32R)
        real, imag = sb("real", [P, 2, BH]), sb("imag", [P, 2, BH])
        colsum = sb("tail_colsum", [P, HALVES, BH])
        mean_w, eps = sb("tail_mean_w", [P, P]), sb("tail_eps", [P, 1])
        y_sb = sb("y_row", [1, HALVES, BH])
        ps = ctx.enter_context(nc.psum_tensor("tail_ps", [P, 8, BH], F32))
        top_x = w_raw

        names = """wt_landed0 wt_landed1 wt_hi wt_lo tail_cols_landed tail_consts sup_landed xs_hi xs_lo
            m_made m_copied m_real m_squared m_power m_amp m_hi m_lo
            p_made p_out p_sum stat1 p_centred p_squared p_sum2 stat2 p_std p_rstd p_scaled p_gelu z_hi z_lo
            top_x_landed t1_made t1_sum t1_relu t1_hi t1_lo t2_made t2_relu t3_made y_copied y_sent"""
        s = {n: sem("tail_" + n) for n in names.split()}
        wt_landed = [s["wt_landed0"], s["wt_landed1"]]
        block = ctx.enter_context(nc.Block())

        def unit(i):
            return i // CK, i % CK

        post_out = rows[:, :, :].rearrange("p (h c) b -> p h c b", h=HALVES)
        z_hi, z_lo = x_hi[:, :, 0:CK, :], x_lo[:, :, 0:CK, :]
        t1_hi, t1_lo = x_hi[:, :, CK:2 * CK, :], x_lo[:, :, CK:2 * CK, :]
        t2 = rows[:, 0:2 * HALVES, :].rearrange("p (h c) b -> p h c b", h=HALVES)

        def width(m):
            return TOP2 if m == 4 else D

        @block.sync
        def _(sp):
            sp.dma_start(cols[:, :, :], tail_cols).then_inc(s["tail_cols_landed"], 16)
            sp.dma_start(w3[:, :], w_top3).then_inc(s["tail_cols_landed"], 16)
            for m in range(2):
                sp.dma_start(w_raw[:, m, :, :], w_tail[m].rearrange("c p o -> p c o")).then_inc(wt_landed[m], 16)
                if m == 0:
                    sp.dma_start(rows[:, :, :], dram["sup"][:, :, 0:BH].rearrange("c p b -> p c b")).then_inc(s["sup_landed"], 16)
            sp.wait_ge(s["xs_lo"], 1)
            sp.dma_start(rows[:, :, :], dram["sup"][:, :, BH:].rearrange("c p b -> p c b")).then_inc(s["sup_landed"], 16)
            for m in range(2, 5):
                sp.wait_ge(s["wt_lo"], m - 1)
                src = w_top2 if m == 4 else w_tail[m]
                sp.dma_start(w_raw[:, m % 2, :, 0:width(m)], src.rearrange("c p o -> p c o")).then_inc(wt_landed[m % 2], 16)
            sp.wait_ge(s["wt_lo"], 5)
            for h in range(HALVES):
                sp.dma_start(top_x[:, h, :, :], dram["top_x"][:, :, h * BH:(h + 1) * BH].rearrange("c p b -> p c b")
                             ).then_inc(s["top_x_landed"], 16)
            for h in range(HALVES):
                sp.wait_ge(s["y_copied"], h + 1)
                sp.dma_start(y[:, h * BH:(h + 1) * BH], y_sb[:, h, :]).then_inc(s["y_sent"], 16)
            sp.wait_ge(s["y_sent"], 16 * HALVES)

        @block.tensor
        def _(pe):
            def products(out, w_place, k_parts, moving, c, h, first=True, last=True):
                b_hi, b_lo = moving
                n = 0
                for k in range(CK):
                    for a, b in ((w_hi, b_hi), (w_hi, b_lo), (w_lo, b_hi)):
                        ins = nc.tensor.matmul(out, a[:, w_place, k, c * P:(c + 1) * P], b[:, h, k_parts + k, :],
                                               start=first and n == 0, stop=last and n == 3 * CK - 1)
                        n += 1
                return ins

            sup = (x_hi, x_lo)
            for i in range(UNITS):
                h, c = unit(i)
                pe.wait_ge(s["xs_lo"], h + 1)
                pe.wait_ge(s["wt_lo"], 2)
                b = 3 * (i % 2)
                if i >= 2:
                    pe.wait_ge(s["m_squared"], i - 1)
                products(ps[:, b, :], 0, 0, sup, c, h)
                products(ps[:, b + 1, :], 1, CK, sup, c, h)
                products(ps[:, b + 2, :], 1, 0, sup, c, h, last=False)
                products(ps[:, b + 2, :], 0, CK, sup, c, h, first=False).then_inc(s["m_made"], 1)
            for i in range(UNITS):
                h, c = unit(i)
                pe.wait_ge(s["m_lo"], h * CK + CK)
                pe.wait_ge(s["wt_lo"], 3)
                if i >= 2:
                    pe.wait_ge(s["p_out"], i - 1)
                products(ps[:, 6 + i % 2, :], 2, 0, (amp_hi, amp_lo), c, h).then_inc(s["p_made"], 1)
            pe.wait_ge(s["tail_consts"], 2)
            pe.wait_ge(s["m_squared"], UNITS)
            for name, bank, source in (("stat1", 0, "p_sum"), ("stat2", 2, "p_sum2")):
                for h in range(HALVES):
                    pe.wait_ge(s[source], (h + 1) * CK)
                    nc.tensor.matmul(ps[:, bank + h, :], mean_w[:, :], colsum[:, h, :], start=True, stop=True).then_inc(s[name], 1)
            for i in range(UNITS):
                h, c = unit(i)
                pe.wait_ge(s["z_lo"], h * CK + CK)
                pe.wait_ge(s["wt_lo"], 4)
                if i >= 2:
                    pe.wait_ge(s["t1_sum"], i - 1)
                products(ps[:, 4 + i % 2, :], 0, 0, (x_hi, x_lo), c, h).then_inc(s["t1_made"], 1)
            for i in range(2 * HALVES):
                h, c = i // 2, i % 2
                pe.wait_ge(s["t1_lo"], h * CK + CK)
                pe.wait_ge(s["wt_lo"], 5)
                pe.wait_ge(s["p_out"], UNITS)
                if i >= 2:
                    pe.wait_ge(s["t2_relu"], i - 1)
                products(ps[:, 6 + i % 2, :], 1, CK, (x_hi, x_lo), c, h).then_inc(s["t2_made"], 1)
            for h in range(HALVES):
                pe.wait_ge(s["t2_relu"], 2 * h + 2)
                pe.wait_ge(s["p_centred"], UNITS)
                for k in range(2):
                    ins = nc.tensor.matmul(ps[0:1, h, :], w3[:, k:k + 1], t2[:, h, k, :], start=(k == 0), stop=(k == 1))
                ins.then_inc(s["t3_made"], 1)

        def lagged(count, *steps):
            for i in range(count + len(steps) - 1):
                for lag, step in enumerate(steps):
                    if 0 <= i - lag < count:
                        step(i - lag)

        @block.scalar
        def _(act):
            def split_w(m):
                if m >= 3:
                    act.wait_ge(s["m_made"], UNITS)
                act.wait_ge(wt_landed[m % 2], 16 * (m // 2 + 1))
                w = width(m)
                nc.scalar.activation(w_hi[:, PLACE[m], :, 0:w], w_raw[:, m % 2, :, 0:w], ACT.Copy).then_inc(s["wt_hi"], 1)

            def split_x(h):
                act.wait_ge(s["sup_landed"], 16 * (h + 1))
                nc.scalar.activation(x_hi[:, h, :, :], rows[:, :, :], ACT.Copy).then_inc(s["xs_hi"], 1)

            split_w(0), split_x(0), split_w(1), split_x(1), split_w(2)

            def copy(i):
                act.wait_ge(s["m_made"], i + 1)
                if i >= 2:
                    act.wait_ge(s["m_lo"], i - 1)
                nc.scalar.activation(real[:, i % 2, :], ps[:, 3 * (i % 2), :], ACT.Copy).then_inc(s["m_copied"], 1)

            def square(i):
                nc.scalar.activation(imag[:, i % 2, :], ps[:, 3 * (i % 2) + 2, :], ACT.Square)
                act.wait_ge(s["m_real"], i + 1)
                nc.scalar.activation(real[:, i % 2, :], real[:, i % 2, :], ACT.Square).then_inc(s["m_squared"], 1)

            def root(i):
                act.wait_ge(s["m_power"], i + 1)
                nc.scalar.activation(real[:, i % 2, :], real[:, i % 2, :], ACT.Sqrt).then_inc(s["m_amp"], 1)
                act.wait_ge(s["m_amp"], i + 1)
                nc.scalar.activation(amp_hi[:, i // CK, i % CK, :], real[:, i % 2, :], ACT.Copy).then_inc(s["m_hi"], 1)

            for i in range(UNITS):
                copy(i), square(i), root(i)
            split_w(3), split_w(4)
            act.wait_ge(s["tail_cols_landed"], 32)

            def bias(i):
                h, c = unit(i)
                act.wait_ge(s["p_made"], i + 1)
                nc.scalar.activation(post_out[:, h, c, :], ps[:, 6 + i % 2, :], ACT.Identity,
                                     bias=cols[:, 0, c:c + 1]).then_inc(s["p_out"], 1)

            for i in range(UNITS):
                bias(i)
            for i in range(UNITS):
                act.wait_ge(s["p_centred"], i + 1)
                if i >= 2:
                    act.wait_ge(s["p_sum2"], i - 1)
                nc.scalar.activation(real[:, i % 2, :], post_out[:, i // CK, i % CK, :], ACT.Square).then_inc(s["p_squared"], 1)
            act.wait_ge(s["p_sum2"], UNITS)
            for h in range(HALVES):
                act.wait_ge(s["stat2"], h + 1)
                nc.scalar.activation(imag[:, h, :], ps[:, 2 + h, :], ACT.Sqrt, bias=eps[:, :]).then_inc(s["p_std"], 1)

            def gelu(i):
                h, c = unit(i)
                act.wait_ge(s["p_scaled"], i + 1)
                nc.scalar.activation(post_out[:, h, c, :], post_out[:, h, c, :], ACT.Gelu, bias=cols[:, 2, c:c + 1],
                                     scale=cols[:, 1, c:c + 1]).then_inc(s["p_gelu"], 1)

            def split_z(i):
                h, c = unit(i)
                act.wait_ge(s["p_gelu"], i + 1)
                nc.scalar.activation(z_hi[:, h, c, :], post_out[:, h, c, :], ACT.Copy).then_inc(s["z_hi"], 1)

            lagged(UNITS, gelu, split_z)

            def relu(i):
                h, c = unit(i)
                act.wait_ge(s["t1_sum"], i + 1)
                nc.scalar.activation(top_x[:, h, c, :], top_x[:, h, c, :], ACT.Relu, bias=cols[:, 3, c:c + 1]).then_inc(s["t1_relu"], 1)

            def split_t(i):
                h, c = unit(i)
                act.wait_ge(s["t1_relu"], i + 1)
                nc.scalar.activation(t1_hi[:, h, c, :], top_x[:, h, c, :], ACT.Copy).then_inc(s["t1_hi"], 1)

            lagged(UNITS, relu, split_t)
            act.wait_ge(s["p_made"], UNITS)
            for i in range(2 * HALVES):
                act.wait_ge(s["t2_made"], i + 1)
                nc.scalar.activation(t2[:, i // 2, i % 2, :], ps[:, 6 + i % 2, :], ACT.Relu,
                                     bias=cols[:, 4, i % 2:i % 2 + 1]).then_inc(s["t2_relu"], 1)
            for h in range(HALVES):
                act.wait_ge(s["t3_made"], h + 1)
                nc.scalar.activation(y_sb[:, h, :], ps[0:1, h, :], ACT.Copy).then_inc(s["y_copied"], 1)

        @block.vector
        def _(dve):
            nc.vector.memset(mean_w[:, :], 1.0 / OUT).then_inc(s["tail_consts"], 1)
            nc.vector.memset(eps[:, :], EPS).then_inc(s["tail_consts"], 1)

            def minus(out, a, b, done):
                nc.vector.tensor_tensor(out, a, b.bitcast(F32), ALU.subtract).then_inc(s[done], 1)

            def split_w(m):
                dve.wait_ge(s["wt_hi"], m + 1)
                w = width(m)
                minus(w_lo[:, PLACE[m], :, 0:w], w_raw[:, m % 2, :, 0:w], w_hi[:, PLACE[m], :, 0:w], "wt_lo")

            def split_x(h):
                dve.wait_ge(s["xs_hi"], h + 1)
                minus(x_lo[:, h, :, :], rows[:, :, :], x_hi[:, h, :, :], "xs_lo")

            split_w(0), split_x(0), split_w(1), split_x(1), split_w(2)
            for i in range(UNITS):
                b = 3 * (i % 2)
                dve.wait_ge(s["m_copied"], i + 1)
                nc.vector.tensor_tensor(real[:, i % 2, :], real[:, i % 2, :], ps[:, b + 1, :], ALU.subtract).then_inc(s["m_real"], 1)
                dve.wait_ge(s["m_squared"], i + 1)
                nc.vector.tensor_tensor(real[:, i % 2, :], real[:, i % 2, :], imag[:, i % 2, :], ALU.add).then_inc(s["m_power"], 1)
                dve.wait_ge(s["m_hi"], i + 1)
                minus(amp_lo[:, i // CK, i % CK, :], real[:, i % 2, :], amp_hi[:, i // CK, i % CK, :], "m_lo")
            split_w(3), split_w(4)

            def summed(i, src, name):
                h, c = unit(i)
                if c == 0:
                    ins = nc.vector.tensor_copy(colsum[:, h, :], src)
                else:
                    dve.wait_ge(s[name], i)
                    ins = nc.vector.tensor_tensor(colsum[:, h, :], colsum[:, h, :], src, ALU.add)
                ins.then_inc(s[name], 1)

            for i in range(UNITS):
                dve.wait_ge(s["p_out"], i + 1)
                summed(i, post_out[:, i // CK, i % CK, :], "p_sum")
            for h in range(HALVES):
                dve.wait_ge(s["stat1"], h + 1)
                for c in range(CK):
                    nc.vector.tensor_tensor(post_out[:, h, c, :], post_out[:, h, c, :], ps[:, h, :],
                                            ALU.subtract).then_inc(s["p_centred"], 1)
            for i in range(UNITS):
                dve.wait_ge(s["p_squared"], i + 1)
                summed(i, real[:, i % 2, :], "p_sum2")
            for h in range(HALVES):
                dve.wait_ge(s["p_std"], h + 1)
                nc.vector.reciprocal(imag[:, h, :], imag[:, h, :]).then_inc(s["p_rstd"], 1)
                dve.wait_ge(s["p_rstd"], h + 1)
                for c in range(CK):
                    nc.vector.tensor_tensor(post_out[:, h, c, :], post_out[:, h, c, :], imag[:, h, :],
                                            ALU.mult).then_inc(s["p_scaled"], 1)
            for i in range(UNITS):
                h, c = unit(i)
                dve.wait_ge(s["z_hi"], i + 1)
                minus(z_lo[:, h, c, :], post_out[:, h, c, :], z_hi[:, h, c, :], "z_lo")
            dve.wait_ge(s["top_x_landed"], 16 * HALVES)

            def add_x(i):
                h, c = unit(i)
                dve.wait_ge(s["t1_made"], i + 1)
                nc.vector.tensor_tensor(top_x[:, h, c, :], top_x[:, h, c, :], ps[:, 4 + i % 2, :], ALU.add).then_inc(s["t1_sum"], 1)

            def split_t(i):
                h, c = unit(i)
                dve.wait_ge(s["t1_hi"], i + 1)
                minus(t1_lo[:, h, c, :], top_x[:, h, c, :], t1_hi[:, h, c, :], "t1_lo")

            lagged(UNITS, add_x, split_t)


def tower(nc, a, y):
    with ExitStack() as ctx:
        def sem(name):
            return ctx.enter_context(nc.semaphore(name))

        def scratch(name, shape):
            return nc.dram_tensor(name, shape, F32, kind="Internal").ap()

        dram = {
            "s": scratch("encoded", [2 * N * CK, 2, P, BATCH]),
            "top_x": scratch("top_x", [CK, P, BATCH]),
            "w": scratch("weights_soft", [P, TILES, N * N * HEADS]),
            "attn": scratch("attended", [2, CK, 2, P, N, BATCH]),
            "sup": scratch("superposed", [2 * CK, P, BATCH]),
        }
        encoders(nc, sem, dram, a["w_stream"], a["x_t"], a["enc_cols"])
        scores(nc, sem, dram, a["w_proj"], a["bias_rows"])
        attend(nc, sem, dram, a["w_proj"], a["bias_rows"], a["out_cols"], a["identity"])
        superpose(nc, sem, dram, a["w_int"], a["ids_t"], [a[f"tbl_{i}"] for i in range(N)], a["identity"])
        towers(nc, sem, dram, a["w_tail"], a["w_top2"], a["w_top3"], a["tail_cols"], y)


def lay_out(np, i):
    L = {k[len("L0_rec_"):]: np.asarray(v) for k, v in i.items() if k.startswith("L0_rec_")}
    top1, top2, top3 = (np.asarray(i[f"W_top{n}"]) for n in (1, 2, 3))

    def stream(w):
        return w.reshape(w.shape[0] // (2 * P), 2, P, w.shape[1] // 512, 512).transpose(3, 0, 2, 1, 4)

    def chunks(w):
        return w.reshape(w.shape[0] // P, P, w.shape[1])

    def columns(v):
        return v.reshape(-1, P).T

    w_stream = np.concatenate([stream(w) for w in (L["er_W1"].T, top1[OUT:], L["ei_W1"].T, L["er_W2"].T, L["ei_W2"].T)])
    b_top2 = np.concatenate([np.asarray(i["b_top2"]), np.zeros(D - TOP2, np.float32)])
    out = {
        "w_stream": w_stream.reshape(-1, P, 2, 512),
        "x_t": chunks(np.asarray(i["r_x"]).T),
        "enc_cols": np.stack([np.stack([columns(L[e + n]) for n in ("_b1", "_g1", "_be1", "_b2")], 1) for e in ("er", "ei")], 1),
        "w_proj": np.stack([chunks(L[f"W{n}_{e}"].T) for n in "qkvo" for e in "ri"]),
        "bias_rows": np.stack([L[f"b{n}_{e}"] for n in "qkv" for e in "ri"]),
        "out_cols": np.stack([columns(L[f"bo_{e}"]) for e in "ri"], 1),
        "identity": np.eye(P, dtype=np.float32),
        "w_int": np.stack([chunks(L[f"int_W{e}"][n].T) for n in range(N) for e in "ri"]),
        "ids_t": np.asarray(i["ids"]).reshape(TILES, P, N).transpose(1, 0, 2),
        "w_tail": np.stack([chunks(w) for w in (L["meas_Mr"].T, L["meas_Mi"].T, L["post_W"].T, top1[:OUT])]),
        "w_top2": chunks(top2),
        "w_top3": columns(top3.reshape(-1)),
        "tail_cols": np.stack([columns(v) for v in (L["post_b"], L["post_g"], L["post_be"], np.asarray(i["b_top1"]), b_top2)], 1),
    }
    out.update({f"tbl_{n}": np.asarray(i[f"tbl_{n}"]) for n in range(N)})
    return {k: np.ascontiguousarray(v) for k, v in out.items()}


def kernel(**inputs):
    import numpy as np
    import concourse.bacc as bacc
    from concourse.bass_utils import run_bass_kernel_spmd

    nc = bacc.Bacc("TRN2", target_bir_lowering=False, num_devices=1)
    arrays = {f"in_{k}": v for k, v in lay_out(np, inputs).items()}
    a = {k[3:]: nc.dram_tensor(k, v.shape, mybir.dt.from_np(v.dtype), kind="ExternalInput").ap() for k, v in arrays.items()}
    y = nc.dram_tensor("y_out", (1, BATCH), F32, kind="ExternalOutput").ap()
    tower(nc, a, y)
    r = run_bass_kernel_spmd(nc, [arrays], core_ids=[0])
    return r.results[0]["y_out"].reshape(BATCH, 1)
```

```python
from contextlib import ExitStack

import concourse.bass as bass
from concourse import mybir

F32 = mybir.dt.float32
F32R = mybir.dt.float32r
I32 = mybir.dt.int32
U32 = mybir.dt.uint32
ALU = mybir.AluOpType
ACT = mybir.ActivationFunctionType
AX_X = mybir.AxisListType.X

P = 128
BATCH, IN, HID, D, N, OUT, HEADS, TOP2 = 1024, 2048, 2048, 512, 4, 512, 8, 256
HD = D // HEADS
CK = D // P
TILES = BATCH // P
EPS = 1e-5



def encoders(nc, sem, dram, w_stream, x_t, enc_cols):
    KT = IN // P
    SLOTS = KT // 2
    HALVES, BH = 2, BATCH // 2
    CH = 4
    G_S1R, G_TOP, G_S1I, G_S2R, G_S2I, GROUPS = 0, 4, 5, 9, 13, 17
    PAIRS = GROUPS * SLOTS

    with ExitStack() as ctx:
        def sb(name, shape, dt=F32):
            return ctx.enter_context(nc.sbuf_tensor(name, shape, dt))

        x_hi, x_lo = sb("x_hi", [P, KT, BH], F32R), sb("x_lo", [P, KT, BH], F32R)
        h_hi, h_lo = sb("h_hi", [P, KT, BH], F32R), sb("h_lo", [P, KT, BH], F32R)
        z = sb("z", [P, KT, BH])
        w_raw = sb("w_raw", [P, 2, 2, 512])
        w_hi, w_lo = sb("w_hi", [P, 2, 2, 512], F32R), sb("w_lo", [P, 2, 2, 512], F32R)
        staged = sb("staged", [P, 2, 2, BH])
        scratch = sb("scratch", [P, 2, BH])
        colsum, rstd = sb("colsum", [P, BH]), sb("rstd", [P, BH])
        cols = sb("enc_columns", [P, 2, 4, KT])
        mean_w, eps = sb("mean_w", [P, P]), sb("eps", [P, 1])
        zeros = sb("zeros", [P, BH])
        acc = ctx.enter_context(nc.psum_tensor("acc", [P, CH, 512], F32))
        stat = ctx.enter_context(nc.psum_tensor("stat", [P, 512], F32))

        raw_landed = [sem("raw_landed0"), sem("raw_landed1")]
        x_landed, cols_landed, consts = sem("x_landed"), sem("cols_landed"), sem("p1_consts")
        hi_ready, lo_ready = sem("w_hi_ready"), sem("w_lo_ready")
        pairs_used = sem("pairs_used")
        xhi_ready, xlo_ready = sem("xhi_ready"), sem("xlo_ready")
        acc_done, drained = sem("acc_done"), sem("drained")
        summed, stats_made = sem("summed"), sem("stats_made")
        centred, squared = sem("centred"), sem("squared")
        std_made, rstd_made = sem("std_made"), sem("rstd_made")
        scaled, gelued = sem("scaled"), sem("gelued")
        hhi_ready, hlo_ready = sem("hhi_ready"), sem("hlo_ready")
        shi_ready = sem("shi_ready")
        sent = [sem("sent0"), sem("sent1")]
        block = ctx.enter_context(nc.Block())

        SUMS = 4 * (1 + KT)

        def pair(half, g, s):
            return half * PAIRS + g * SLOTS + s

        def unit(half, g, c):
            return half * (GROUPS * CH) + g * CH + c

        def sends(half, g, c):
            j = 0 if isinstance(g, int) and g == G_TOP else (g - G_S2R) * 2 + 2
            return half * 18 + j + c // 2

        def schedule(run):
            for first, last in ((0, 0), (1, 3), (4, 4), (5, 5), (6, 6), (7, 8), (9, 9), (10, 11),
                                (12, 12), (13, 13), (14, 16)):
                run(first, last)

        def kind(g):
            return "top" if g == G_TOP else ("s1" if g < G_S2R else "s2")

        def norm1(g, s):
            if g not in (G_TOP, G_S2R) or s < 2:
                return 0, ()
            cut = (0, 3, 6, 9, 12, 14, 16)
            return int(g == G_S2R), range(cut[s - 2], cut[s - 1])

        def norm2(g, s):
            e = int(g in (G_S2R + 3, G_S2I))
            if g in (G_S1I, G_S2R + 3) and s >= 2:
                return e, range(2 * s - 4, 2 * s - 2)
            if g in (G_S1I + 1, G_S2I) and s < 2:
                return e, range(12 + 2 * s, 14 + 2 * s)
            return e, ()

        @block.sync
        def _(sp):
            sp.sem_inc(sent[0], 16)
            sp.sem_inc(sent[1], 16)
            sp.dma_start(cols[:, :, :, :], enc_cols).then_inc(cols_landed, 16)

            def out(half, g):
                for c in range(CH):
                    sp.wait_ge(drained, unit(half, g, c) + 5)
                    u = c % 2
                    if isinstance(g, int) and g == G_TOP:
                        dst = dram["top_x"][c, :, bass.ts(half, BH)]
                        sp.dma_start(dst, staged[:, u, 0, :]).then_inc(sent[u], 16)
                    else:
                        dst = dram["s"][(g - G_S2R) * CH + c][:, :, bass.ts(half, BH)]
                        sp.dma_start(dst.rearrange("a p b -> p a b"), staged[:, u, :, :]).then_inc(sent[u], 16)

            def group(half, g, before):
                for s in range(SLOTS):
                    sp.wait_ge(lo_ready, pair(half, g, s) + 1)
                    sp.dma_start(w_raw[:, s % 2, :, :], w_stream[g * SLOTS + s, :, :, :]).then_inc(raw_landed[s % 2], 16)
                    if isinstance(g, int) and g == 0:
                        sp.wait_ge(xlo_ready, half * SLOTS + s + 1)
                        sp.dma_start(scratch[:, :, :],
                                     x_t[2 * s:2 * s + 2, :, bass.ts(half, BH)].rearrange("k p b -> p k b")
                                     ).then_inc(x_landed, 16)
                    if s == 2 and before in ("top", "s2"):
                        out(half, g - 1)

            with nc.sync.Fori(0, HALVES) as half:
                def run(first, last):
                    before = kind(first - 1) if first else None
                    if first == last:
                        group(half, first, before)
                    else:
                        with nc.sync.Fori(first, last + 1) as g:
                            group(half, g, before)
                schedule(run)
                out(half, GROUPS - 1)
            for u in range(2):
                sp.wait_ge(sent[u], 16 * (18 * HALVES + 1))

        @block.scalar
        def _(act):
            act.wait_ge(cols_landed, 16)
            act.wait_ge(consts, 3)

            def drain(half, g, what):
                for c in range(CH):
                    if c < CH - 1:
                        act.wait_ge(acc_done, (half * GROUPS + g) * (CH - 1) + c + 1)
                    else:
                        act.wait_ge(pairs_used, pair(half, g, SLOTS - 1) + 3)
                    if what == "top":
                        act.wait_ge(sent[c % 2], 16 * (sends(half, g, c) + 1))
                        nc.scalar.activation(staged[:, c % 2, 0, :], acc[:, c, :], ACT.Copy).then_inc(drained, 1)
                    elif what == "s2r" or what == "s2i":
                        e = int(what == "s2i")
                        col = (g - (G_S2I if e else G_S2R)) * CH + c
                        act.wait_ge(sent[c % 2], 16 * (sends(half, g, c) + 1))
                        nc.scalar.activation(staged[:, c % 2, 0, :].bitcast(F32R), acc[:, c, :], ACT.Identity,
                                             bias=cols[:, e, 3, bass.ds(col, 1)]).then_inc(shi_ready, 1)
                    else:
                        e = int(what == "s1i")
                        col = (g - (G_S1I if e else G_S1R)) * CH + c
                        if e:
                            act.wait_ge(hlo_ready, half * 32 + col + 1)
                        nc.scalar.activation(z[:, bass.ds(col, 1), :], acc[:, c:c + 1, :], ACT.Identity,
                                             bias=cols[:, e, 0, bass.ds(col, 1)]).then_inc(drained, 1)

            def group(half, g, before):
                for s in range(SLOTS):
                    u = s % 2
                    act.wait_ge(raw_landed[u], 16 * (half * (PAIRS // 2) + g * (SLOTS // 2) + s // 2 + 1))
                    act.wait_ge(pairs_used, pair(half, g, s) + 1)
                    nc.scalar.activation(w_hi[:, u, :, :], w_raw[:, u, :, :], ACT.Copy).then_inc(hi_ready, 1)
                    if isinstance(g, int) and g == 0:
                        act.wait_ge(x_landed, 16 * (half * SLOTS + s + 1))
                        nc.scalar.activation(x_hi[:, 2 * s:2 * s + 2, :], scratch[:, :, :], ACT.Copy).then_inc(xhi_ready, 1)
                    if s == 0 and before:
                        drain(half, g - 1, before)
                    if not isinstance(g, int):
                        continue
                    e, chunks = norm1(g, s)
                    for i in chunks:
                        act.wait_ge(centred, half * 32 + e * KT + i + 1)
                        if i >= 2:
                            act.wait_ge(summed, half * SUMS + (2 * e + 1) * (1 + KT) + i)
                        nc.scalar.activation(scratch[:, i % 2, :], z[:, i, :], ACT.Square).then_inc(squared, 1)
                    if g in (G_S1I, G_S2R + 3) and s == 1:
                        e = int(g != G_S1I)
                        act.wait_ge(stats_made, half * 4 + 2 * e + 3)
                        nc.scalar.activation(rstd[:, :], stat[:, :], ACT.Sqrt, bias=eps[:, :]).then_inc(std_made, 1)
                    e, chunks = norm2(g, s)
                    for i in chunks:
                        act.wait_ge(scaled, half * 32 + e * KT + i + 1)
                        nc.scalar.activation(z[:, i, :], z[:, i, :], ACT.Gelu, bias=cols[:, e, 2, i:i + 1],
                                             scale=cols[:, e, 1, i:i + 1]).then_inc(gelued, 1)
                    for i in chunks:
                        act.wait_ge(gelued, half * 32 + e * KT + i + 1)
                        nc.scalar.activation(h_hi[:, i, :], z[:, i, :], ACT.Copy).then_inc(hhi_ready, 1)

            def what(g):
                return {0: "s1r", 4: "top", 5: "s1i", 9: "s2r", 13: "s2i"}[max(b for b in (0, 4, 5, 9, 13) if b <= g)]

            with nc.scalar.Fori(0, HALVES) as half:
                def run(first, last):
                    before = what(first - 1) if first else None
                    if first == last:
                        group(half, first, before)
                    else:
                        with nc.scalar.Fori(first, last + 1) as g:
                            group(half, g, before)
                schedule(run)
                drain(half, GROUPS - 1, "s2i")

        @block.vector
        def _(dve):
            dve.wait_ge(cols_landed, 16)
            dve.sem_inc(lo_ready, 2)
            dve.sem_inc(xlo_ready, 1)
            dve.sem_inc(drained, CH)
            nc.vector.memset(mean_w[:, :], 1.0 / HID).then_inc(consts, 1)
            nc.vector.memset(eps[:, :], EPS).then_inc(consts, 1)
            nc.vector.memset(zeros[:, :], 0.0).then_inc(consts, 1)

            def group(half, g, before):
                for s in range(SLOTS):
                    u = s % 2
                    dve.wait_ge(hi_ready, pair(half, g, s) + 1)
                    nc.vector.tensor_tensor(w_lo[:, u, :, :], w_raw[:, u, :, :], w_hi[:, u, :, :].bitcast(F32),
                                            ALU.subtract).then_inc(lo_ready, 1)
                    if isinstance(g, int) and g == 0:
                        dve.wait_ge(xhi_ready, half * SLOTS + s + 1)
                        nc.vector.tensor_tensor(x_lo[:, 2 * s:2 * s + 2, :], scratch[:, :, :],
                                                x_hi[:, 2 * s:2 * s + 2, :].bitcast(F32),
                                                ALU.subtract).then_inc(xlo_ready, 1)
                    if s == 0 and before:
                        drain(half, g - 1, before)
                    if not isinstance(g, int):
                        continue
                    e, chunks = norm1(g, s)
                    if chunks and s == 2:
                        dve.wait_ge(stats_made, half * 4 + 2 * e + 2)
                    for i in chunks:
                        nc.vector.tensor_tensor(z[:, i, :], z[:, i, :], stat[:, :], ALU.subtract).then_inc(centred, 1)
                    if g in (G_S1I, G_S2R + 3) and s == 1:
                        e = int(g != G_S1I)
                        dve.wait_ge(std_made, half * 2 + e + 1)
                        nc.vector.reciprocal(rstd[:, :], rstd[:, :]).then_inc(rstd_made, 1)
                    e, chunks = norm2(g, s)
                    for i in chunks:
                        dve.wait_ge(hhi_ready, half * 32 + e * KT + i + 1)
                        nc.vector.tensor_tensor(h_lo[:, i, :], z[:, i, :], h_hi[:, i, :].bitcast(F32),
                                                ALU.subtract).then_inc(hlo_ready, 1)

            def drain(half, g, what):
                if what != "s2r" and what != "s2i":
                    return
                e = int(what == "s2i")
                for c in range(CH):
                    col = (g - (G_S2I if e else G_S2R)) * CH + c
                    dve.wait_ge(shi_ready, half * 32 + (g - G_S2R) * CH + c + 1)
                    nc.vector.scalar_tensor_tensor(
                        staged[:, c % 2, 1, :].bitcast(F32R), acc[:, c, :], cols[:, e, 3, bass.ds(col, 1)],
                        staged[:, c % 2, 0, :], ALU.add, ALU.subtract).then_inc(drained, 1)

            def what(g):
                return {0: "s1", 9: "s2r", 13: "s2i"}[max(b for b in (0, 9, 13) if b <= g)]

            with nc.vector.Fori(0, HALVES) as half:
                def run(first, last):
                    before = what(first - 1) if first else None
                    if first == last:
                        group(half, first, before)
                    else:
                        with nc.vector.Fori(first, last + 1) as g:
                            group(half, g, before)
                schedule(run)
                drain(half, GROUPS - 1, "s2i")

        @block.gpsimd
        def _(pool):
            def clear(half, n):
                pool.wait_ge(stats_made, half * 4 + n + 1)
                nc.gpsimd.tensor_tensor(colsum[:, :], zeros[:, :], zeros[:, :], ALU.add).then_inc(summed, 1)

            def add(half, n, i, src, sq=None):
                pool.wait_ge(summed, half * SUMS + n * (1 + KT) + i + 1)
                nc.gpsimd.tensor_tensor(colsum[:, :], colsum[:, :], src, ALU.add).then_inc(summed, 1)

            pool.wait_ge(consts, 3)
            with nc.gpsimd.Fori(0, HALVES) as half:
                for e, g0 in ((0, G_S1R), (1, G_S1I)):
                    clear(half, 2 * e)
                    with nc.gpsimd.Fori(0, 4) as q:
                        for c in range(CH):
                            pool.wait_ge(drained, half * (GROUPS * CH) + g0 * CH + q * CH + c + 5)
                            add(half, 2 * e, q * CH + c, z[:, bass.ds(q * CH + c, 1), :])
                    clear(half, 2 * e + 1)
                    with nc.gpsimd.Fori(0, KT // 2) as q:
                        for u in range(2):
                            pool.wait_ge(squared, half * 32 + e * KT + q * 2 + u + 1)
                            add(half, 2 * e + 1, q * 2 + u, scratch[:, u, :])
                    with nc.gpsimd.Fori(0, KT) as i:
                        pool.wait_ge(rstd_made, half * 2 + e + 1)
                        nc.gpsimd.tensor_tensor(z[:, bass.ds(i, 1), :], z[:, bass.ds(i, 1), :],
                                                rstd[:, :].unsqueeze(1), ALU.mult).then_inc(scaled, 1)

        @block.tensor
        def _(pe):
            pe.sem_inc(pairs_used, 2)
            pe.sem_inc(stats_made, 1)
            pe.wait_ge(consts, 3)

            def statistic(half, n):
                pe.wait_ge(summed, half * SUMS + (n + 1) * (1 + KT))
                nc.tensor.matmul(stat[:, :], mean_w[:, :], colsum[:, :], start=True, stop=True).then_inc(stats_made, 1)

            sums_at = {(G_TOP, 1): 0, (G_S1I, 0): 1, (G_S2R, 1): 2, (G_S2R + 3, 0): 3}

            def group(half, g, moving):
                a_hi, a_lo = moving
                for s in range(SLOTS):
                    pe.wait_ge(lo_ready, pair(half, g, s) + 3)
                    if isinstance(g, int) and g == G_S1R:
                        pe.wait_ge(xlo_ready, half * SLOTS + s + 2)
                    if isinstance(g, int) and g == G_S2R and s == 0:
                        pe.wait_ge(hlo_ready, half * 32 + KT)
                    if isinstance(g, int) and g == G_S2I:
                        pe.wait_ge(hlo_ready, half * 32 + KT + 2 * s + 2)
                    for c in range(CH):
                        if s == 0:
                            pe.wait_ge(drained, unit(half, g, c) + 1)
                        for kk in range(2):
                            k = 2 * s + kk
                            for n, (a, b) in enumerate(((w_hi, a_hi), (w_hi, a_lo), (w_lo, a_hi))):
                                last = nc.tensor.matmul(acc[:, c, :], a[:, s % 2, kk, c * P:(c + 1) * P], b[:, k, :],
                                                        start=(k == 0 and n == 0), stop=(k == KT - 1 and n == 2))
                        if s == SLOTS - 1 and c < CH - 1:
                            last.then_inc(acc_done, 1)
                    last.then_inc(pairs_used, 1)
                    if isinstance(g, int) and (g, s) in sums_at:
                        statistic(half, sums_at[g, s])

            with nc.tensor.Fori(0, HALVES) as half:
                def run(first, last):
                    moving = (x_hi, x_lo) if first < G_S2R else (h_hi, h_lo)
                    if first == last:
                        group(half, first, moving)
                    else:
                        with nc.tensor.Fori(first, last + 1) as g:
                            group(half, g, moving)
                schedule(run)



def attention(nc, sem, dram, w_proj, bias_rows, out_cols, identity):
    with ExitStack() as ctx:
        w_hi = ctx.enter_context(nc.sbuf_tensor("proj_w_hi", [P, 4, CK, D], F32R))
        w_lo = ctx.enter_context(nc.sbuf_tensor("proj_w_lo", [P, 4, CK, D], F32R))
        w_soft = ctx.enter_context(nc.sbuf_tensor("w_soft", [P, TILES, N * N * HEADS], F32))
        scores(nc, sem, dram, w_proj, bias_rows, w_hi, w_lo, w_soft)
        attend(nc, sem, dram, bias_rows, out_cols, identity, w_hi, w_lo, w_soft)


def scores(nc, sem, dram, w_proj, bias_rows, w_hi, w_lo, w_soft):
    with ExitStack() as ctx:
        def sb(name, shape, dt=F32):
            return ctx.enter_context(nc.sbuf_tensor(name, shape, dt))

        MATS = 4
        UNITS = 2 * N * 2
        RING = 4
        bias = sb("qk_bias", [P, MATS, D])
        s_in = sb("qk_s", [P, RING, CK, 2, P], F32R)
        qk = sb("qk", [P, 2, 2, 2, N, D])
        mixed = sb("qk_mixed", [P, 2, N, D])
        prod = sb("qk_prod", [P, 3, N, D])
        dots = [w_soft] + [sb(f"qk_dots{i}", [P, TILES, N * N * HEADS]) for i in (1, 2)]
        tiny = sb("qk_tiny", [P, 1])
        ps = ctx.enter_context(nc.psum_tensor("qk_ps", [P, 8, D], F32))
        w_landed, bias_landed = [sem(f"qk_w_landed{i}") for i in range(MATS)], sem("qk_bias_landed")
        w_hi_made, w_lo_made = sem("qk_w_hi_made"), sem("qk_w_lo_made")
        s_landed = [sem(f"qk_s_landed{i}") for i in range(RING)]
        s_used = sem("qk_s_used")
        made, evicted = sem("qk_made"), sem("qk_evicted")
        mixes = sem("qk_mixes")
        pooled, reduced = sem("qk_pooled"), sem("qk_reduced")
        own_product, own_reduced = sem("qk_own_product"), sem("qk_own_reduced")
        soft, acted = sem("qk_soft"), sem("qk_acted")
        block = ctx.enter_context(nc.Block())

        LAG = UNITS + 3
        ORDER = (0, 2, 1, 3)

        def stages(fori, run):
            run(0, 0)
            run(1, 1)
            with fori(1, TILES // 2) as q:
                run(2 * q, 0)
                run(2 * q + 1, 1)
            run(TILES, 0)
            run(TILES + 1, 1)

        def live(t, u, lag):
            return not isinstance(t, int) or 0 <= t * UNITS + u - lag < TILES * UNITS

        def mat(j, e):
            return 2 * j + e

        def raw(par, m):
            return qk[:, par, m // 2, m % 2, :, :]

        @block.sync
        def _(sp):
            for m in ORDER:
                sp.dma_start(raw(1, m), w_proj[m, :, :, :].rearrange("c p o -> p c o")).then_inc(w_landed[m], 16)
            sp.dma_start(bias[:, :, :], bias_rows[0:MATS, :].unsqueeze(0).broadcast_to([P, MATS, D])).then_inc(bias_landed, 16)
            with nc.sync.Fori(0, TILES) as t:
                for n in range(N):
                    for e in range(2):
                        i = 2 * n + e
                        sp.wait_ge(s_used, t * 2 * N + i + 1)
                        src = dram["s"][(e * N + n) * CK:(e * N + n + 1) * CK, :, :, bass.ts(t, P)]
                        for c in range(CK):
                            sp.dma_start(s_in[:, i % RING, c, :, :].bitcast(F32),
                                         src[c].rearrange("a p b -> p a b")).then_inc(s_landed[i % RING], 16)
            sp.wait_ge(pooled, (TILES - 1) * 2 * N)
            for m in range(MATS):
                sp.dma_start(raw(0, m), w_proj[MATS + m, :, :, :].rearrange("c p o -> p c o")).then_inc(w_landed[m], 16)

        @block.scalar
        def _(act):
            for m in ORDER:
                act.wait_ge(w_landed[m], 16)
                nc.scalar.activation(w_hi[:, m, :, :], raw(1, m), ACT.Copy).then_inc(w_hi_made, 1)
            act.wait_ge(s_used, RING + TILES * 2 * N)
            for m in range(MATS):
                act.wait_ge(w_landed[m], 32)
                nc.scalar.activation(w_hi[:, m, :, :], raw(0, m), ACT.Copy).then_inc(w_hi_made, 1)
            act.wait_ge(soft, 7)
            nc.scalar.activation(w_soft[:, :, :], w_soft[:, :, :], ACT.Sqrt, bias=tiny[:, :],
                                 scale=1.0 / HD).then_inc(acted, 1)
            act.wait_ge(soft, 9)
            nc.scalar.activation(w_soft[:, :, :], w_soft[:, :, :], ACT.Exp).then_inc(acted, 1)

        @block.tensor
        def _(pe):
            pe.sem_inc(s_used, RING)
            with nc.tensor.Fori(0, TILES) as t:
                for n in range(N):
                    for e in range(2):
                        i = 2 * n + e
                        pe.wait_ge(s_landed[i % RING], 16 * CK * (t * 2 + i // RING + 1))
                        for j in range(2):
                            u = 2 * i + j
                            pe.wait_ge(w_lo_made, ORDER.index(mat(j, e)) + 1)
                            pe.wait_ge(evicted, t * UNITS + u + 1)
                            k = 0
                            for c in range(CK):
                                for a, b in ((0, w_hi), (1, w_hi), (0, w_lo)):
                                    last = nc.tensor.matmul(ps[:, u % 8, :], s_in[:, i % RING, c, a, :],
                                                            b[:, mat(j, e), c, :], start=(k == 0), stop=(k == 3 * CK - 1))
                                    k += 1
                            last.then_inc(s_used if j else made, 1)

        @block.vector
        def _(dve):
            dve.sem_inc(evicted, 8)
            dve.sem_inc(reduced, 2)
            dve.sem_inc(own_reduced, 1)
            nc.vector.memset(tiny[:, :], 1e-8 / HD)
            for i, m in enumerate(ORDER):
                dve.wait_ge(w_hi_made, i + 1)
                nc.vector.tensor_tensor(w_lo[:, m, :, :], raw(1, m), w_hi[:, m, :, :].bitcast(F32),
                                        ALU.subtract).then_inc(w_lo_made, 1)
            dve.wait_ge(bias_landed, 16)

            def evict(t, par, u):
                i, j = u // 2, u % 2
                n, e = i // 2, i % 2
                dve.wait_ge(s_used if j else made, t * 2 * N + i + 1 + (RING if j else 0))
                if u == 0 and not (isinstance(t, int) and t < 2):
                    dve.wait_ge(pooled, (t - 1) * 2 * N)
                if isinstance(t, int) and t == 1 and u == 0:
                    dve.wait_ge(w_lo_made, MATS)
                nc.vector.tensor_tensor(qk[:, par, j, e, n, :], ps[:, u % 8, :], bias[:, mat(j, e), :],
                                        ALU.add).then_inc(evicted, 1)

            def dot(t, n, what):
                if what == 1:
                    if n == 0:
                        dve.wait_ge(mixes, t * 2 + 2)
                    dve.wait_ge(own_reduced, t * N + n + 1)
                    nc.vector.tensor_tensor(prod[:, 2, :, :], mixed[:, 0, n:n + 1, :].broadcast_to([P, N, D]),
                                            mixed[:, 1, :, :], ALU.mult).then_inc(own_product, 1)
                    return
                kind = {0: 0, 3: 1, 2: 2}[what]
                if kind < 2:
                    dve.wait_ge(pooled, t * 2 * N + n * 2 + kind + 1)
                else:
                    dve.wait_ge(own_product, t * N + n + 1)
                W = N * HEADS
                nc.vector.tensor_reduce(
                    dots[kind][:, bass.ds(t, 1), n * W:(n + 1) * W].rearrange("p t w -> p (t w)"),
                    prod[:, kind, :, :].rearrange("p m (h d) -> p (m h) d", d=HD), AX_X,
                    ALU.add).then_inc(own_reduced if kind == 2 else reduced, 1)

            def stage(t, par):
                for u in range(UNITS):
                    if live(t, u, 0):
                        evict(t, par, u)
                    if live(t, u, LAG):
                        v = (u - LAG) % UNITS
                        dot(t - 1 if u >= LAG - UNITS else t - 2, v // 4, v % 4)
                    if isinstance(t, int) and t == TILES and u % 4 == 3:
                        m = u // 4
                        dve.wait_ge(w_hi_made, MATS + m + 1)
                        nc.vector.tensor_tensor(w_lo[:, m, :, :], raw(0, m), w_hi[:, m, :, :].bitcast(F32),
                                                ALU.subtract).then_inc(w_lo_made, 1)

            stages(nc.vector.Fori, stage)

            steps = [0]

            def link(ins):
                steps[0] += 1
                ins.then_inc(soft, 1)
                dve.wait_ge(soft, steps[0])

            a, b, c = (kind[:, :, :] for kind in dots)
            most = mixed[:, 0, 0, 0:TILES * N * HEADS]
            dve.wait_ge(own_reduced, TILES * N + 1)
            dve.wait_ge(reduced, TILES * 2 * N + 2)
            link(nc.vector.tensor_tensor(c, c, a, ALU.subtract))
            link(nc.vector.tensor_tensor(c, c, b, ALU.add))
            link(nc.vector.tensor_tensor(a, a, b, ALU.add))
            link(nc.vector.tensor_tensor(c, c, c, ALU.mult))
            link(nc.vector.tensor_tensor(a, a, a, ALU.mult))
            link(nc.vector.tensor_tensor(a, a, c, ALU.add))
            nc.vector.tensor_copy(tiny[:, :], tiny[:, :]).then_inc(soft, 1)
            steps[0] += 1
            dve.wait_ge(acted, 1)
            flat = a.rearrange("p t (n m h) -> p (t n) m h", m=N, h=HEADS)
            by_m = flat.rearrange("p x m h -> p x h m")
            m3 = most.rearrange("p (x h) -> p x h", h=HEADS)
            link(nc.vector.tensor_reduce(m3, by_m, AX_X, ALU.max))
            spread = m3.unsqueeze(2).broadcast_to([P, TILES * N, N, HEADS])
            nc.vector.tensor_tensor(flat, flat, spread, ALU.subtract).then_inc(soft, 1)
            steps[0] += 1
            dve.wait_ge(acted, 2)
            link(nc.vector.tensor_reduce(m3, by_m, AX_X, ALU.add))
            link(nc.vector.reciprocal(most, most))
            link(nc.vector.tensor_tensor(flat, flat, spread, ALU.mult))

        @block.gpsimd
        def _(pool):
            def work(t, par):
                def product(n, e):
                    pool.wait_ge(reduced, t * 2 * N + n * 2 + e + 1)
                    nc.gpsimd.tensor_tensor(prod[:, e, :, :],
                                            qk[:, par, 0, e, n:n + 1, :].broadcast_to([P, N, D]),
                                            qk[:, par, 1, e, :, :], ALU.mult).then_inc(pooled, 1)

                pool.wait_ge(evicted, t * UNITS + UNITS - 2 + 8)
                product(0, 0)
                pool.wait_ge(evicted, t * UNITS + UNITS + 8)
                for j, op in ((0, ALU.add), (1, ALU.subtract)):
                    if not (isinstance(t, int) and t == 0):
                        pool.wait_ge(own_product, t * N)
                    nc.gpsimd.tensor_tensor(mixed[:, j, :, :], qk[:, par, j, 0, :, :], qk[:, par, j, 1, :, :], op).then_inc(mixes, 1)
                product(0, 1)
                for n in range(1, N):
                    product(n, 0)
                    product(n, 1)

            work(0, 0)
            with nc.gpsimd.Fori(0, TILES // 2 - 1) as q:
                work(2 * q + 1, 1)
                work(2 * q + 2, 0)
            work(TILES - 1, 1)


def attend(nc, sem, dram, bias_rows, out_cols, identity, w_hi, w_lo, w_soft):
    with ExitStack() as ctx:
        def sb(name, shape, dt=F32):
            return ctx.enter_context(nc.sbuf_tensor(name, shape, dt))

        UNITS = 2 * N
        RING = 4
        bias = sb("v_bias", [P, 2, D])
        o_bias = sb("o_bias", [P, 2, CK])
        ident = sb("ident", [P, P])
        s_in = sb("v_s", [P, RING, CK, 2, P], F32R)
        v = sb("v", [P, 2, 2, N, D])
        w_tile = sb("w_tile", [P, 2, N * N * HEADS])
        prod = sb("v_prod", [P, 2, N, D])
        mixed = sb("v_mixed", [P, 2, D])
        m_hi = sb("m_hi", [P, 2, CK, N, P], F32R)
        m_lo = sb("m_lo", [P, 2, CK, N, P], F32R)
        staged = sb("attn_staged", [P, 2, 2, N, P])
        ps_v = ctx.enter_context(nc.psum_tensor("ps_v", [P, 4, D], F32))
        ps_t = ctx.enter_context(nc.psum_tensor("ps_t", [P, 2, CK, P], F32))
        ps_o = ctx.enter_context(nc.psum_tensor("ps_o", [P, 2, N, P], F32))
        consts_landed = sem("v_consts_landed")
        s_landed = [sem(f"v_s_landed{i}") for i in range(RING)]
        v_made, evicted = sem("v_made"), sem("v_evicted")
        pooled, halved, mixes = sem("v_pooled"), sem("v_halved"), sem("v_mixes")
        turned, t_hi, t_lo = sem("turned"), sem("t_hi"), sem("t_lo")
        w_picked = sem("w_picked")
        o_made, o_hi, o_lo = sem("o_made"), sem("o_hi"), sem("o_lo")
        sent = [sem("attn_sent0"), sem("attn_sent1")]
        block = ctx.enter_context(nc.Block())

        MIX, TURN, OUT, OUT_LO = UNITS, UNITS + 1, UNITS + N + 1, UNITS + N + 2

        def stages(fori, run):
            run(0, 0)
            run(1, 1)
            with fori(1, TILES // 2) as q:
                run(2 * q, 0)
                run(2 * q + 1, 1)
            run(TILES, 0)
            run(TILES + 1, 1)

        def live(t, u, lag):
            return not isinstance(t, int) or 0 <= t * UNITS + u - lag < TILES * UNITS

        def piece_of(t, u, lag):
            v = u + 2 * UNITS - lag
            w = v % UNITS
            return (t - 2) * UNITS + v, (t - 2) * N + v // 2, t - 2 + v // UNITS, w // N, w % N

        @block.sync
        def _(sp):
            for u in range(2):
                sp.sem_inc(sent[u], 16)
            sp.dma_start(bias[:, :, :], bias_rows[4:6, :].unsqueeze(0).broadcast_to([P, 2, D])).then_inc(consts_landed, 16)
            sp.dma_start(o_bias[:, :, :], out_cols).then_inc(consts_landed, 16)
            sp.dma_start(ident[:, :], identity).then_inc(consts_landed, 16)

            with nc.sync.Fori(0, TILES) as t:
                for u in range(UNITS):
                    sp.wait_ge(v_made, t * UNITS + u + 1)
                    for c in range(CK):
                        src = dram["s"][u * CK + c][:, :, bass.ts(t, P)]
                        sp.dma_start(s_in[:, u % RING, c, :, :].bitcast(F32),
                                     src.rearrange("a p b -> p a b")).then_inc(s_landed[u % RING], 16)

        @block.scalar
        def _(act):
            act.wait_ge(consts_landed, 48)

            def stage(t, par):
                for u in range(UNITS):
                    if live(t, u, OUT_LO):
                        piece, before, tile, e, c = piece_of(t, u, OUT_LO)
                        act.wait_ge(o_lo, piece + 3)
                        for a in range(2):
                            act.dma_start(dram["attn"][e, c, a][:, :, bass.ts(tile, P)],
                                          staged[:, c % 2, a, :, :]).then_inc(sent[c % 2], 16)
                    if live(t, u, TURN):
                        x, w = (t - 1) * UNITS + u - 1, (u - 1) % UNITS
                        act.wait_ge(turned, x + 3)
                        nc.scalar.activation(m_hi[:, w // N, :, w % N, :], ps_t[:, w % 2, :, :],
                                             ACT.Copy).then_inc(t_hi, 1)
                    if live(t, u, OUT):
                        piece, before, tile, e, c = piece_of(t, u, OUT)
                        act.wait_ge(o_made, piece + 1)
                        act.wait_ge(sent[c % 2], before * 32 + 16)
                        nc.scalar.activation(staged[:, c % 2, 0, :, :].bitcast(F32R), ps_o[:, c % 2, :, :], ACT.Identity,
                                             bias=o_bias[:, e, c:c + 1]).then_inc(o_hi, 1)

            stages(nc.scalar.Fori, stage)
            for u in range(2):
                act.wait_ge(sent[u], 16 + 32 * 4 * TILES)

        @block.tensor
        def _(pe):
            pe.sem_inc(v_made, RING)
            pe.sem_inc(turned, 2)
            pe.wait_ge(consts_landed, 48)

            def stage(t, par):
                for u in range(UNITS):
                    e, n = u // N, u % N
                    if live(t, u, 0):
                        pe.wait_ge(s_landed[u % RING], 16 * CK * (t * 2 + u // RING + 1))
                        pe.wait_ge(evicted, t * UNITS + u + 1)
                        k = 0
                        for c in range(CK):
                            for a, b in ((0, w_hi), (1, w_hi), (0, w_lo)):
                                last = nc.tensor.matmul(ps_v[:, u % 4, :], s_in[:, u % RING, c, a, :], b[:, e, c, :],
                                                        start=(k == 0), stop=(k == 3 * CK - 1))
                                k += 1
                        last.then_inc(v_made, 1)
                    if live(t, u, TURN):
                        x, w = (t - 1) * UNITS + u - 1, (u - 1) % UNITS
                        pe.wait_ge(mixes, x + 3)
                        pe.wait_ge(t_lo, x + 1)
                        for c in range(CK):
                            last = nc.tensor.transpose(ps_t[:, w % 2, c, :], mixed[:, w % 2, c * P:(c + 1) * P], ident[:, :])
                        last.then_inc(turned, 1)
                    if live(t, u, OUT):
                        piece, before, tile, e, c = piece_of(t, u, OUT)
                        pe.wait_ge(t_lo, tile * UNITS + (e + 1) * N + 2)
                        pe.wait_ge(o_lo, piece + 1)
                        k = 0
                        for j in range(CK):
                            for a, b in ((w_hi, m_hi), (w_hi, m_lo), (w_lo, m_hi)):
                                last = nc.tensor.matmul(ps_o[:, c % 2, :, :], a[:, 2 + e, j, c * P:(c + 1) * P], b[:, e, j, :, :],
                                                        start=(k == 0), stop=(k == 3 * CK - 1))
                                k += 1
                        last.then_inc(o_made, 1)

            stages(nc.tensor.Fori, stage)

        @block.vector
        def _(dve):
            dve.sem_inc(evicted, 4)
            dve.sem_inc(mixes, 2)
            dve.sem_inc(t_lo, 2)
            dve.sem_inc(o_lo, 2)
            dve.wait_ge(consts_landed, 48)

            def stage(t, par):
                for u in range(UNITS):
                    if live(t, u, OUT_LO):
                        piece, before, tile, e, c = piece_of(t, u, OUT_LO)
                        dve.wait_ge(o_hi, piece + 1)
                        nc.vector.scalar_tensor_tensor(
                            staged[:, c % 2, 1, :, :].bitcast(F32R), ps_o[:, c % 2, :, :], o_bias[:, e, c:c + 1],
                            staged[:, c % 2, 0, :, :], ALU.add, ALU.subtract).then_inc(o_lo, 1)
                    if live(t, u, 0) and u == 0:
                        nc.vector.tensor_copy(w_tile[:, par:par + 1, :], w_soft[:, bass.ds(t, 1), :]).then_inc(w_picked, 1)
                    if live(t, u, MIX):
                        x = (t - 1) * UNITS + u
                        dve.wait_ge(pooled, x + 1)
                        nc.vector.tensor_tensor(prod[:, u % 2, 0:2, :], prod[:, u % 2, 0:2, :], prod[:, u % 2, 2:4, :],
                                                ALU.add).then_inc(halved, 1)
                    if live(t, u, 0):
                        dve.wait_ge(v_made, t * UNITS + u + 1 + RING)
                        nc.vector.tensor_tensor(v[:, par, u // N, u % N, :], ps_v[:, u % 4, :], bias[:, u // N, :],
                                                ALU.add).then_inc(evicted, 1)
                    if live(t, u, MIX):
                        dve.wait_ge(turned, x + 1)
                        dve.wait_ge(halved, x + 1)
                        nc.vector.tensor_tensor(mixed[:, u % 2, :], prod[:, u % 2, 0, :], prod[:, u % 2, 1, :],
                                                ALU.add).then_inc(mixes, 1)
                    if live(t, u, TURN):
                        x, w = (t - 1) * UNITS + u - 1, (u - 1) % UNITS
                        dve.wait_ge(t_hi, x + 1)
                        nc.vector.tensor_tensor(m_lo[:, w // N, :, w % N, :], ps_t[:, w % 2, :, :],
                                                m_hi[:, w // N, :, w % N, :].bitcast(F32),
                                                ALU.subtract).then_inc(t_lo, 1)

            stages(nc.vector.Fori, stage)

        @block.gpsimd
        def _(pool):
            def work(t, par):
                pool.wait_ge(w_picked, t + 1)
                for u in range(UNITS):
                    e, n = u // N, u % N
                    if n == 0:
                        pool.wait_ge(evicted, t * UNITS + (e + 1) * N + 4)
                    pool.wait_ge(mixes, t * UNITS + u + 1)
                    w = w_tile[:, par, n * N * HEADS:(n + 1) * N * HEADS]
                    nc.gpsimd.tensor_tensor(prod[:, u % 2, :, :].rearrange("p m (h d) -> p (m h) d", d=HD),
                                            v[:, par, e, :, :].rearrange("p m (h d) -> p (m h) d", d=HD),
                                            w.unsqueeze(2).broadcast_to([P, N * HEADS, HD]), ALU.mult).then_inc(pooled, 1)

            with nc.gpsimd.Fori(0, TILES // 2) as q:
                work(2 * q, 0)
                work(2 * q + 1, 1)



def superpose(nc, sem, dram, w_int, ids_t, tables, identity):
    with ExitStack() as ctx:
        def sb(name, shape, dt=F32):
            return ctx.enter_context(nc.sbuf_tensor(name, shape, dt))

        MATS, RING, Q = 2 * N, 4, 4
        w_hi = sb("int_w_hi", [P, MATS, CK, D], F32R)
        w_lo = sb("int_w_lo", [P, MATS, CK, D], F32R)
        a_in = sb("a_in", [P, RING, 2, 2, P], F32R)
        ri = sb("ri", [P, 2, 2, N, D])
        raw = ri[:, :, :, :, :].rearrange("p x e n d -> p (x e) n d")
        sq = sb("sq", [P, 2, 2, N, P])
        unit = sb("unit", [P, 2, 3, N, P])
        d = sb("d", [P, 6, P])
        d_part = sb("d_part", [P, 6, P])
        c_sum = sb("c_sum", [P, 2, N, P])
        sup = sb("sup_rows", [P, 2, D])
        turned = sb("sup_turned", [P, 2, CK, P])
        strength = sb("strength", [P, TILES, N, N])
        st = sb("strength_tile", [P, N, N])
        st_sum = sb("strength_sum", [P, N])
        ids = sb("ids_sb", [P, TILES, N], I32)
        ident = sb("ident3", [P, P])
        tiny = sb("tiny3", [P, 1])
        norm = sb("norm", [P, 2])
        ps = ctx.enter_context(nc.psum_tensor("ri_ps", [P, 2, 3, D], F32))
        ps_t = ctx.enter_context(nc.psum_tensor("sup_ps", [P, 2, CK, P], F32))
        w_landed = [sem(f"int_w_landed{i}") for i in range(4)]
        w_hi_made, w_lo_made = sem("int_w_hi_made"), sem("int_w_lo_made")
        consts_landed, gathered = sem("p3_consts_landed"), sem("gathered")
        a_landed = [sem(f"a_landed{i}") for i in range(RING)]
        a_used = sem("a_used")
        copied, ri_ready = sem("ri_copied"), sem("ri_ready")
        squares, mags, present = sem("sup_squares"), sem("mags"), sem("present")
        roots, guarded, inverted = sem("roots"), sem("guarded"), sem("inverted")
        units = sem("units")
        paired, parts, d_steps = sem("paired"), sem("d_parts"), sem("d_steps")
        mixing, c_made, products = sem("mixing"), sem("c_made"), sem("sup_products")
        folded, quarters = sem("folded"), sem("quarters")
        power, normed, sup_ready = sem("power"), sem("normed"), sem("sup_ready")
        sup_turned, sent = sem("sup_turned"), sem("sup_sent")
        out_copied = sem("sup_copied")
        picked, inv_norm = sem("picked"), sem("inv_norm")
        RUNS = ((0, 0, 1, 3), (3, 0, 2, 2), (5, 0, 3, 1))
        PAIR = {}
        for at, i0, j0, count in RUNS:
            for x in range(count):
                PAIR[i0 + x, j0 + x] = PAIR[j0 + x, i0 + x] = at + x
        block = ctx.enter_context(nc.Block())

        def stages(fori, run):
            run(0, 0, "m")
            run(1, 1, "ms")
            with fori(1, TILES // 2) as q:
                run(2 * q, 0, "ms")
                run(2 * q + 1, 1, "ms")
            run(TILES, 0, "s")

        @block.sync
        def _(sp):
            sp.sem_inc(sent, 16)
            for m in range(MATS):
                if m >= 4:
                    sp.wait_ge(w_lo_made, m - 3)
                sp.dma_start(raw[:, m % 4, :, :], w_int[m, :, :, :].rearrange("c p o -> p c o")).then_inc(w_landed[m % 4], 16)
                if m == 1:
                    sp.dma_start(ident[:, :], identity).then_inc(consts_landed, 16)
            with nc.sync.Fori(0, TILES) as t:
                for i in range(4 * N):
                    n, e, cp = i // 4, i // 2 % 2, i % 2
                    sp.wait_ge(a_used, t * 4 * N + i + 1)
                    for cc in range(2):
                        src = dram["attn"][e, 2 * cp + cc][:, :, n, bass.ts(t, P)]
                        sp.dma_start(a_in[:, i % RING, cc, :, :].bitcast(F32),
                                     src.rearrange("a p b -> p a b")).then_inc(a_landed[i % RING], 16)

        @block.gpsimd
        def _(pool):
            pool.sem_inc(units, 4)
            nc.gpsimd.dma_start(ids[:, :, :], ids_t).then_inc(gathered, 16)
            pool.wait_ge(gathered, 16)
            for t in range(TILES):
                for i in range(N):
                    nc.gpsimd.indirect_dma_start(
                        strength[:, t, i, :], None, tables[i],
                        bass.IndirectOffsetOnAxis(ap=ids[:, t, i:i + 1].bitcast(U32), axis=0)).then_inc(gathered, 16)

            def magnitude(t, par, q):
                k, b = t * Q + q, q % 2
                pool.wait_ge(squares, k + 1)
                nc.gpsimd.tensor_tensor(sq[:, b, 0, :, :], sq[:, b, 0, :, :], sq[:, b, 1, :, :], ALU.add).then_inc(mags, 1)

            def units_of(t, par, q):
                k, b = t * Q + q, q % 2
                pool.wait_ge(inverted, k + 1)
                pool.wait_ge(quarters, k + 1)
                for e in range(2):
                    nc.gpsimd.tensor_tensor(unit[:, b, e, :, :], ri[:, par, e, :, q * P:(q + 1) * P], sq[:, b, 1, :, :],
                                            ALU.mult).then_inc(units, 1)

            def pairs(t, par, q):
                k, b = t * Q + q, q % 2
                pool.wait_ge(units, 2 * k + 2 + 4)
                pool.wait_ge(c_made, k + 1)
                for at, i0, j0, count in RUNS:
                    nc.gpsimd.tensor_tensor(d[:, at:at + count, :], unit[:, b, 0, i0:i0 + count, :],
                                            unit[:, b, 0, j0:j0 + count, :], ALU.mult).then_inc(paired, 1)

            def product(t, par, q):
                k, b = t * Q + q, q % 2
                pool.wait_ge(c_made, k + 2)
                for e in range(2):
                    nc.gpsimd.tensor_tensor(unit[:, b, e, :, :], ri[:, par, e, :, q * P:(q + 1) * P], c_sum[:, b, :, :],
                                            ALU.mult).then_inc(products, 1)

            def tile(t, par):
                for step, q in ((magnitude, 0), (magnitude, 1), (units_of, 0), (pairs, 0), (units_of, 1),
                                (magnitude, 2), (pairs, 1), (product, 0), (units_of, 2), (magnitude, 3),
                                (pairs, 2), (product, 1), (units_of, 3), (pairs, 3), (product, 2), (product, 3)):
                    step(t, par, q)

            with nc.gpsimd.Fori(0, TILES // 2) as h:
                tile(2 * h, 0)
                tile(2 * h + 1, 1)

        @block.scalar
        def _(act):
            for m in range(MATS):
                act.wait_ge(w_landed[m % 4], 16 * (m // 4 + 1))
                nc.scalar.activation(w_hi[:, m, :, :], raw[:, m % 4, :, :], ACT.Copy).then_inc(w_hi_made, 1)

            def stage(t, par, has):
                def copy(n):
                    if "m" not in has:
                        return
                    if isinstance(t, int) and t < 2 and n == 0:
                        act.wait_ge(w_lo_made, MATS)
                    act.wait_ge(a_used, t * 4 * N + 4 * n + 4 + RING)
                    for e in range(2):
                        nc.scalar.activation(ri[:, par, e, n, :], ps[:, n % 2, 2 * e, :], ACT.Copy).then_inc(copied, 1)

                def square(q):
                    k, b = (t - 1) * Q + q, q % 2
                    act.wait_ge(ri_ready, t * N + 2)
                    act.wait_ge(units, 2 * k + 2)
                    nc.scalar.activation(sq[:, b, :, :, :].rearrange("p e n d -> p (e n) d"),
                                         ri[:, 1 - par, :, :, q * P:(q + 1) * P].rearrange("p e n d -> p (e n) d"),
                                         ACT.Square).then_inc(squares, 1)

                def root(q):
                    k, b = (t - 1) * Q + q, q % 2
                    act.wait_ge(mags, k + 1)
                    nc.scalar.activation(sq[:, b, 1, :, :], sq[:, b, 0, :, :], ACT.Sqrt).then_inc(roots, 1)

                copy(0)
                if "s" in has:
                    square(0), square(1), root(0), root(1)
                copy(1)
                if "s" in has:
                    square(2), root(2)
                copy(2)
                if "s" in has:
                    square(3), root(3)
                copy(3)
                if "s" in has:
                    act.wait_ge(power, 3 * t)
                    nc.scalar.activation(norm[:, 1:2], norm[:, 0:1], ACT.Sqrt, bias=tiny[:, :]).then_inc(normed, 1)
                    act.wait_ge(sup_turned, t + 1)
                    act.wait_ge(sent, 16 * t)
                    nc.scalar.activation(turned[:, :, :, :], ps_t[:, :, :, :], ACT.Copy).then_inc(out_copied, 1)
                    act.wait_ge(out_copied, t)
                    act.dma_start(dram["sup"][:, :, bass.ts(t - 1, P)].rearrange("c p b -> p c b"),
                                  turned[:, :, :, :].rearrange("p e c b -> p (e c) b")).then_inc(sent, 16)

            stages(nc.scalar.Fori, stage)
            act.wait_ge(sent, 16 * (TILES + 1))

        @block.tensor
        def _(pe):
            pe.sem_inc(a_used, RING)
            pe.sem_inc(sup_turned, 1)
            pe.wait_ge(consts_landed, 16)

            def turn(t):
                pe.wait_ge(sup_ready, t + 1)
                for i in range(2 * CK):
                    last = nc.tensor.transpose(ps_t[:, i // CK, i % CK, :], sup[:, i // CK, i % CK * P:(i % CK + 1) * P], ident[:, :])
                last.then_inc(sup_turned, 1)

            def maps(t, before=None):
                for i in range(4 * N):
                    if i == 4 and before is not None:
                        turn(before)
                    n, e, cp = i // 4, i // 2 % 2, i % 2
                    pe.wait_ge(a_landed[i % RING], 32 * (t * N + i // RING + 1))
                    pe.wait_ge(w_lo_made, 2 * n + 2)
                    if e == 0 and cp == 0:
                        pe.wait_ge(ri_ready, t * N + n + 1)
                    for to, m in ((e, e), (2, 1 - e)):
                        k = 0
                        for cc in range(2):
                            for a, b in ((0, w_hi), (1, w_hi), (0, w_lo)):
                                first = cp == 0 and k == 0 and (to < 2 or e == 0)
                                final = cp == 1 and k == 5 and (to < 2 or e == 1)
                                last = nc.tensor.matmul(ps[:, n % 2, (0, 1, 2)[to], :], a_in[:, i % RING, cc, a, :],
                                                        b[:, 2 * n + m, 2 * cp + cc, :], start=first, stop=final)
                                k += 1
                    last.then_inc(a_used, 1)

            maps(0)
            maps(1)
            with nc.tensor.Fori(2, TILES) as t:
                maps(t, before=t - 2)
            turn(TILES - 2)
            turn(TILES - 1)

        @block.vector
        def _(dve):
            dve.sem_inc(ri_ready, 2)
            dve.sem_inc(quarters, 2)
            dve.sem_inc(c_made, 1)
            nc.vector.memset(tiny[:, :], 1e-8)
            for m in range(MATS):
                dve.wait_ge(w_hi_made, m + 1)
                nc.vector.tensor_tensor(w_lo[:, m, :, :], raw[:, m % 4, :, :], w_hi[:, m, :, :].bitcast(F32),
                                        ALU.subtract).then_inc(w_lo_made, 1)
            dve.wait_ge(gathered, 16 * (1 + TILES * N))
            MIX = N * (N - 1) - 1

            def stage(t, par, has):
                def finish(n):
                    if "m" in has:
                        dve.wait_ge(copied, 2 * (t * N + n) + 2)
                        nc.vector.tensor_tensor(ri[:, par, 0, n, :], ri[:, par, 0, n, :], ps[:, n % 2, 1, :],
                                                ALU.subtract).then_inc(ri_ready, 1)

                def invert(q):
                    k, b = (t - 1) * Q + q, q % 2
                    dve.wait_ge(roots, k + 1)
                    dve.wait_ge(quarters, k + 1)
                    nc.vector.tensor_scalar(unit[:, b, 2, :, :], sq[:, b, 1, :, :], 0.0, None, ALU.is_gt).then_inc(present, 1)
                    dve.wait_ge(present, k + 1)
                    nc.vector.scalar_tensor_tensor(sq[:, b, 1, :, :], sq[:, b, 1, :, :], 0.0, sq[:, b, 1, :, :],
                                                   ALU.is_equal, ALU.add).then_inc(guarded, 1)
                    dve.wait_ge(guarded, k + 1)
                    nc.vector.reciprocal(sq[:, b, 1, :, :], sq[:, b, 1, :, :]).then_inc(inverted, 1)

                def mix(q):
                    k, b = (t - 1) * Q + q, q % 2
                    dve.wait_ge(units, 2 * k + 2 + 4)

                    def part(e):
                        if not (isinstance(k, int) and k == 0 and e == 1):
                            dve.wait_ge(d_steps, k * 2 + (e == 2))
                        for at, i0, j0, count in RUNS:
                            nc.vector.tensor_tensor(d_part[:, at:at + count, :], unit[:, b, e, i0:i0 + count, :],
                                                    unit[:, b, e, j0:j0 + count, :], ALU.mult).then_inc(parts, 1)
                        dve.wait_ge(parts, k * 6 + (3 if e == 1 else 6))

                    part(1)
                    dve.wait_ge(paired, 3 * k + 3)
                    nc.vector.tensor_tensor(d[:, :, :], d[:, :, :], d_part[:, :, :], ALU.add).then_inc(d_steps, 1)
                    part(2)
                    nc.vector.tensor_tensor(d[:, :, :], d[:, :, :], d_part[:, :, :], ALU.subtract).then_inc(d_steps, 1)
                    dve.wait_ge(d_steps, k * 2 + 2)
                    for x in range(N - 1):
                        for j in range(N):
                            i = [n for n in range(N) if n != j][x]
                            out, src, by = c_sum[:, b, j, :], d[:, PAIR[i, j], :], st[:, i, j:j + 1]
                            if x == 0:
                                ins = nc.vector.tensor_scalar(out, src, by, st_sum[:, j:j + 1], ALU.mult, ALU.add)
                            else:
                                dve.wait_ge(mixing, k * MIX + (x - 1) * N + j + 1)
                                ins = nc.vector.scalar_tensor_tensor(out, src, by, out, ALU.mult, ALU.add)
                            ins.then_inc(c_made if x == N - 2 and j == N - 1 else mixing, 1)

                def total(q):
                    k, b = (t - 1) * Q + q, q % 2
                    dve.wait_ge(products, 2 * k + 2)
                    if q == 0:
                        dve.wait_ge(sup_turned, t)
                    u = unit[:, b, 0:2, :, :]
                    nc.vector.tensor_tensor(u[:, :, 0:2, :], u[:, :, 0:2, :], u[:, :, 2:4, :], ALU.add).then_inc(folded, 1)
                    dve.wait_ge(folded, k + 1)
                    nc.vector.tensor_tensor(sup[:, :, q * P:(q + 1) * P], u[:, :, 0, :], u[:, :, 1, :],
                                            ALU.add).then_inc(quarters, 1)

                if "s" in has:
                    nc.vector.tensor_copy(st[:, :, :], strength[:, bass.ds(t - 1, 1), :, :].rearrange("p t i j -> p (t i) j")
                                          ).then_inc(picked, 1)
                    dve.wait_ge(picked, 2 * t - 1)
                    nc.vector.tensor_reduce(st_sum[:, :], st[:, :, :].rearrange("p i j -> p j i"), AX_X,
                                            ALU.add).then_inc(picked, 1)
                    dve.wait_ge(picked, 2 * t)
                finish(0)
                if "s" in has:
                    invert(0)
                    invert(1)
                    mix(0)
                finish(1)
                if "s" in has:
                    mix(1)
                    total(0)
                    invert(2)
                finish(2)
                if "s" in has:
                    mix(2)
                    total(1)
                    invert(3)
                finish(3)
                if "s" in has:
                    mix(3)
                    total(2)
                    total(3)
                    dve.wait_ge(quarters, t * Q + 2)
                    flat = sup[:, :, :].rearrange("p e d -> p (e d)")
                    waste = d_part[:, 0:N, :].rearrange("p n d -> p (n d)")
                    for e in range(2):
                        nc.vector.tensor_tensor_reduce(out=waste, in0=sup[:, e, :], in1=sup[:, e, :], scale=1.0, scalar=0.0,
                                                       op0=ALU.mult, op1=ALU.add, accum_out=norm[:, e:e + 1]).then_inc(power, 1)
                        dve.wait_ge(power, 3 * t - 2 + e)
                    nc.vector.tensor_tensor(norm[:, 0:1], norm[:, 0:1], norm[:, 1:2], ALU.add).then_inc(power, 1)
                    dve.wait_ge(normed, t)
                    nc.vector.reciprocal(norm[:, 1:2], norm[:, 1:2]).then_inc(inv_norm, 1)
                    dve.wait_ge(inv_norm, t)
                    nc.vector.tensor_scalar(flat, flat, norm[:, 1:2], None, ALU.mult).then_inc(sup_ready, 1)

            stages(nc.vector.Fori, stage)



def towers(nc, sem, dram, w_tail, w_top2, w_top3, tail_cols, y):
    with ExitStack() as ctx:
        def sb(name, shape, dt=F32):
            return ctx.enter_context(nc.sbuf_tensor(name, shape, dt))

        HALVES, BH = 2, BATCH // 2
        UNITS = HALVES * CK
        PLACE = (0, 1, 2, 0, 1)
        w_raw = sb("tail_w_raw", [P, 2, CK, D])
        w_hi, w_lo = sb("tail_w_hi", [P, 3, CK, D], F32R), sb("tail_w_lo", [P, 3, CK, D], F32R)
        w3 = sb("w_top3", [P, 2])
        cols = sb("tail_columns", [P, 5, CK])
        rows = sb("rows", [P, 2 * CK, BH])
        x_hi = sb("tail_x_hi", [P, HALVES, 2 * CK, BH], F32R)
        x_lo = sb("tail_x_lo", [P, HALVES, 2 * CK, BH], F32R)
        amp_hi, amp_lo = sb("amp_hi", [P, HALVES, CK, BH], F32R), sb("amp_lo", [P, HALVES, CK, BH], F32R)
        real, imag = sb("real", [P, 2, BH]), sb("imag", [P, 2, BH])
        colsum = sb("tail_colsum", [P, HALVES, BH])
        mean_w, eps = sb("tail_mean_w", [P, P]), sb("tail_eps", [P, 1])
        y_sb = sb("y_row", [1, HALVES, BH])
        ps = ctx.enter_context(nc.psum_tensor("tail_ps", [P, 8, BH], F32))
        top_x = w_raw

        names = """wt_landed0 wt_landed1 wt_hi wt_lo tail_cols_landed tail_consts sup_landed xs_hi xs_lo
            m_made m_copied m_real m_squared m_power m_amp m_hi m_lo
            p_made p_out p_sum stat1 p_centred p_squared p_sum2 stat2 p_std p_rstd p_scaled p_gelu z_hi z_lo
            top_x_landed t1_made t1_sum t1_relu t1_hi t1_lo t2_made t2_relu t3_made y_copied y_sent"""
        s = {n: sem("tail_" + n) for n in names.split()}
        wt_landed = [s["wt_landed0"], s["wt_landed1"]]
        block = ctx.enter_context(nc.Block())

        def unit(i):
            return i // CK, i % CK

        post_out = rows[:, :, :].rearrange("p (h c) b -> p h c b", h=HALVES)
        z_hi, z_lo = x_hi[:, :, 0:CK, :], x_lo[:, :, 0:CK, :]
        t1_hi, t1_lo = x_hi[:, :, CK:2 * CK, :], x_lo[:, :, CK:2 * CK, :]
        t2 = rows[:, 0:2 * HALVES, :].rearrange("p (h c) b -> p h c b", h=HALVES)

        def width(m):
            return TOP2 if m == 4 else D

        @block.sync
        def _(sp):
            sp.dma_start(cols[:, :, :], tail_cols).then_inc(s["tail_cols_landed"], 16)
            sp.dma_start(w3[:, :], w_top3).then_inc(s["tail_cols_landed"], 16)
            for m in range(2):
                sp.dma_start(w_raw[:, m, :, :], w_tail[m].rearrange("c p o -> p c o")).then_inc(wt_landed[m], 16)
                if m == 0:
                    sp.dma_start(rows[:, :, :], dram["sup"][:, :, 0:BH].rearrange("c p b -> p c b")).then_inc(s["sup_landed"], 16)
            sp.wait_ge(s["xs_lo"], 1)
            sp.dma_start(rows[:, :, :], dram["sup"][:, :, BH:].rearrange("c p b -> p c b")).then_inc(s["sup_landed"], 16)
            for m in range(2, 5):
                sp.wait_ge(s["wt_lo"], m - 1)
                src = w_top2 if m == 4 else w_tail[m]
                sp.dma_start(w_raw[:, m % 2, :, 0:width(m)], src.rearrange("c p o -> p c o")).then_inc(wt_landed[m % 2], 16)
            sp.wait_ge(s["wt_lo"], 5)
            for h in range(HALVES):
                sp.dma_start(top_x[:, h, :, :], dram["top_x"][:, :, h * BH:(h + 1) * BH].rearrange("c p b -> p c b")
                             ).then_inc(s["top_x_landed"], 16)
            for h in range(HALVES):
                sp.wait_ge(s["y_copied"], h + 1)
                sp.dma_start(y[:, h * BH:(h + 1) * BH], y_sb[:, h, :]).then_inc(s["y_sent"], 16)
            sp.wait_ge(s["y_sent"], 16 * HALVES)

        @block.tensor
        def _(pe):
            def products(out, w_place, k_parts, moving, c, h, first=True, last=True):
                b_hi, b_lo = moving
                n = 0
                for k in range(CK):
                    for a, b in ((w_hi, b_hi), (w_hi, b_lo), (w_lo, b_hi)):
                        ins = nc.tensor.matmul(out, a[:, w_place, k, c * P:(c + 1) * P], b[:, h, k_parts + k, :],
                                               start=first and n == 0, stop=last and n == 3 * CK - 1)
                        n += 1
                return ins

            sup = (x_hi, x_lo)
            for i in range(UNITS):
                h, c = unit(i)
                pe.wait_ge(s["xs_lo"], h + 1)
                pe.wait_ge(s["wt_lo"], 2)
                b = 3 * (i % 2)
                if i >= 2:
                    pe.wait_ge(s["m_squared"], i - 1)
                products(ps[:, b, :], 0, 0, sup, c, h)
                products(ps[:, b + 1, :], 1, CK, sup, c, h)
                products(ps[:, b + 2, :], 1, 0, sup, c, h, last=False)
                products(ps[:, b + 2, :], 0, CK, sup, c, h, first=False).then_inc(s["m_made"], 1)
            for i in range(UNITS):
                h, c = unit(i)
                pe.wait_ge(s["m_lo"], h * CK + CK)
                pe.wait_ge(s["wt_lo"], 3)
                if i >= 2:
                    pe.wait_ge(s["p_out"], i - 1)
                products(ps[:, 6 + i % 2, :], 2, 0, (amp_hi, amp_lo), c, h).then_inc(s["p_made"], 1)
            pe.wait_ge(s["tail_consts"], 2)
            pe.wait_ge(s["m_squared"], UNITS)
            for name, bank, source in (("stat1", 0, "p_sum"), ("stat2", 2, "p_sum2")):
                for h in range(HALVES):
                    pe.wait_ge(s[source], (h + 1) * CK)
                    nc.tensor.matmul(ps[:, bank + h, :], mean_w[:, :], colsum[:, h, :], start=True, stop=True).then_inc(s[name], 1)
            for i in range(UNITS):
                h, c = unit(i)
                pe.wait_ge(s["z_lo"], h * CK + CK)
                pe.wait_ge(s["wt_lo"], 4)
                if i >= 2:
                    pe.wait_ge(s["t1_sum"], i - 1)
                products(ps[:, 4 + i % 2, :], 0, 0, (x_hi, x_lo), c, h).then_inc(s["t1_made"], 1)
            for i in range(2 * HALVES):
                h, c = i // 2, i % 2
                pe.wait_ge(s["t1_lo"], h * CK + CK)
                pe.wait_ge(s["wt_lo"], 5)
                pe.wait_ge(s["p_out"], UNITS)
                if i >= 2:
                    pe.wait_ge(s["t2_relu"], i - 1)
                products(ps[:, 6 + i % 2, :], 1, CK, (x_hi, x_lo), c, h).then_inc(s["t2_made"], 1)
            for h in range(HALVES):
                pe.wait_ge(s["t2_relu"], 2 * h + 2)
                pe.wait_ge(s["p_centred"], UNITS)
                for k in range(2):
                    ins = nc.tensor.matmul(ps[0:1, h, :], w3[:, k:k + 1], t2[:, h, k, :], start=(k == 0), stop=(k == 1))
                ins.then_inc(s["t3_made"], 1)

        def lagged(count, *steps):
            for i in range(count + len(steps) - 1):
                for lag, step in enumerate(steps):
                    if 0 <= i - lag < count:
                        step(i - lag)

        @block.scalar
        def _(act):
            def split_w(m):
                if m >= 3:
                    act.wait_ge(s["m_made"], UNITS)
                act.wait_ge(wt_landed[m % 2], 16 * (m // 2 + 1))
                w = width(m)
                nc.scalar.activation(w_hi[:, PLACE[m], :, 0:w], w_raw[:, m % 2, :, 0:w], ACT.Copy).then_inc(s["wt_hi"], 1)

            def split_x(h):
                act.wait_ge(s["sup_landed"], 16 * (h + 1))
                nc.scalar.activation(x_hi[:, h, :, :], rows[:, :, :], ACT.Copy).then_inc(s["xs_hi"], 1)

            split_w(0), split_x(0), split_w(1), split_x(1), split_w(2)

            def copy(i):
                act.wait_ge(s["m_made"], i + 1)
                if i >= 2:
                    act.wait_ge(s["m_lo"], i - 1)
                nc.scalar.activation(real[:, i % 2, :], ps[:, 3 * (i % 2), :], ACT.Copy).then_inc(s["m_copied"], 1)

            def square(i):
                nc.scalar.activation(imag[:, i % 2, :], ps[:, 3 * (i % 2) + 2, :], ACT.Square)
                act.wait_ge(s["m_real"], i + 1)
                nc.scalar.activation(real[:, i % 2, :], real[:, i % 2, :], ACT.Square).then_inc(s["m_squared"], 1)

            def root(i):
                act.wait_ge(s["m_power"], i + 1)
                nc.scalar.activation(real[:, i % 2, :], real[:, i % 2, :], ACT.Sqrt).then_inc(s["m_amp"], 1)
                act.wait_ge(s["m_amp"], i + 1)
                nc.scalar.activation(amp_hi[:, i // CK, i % CK, :], real[:, i % 2, :], ACT.Copy).then_inc(s["m_hi"], 1)

            for i in range(UNITS):
                copy(i), square(i), root(i)
            split_w(3), split_w(4)
            act.wait_ge(s["tail_cols_landed"], 32)

            def bias(i):
                h, c = unit(i)
                act.wait_ge(s["p_made"], i + 1)
                nc.scalar.activation(post_out[:, h, c, :], ps[:, 6 + i % 2, :], ACT.Identity,
                                     bias=cols[:, 0, c:c + 1]).then_inc(s["p_out"], 1)

            for i in range(UNITS):
                bias(i)
            for i in range(UNITS):
                act.wait_ge(s["p_centred"], i + 1)
                if i >= 2:
                    act.wait_ge(s["p_sum2"], i - 1)
                nc.scalar.activation(real[:, i % 2, :], post_out[:, i // CK, i % CK, :], ACT.Square).then_inc(s["p_squared"], 1)
            act.wait_ge(s["p_sum2"], UNITS)
            for h in range(HALVES):
                act.wait_ge(s["stat2"], h + 1)
                nc.scalar.activation(imag[:, h, :], ps[:, 2 + h, :], ACT.Sqrt, bias=eps[:, :]).then_inc(s["p_std"], 1)

            def gelu(i):
                h, c = unit(i)
                act.wait_ge(s["p_scaled"], i + 1)
                nc.scalar.activation(post_out[:, h, c, :], post_out[:, h, c, :], ACT.Gelu, bias=cols[:, 2, c:c + 1],
                                     scale=cols[:, 1, c:c + 1]).then_inc(s["p_gelu"], 1)

            def split_z(i):
                h, c = unit(i)
                act.wait_ge(s["p_gelu"], i + 1)
                nc.scalar.activation(z_hi[:, h, c, :], post_out[:, h, c, :], ACT.Copy).then_inc(s["z_hi"], 1)

            lagged(UNITS, gelu, split_z)

            def relu(i):
                h, c = unit(i)
                act.wait_ge(s["t1_sum"], i + 1)
                nc.scalar.activation(top_x[:, h, c, :], top_x[:, h, c, :], ACT.Relu, bias=cols[:, 3, c:c + 1]).then_inc(s["t1_relu"], 1)

            def split_t(i):
                h, c = unit(i)
                act.wait_ge(s["t1_relu"], i + 1)
                nc.scalar.activation(t1_hi[:, h, c, :], top_x[:, h, c, :], ACT.Copy).then_inc(s["t1_hi"], 1)

            lagged(UNITS, relu, split_t)
            act.wait_ge(s["p_made"], UNITS)
            for i in range(2 * HALVES):
                act.wait_ge(s["t2_made"], i + 1)
                nc.scalar.activation(t2[:, i // 2, i % 2, :], ps[:, 6 + i % 2, :], ACT.Relu,
                                     bias=cols[:, 4, i % 2:i % 2 + 1]).then_inc(s["t2_relu"], 1)
            for h in range(HALVES):
                act.wait_ge(s["t3_made"], h + 1)
                nc.scalar.activation(y_sb[:, h, :], ps[0:1, h, :], ACT.Copy).then_inc(s["y_copied"], 1)

        @block.vector
        def _(dve):
            nc.vector.memset(mean_w[:, :], 1.0 / OUT).then_inc(s["tail_consts"], 1)
            nc.vector.memset(eps[:, :], EPS).then_inc(s["tail_consts"], 1)

            def minus(out, a, b, done):
                nc.vector.tensor_tensor(out, a, b.bitcast(F32), ALU.subtract).then_inc(s[done], 1)

            def split_w(m):
                dve.wait_ge(s["wt_hi"], m + 1)
                w = width(m)
                minus(w_lo[:, PLACE[m], :, 0:w], w_raw[:, m % 2, :, 0:w], w_hi[:, PLACE[m], :, 0:w], "wt_lo")

            def split_x(h):
                dve.wait_ge(s["xs_hi"], h + 1)
                minus(x_lo[:, h, :, :], rows[:, :, :], x_hi[:, h, :, :], "xs_lo")

            split_w(0), split_x(0), split_w(1), split_x(1), split_w(2)
            for i in range(UNITS):
                b = 3 * (i % 2)
                dve.wait_ge(s["m_copied"], i + 1)
                nc.vector.tensor_tensor(real[:, i % 2, :], real[:, i % 2, :], ps[:, b + 1, :], ALU.subtract).then_inc(s["m_real"], 1)
                dve.wait_ge(s["m_squared"], i + 1)
                nc.vector.tensor_tensor(real[:, i % 2, :], real[:, i % 2, :], imag[:, i % 2, :], ALU.add).then_inc(s["m_power"], 1)
                dve.wait_ge(s["m_hi"], i + 1)
                minus(amp_lo[:, i // CK, i % CK, :], real[:, i % 2, :], amp_hi[:, i // CK, i % CK, :], "m_lo")
            split_w(3), split_w(4)

            def summed(i, src, name):
                h, c = unit(i)
                if c == 0:
                    ins = nc.vector.tensor_copy(colsum[:, h, :], src)
                else:
                    dve.wait_ge(s[name], i)
                    ins = nc.vector.tensor_tensor(colsum[:, h, :], colsum[:, h, :], src, ALU.add)
                ins.then_inc(s[name], 1)

            for i in range(UNITS):
                dve.wait_ge(s["p_out"], i + 1)
                summed(i, post_out[:, i // CK, i % CK, :], "p_sum")
            for h in range(HALVES):
                dve.wait_ge(s["stat1"], h + 1)
                for c in range(CK):
                    nc.vector.tensor_tensor(post_out[:, h, c, :], post_out[:, h, c, :], ps[:, h, :],
                                            ALU.subtract).then_inc(s["p_centred"], 1)
            for i in range(UNITS):
                dve.wait_ge(s["p_squared"], i + 1)
                summed(i, real[:, i % 2, :], "p_sum2")
            for h in range(HALVES):
                dve.wait_ge(s["p_std"], h + 1)
                nc.vector.reciprocal(imag[:, h, :], imag[:, h, :]).then_inc(s["p_rstd"], 1)
                dve.wait_ge(s["p_rstd"], h + 1)
                for c in range(CK):
                    nc.vector.tensor_tensor(post_out[:, h, c, :], post_out[:, h, c, :], imag[:, h, :],
                                            ALU.mult).then_inc(s["p_scaled"], 1)
            for i in range(UNITS):
                h, c = unit(i)
                dve.wait_ge(s["z_hi"], i + 1)
                minus(z_lo[:, h, c, :], post_out[:, h, c, :], z_hi[:, h, c, :], "z_lo")
            dve.wait_ge(s["top_x_landed"], 16 * HALVES)

            def add_x(i):
                h, c = unit(i)
                dve.wait_ge(s["t1_made"], i + 1)
                nc.vector.tensor_tensor(top_x[:, h, c, :], top_x[:, h, c, :], ps[:, 4 + i % 2, :], ALU.add).then_inc(s["t1_sum"], 1)

            def split_t(i):
                h, c = unit(i)
                dve.wait_ge(s["t1_hi"], i + 1)
                minus(t1_lo[:, h, c, :], top_x[:, h, c, :], t1_hi[:, h, c, :], "t1_lo")

            lagged(UNITS, add_x, split_t)


def tower(nc, a, y):
    with ExitStack() as ctx:
        def sem(name):
            return ctx.enter_context(nc.semaphore(name))

        def scratch(name, shape):
            return nc.dram_tensor(name, shape, F32, kind="Internal").ap()

        dram = {
            "s": scratch("encoded", [2 * N * CK, 2, P, BATCH]),
            "top_x": scratch("top_x", [CK, P, BATCH]),
            "attn": scratch("attended", [2, CK, 2, P, N, BATCH]),
            "sup": scratch("superposed", [2 * CK, P, BATCH]),
        }
        encoders(nc, sem, dram, a["w_stream"], a["x_t"], a["enc_cols"])
        attention(nc, sem, dram, a["w_proj"], a["bias_rows"], a["out_cols"], a["identity"])
        superpose(nc, sem, dram, a["w_int"], a["ids_t"], [a[f"tbl_{i}"] for i in range(N)], a["identity"])
        towers(nc, sem, dram, a["w_tail"], a["w_top2"], a["w_top3"], a["tail_cols"], y)


def lay_out(np, i):
    L = {k[len("L0_rec_"):]: np.asarray(v) for k, v in i.items() if k.startswith("L0_rec_")}
    top1, top2, top3 = (np.asarray(i[f"W_top{n}"]) for n in (1, 2, 3))

    def stream(w):
        return w.reshape(w.shape[0] // (2 * P), 2, P, w.shape[1] // 512, 512).transpose(3, 0, 2, 1, 4)

    def chunks(w):
        return w.reshape(w.shape[0] // P, P, w.shape[1])

    def columns(v):
        return v.reshape(-1, P).T

    w_stream = np.concatenate([stream(w) for w in (L["er_W1"].T, top1[OUT:], L["ei_W1"].T, L["er_W2"].T, L["ei_W2"].T)])
    b_top2 = np.concatenate([np.asarray(i["b_top2"]), np.zeros(D - TOP2, np.float32)])
    out = {
        "w_stream": w_stream.reshape(-1, P, 2, 512),
        "x_t": chunks(np.asarray(i["r_x"]).T),
        "enc_cols": np.stack([np.stack([columns(L[e + n]) for n in ("_b1", "_g1", "_be1", "_b2")], 1) for e in ("er", "ei")], 1),
        "w_proj": np.stack([chunks(L[f"W{n}_{e}"].T) for n in "qkvo" for e in "ri"]),
        "bias_rows": np.stack([L[f"b{n}_{e}"] for n in "qkv" for e in "ri"]),
        "out_cols": np.stack([columns(L[f"bo_{e}"]) for e in "ri"], 1),
        "identity": np.eye(P, dtype=np.float32),
        "w_int": np.stack([chunks(L[f"int_W{e}"][n].T) for n in range(N) for e in "ri"]),
        "ids_t": np.asarray(i["ids"]).reshape(TILES, P, N).transpose(1, 0, 2),
        "w_tail": np.stack([chunks(w) for w in (L["meas_Mr"].T, L["meas_Mi"].T, L["post_W"].T, top1[:OUT])]),
        "w_top2": chunks(top2),
        "w_top3": columns(top3.reshape(-1)),
        "tail_cols": np.stack([columns(v) for v in (L["post_b"], L["post_g"], L["post_be"], np.asarray(i["b_top1"]), b_top2)], 1),
    }
    out.update({f"tbl_{n}": np.asarray(i[f"tbl_{n}"]) for n in range(N)})
    return {k: np.ascontiguousarray(v) for k, v in out.items()}


def kernel(**inputs):
    import numpy as np
    import concourse.bacc as bacc
    from concourse.bass_utils import run_bass_kernel_spmd

    nc = bacc.Bacc("TRN2", target_bir_lowering=False, num_devices=1)
    arrays = {f"in_{k}": v for k, v in lay_out(np, inputs).items()}
    a = {k[3:]: nc.dram_tensor(k, v.shape, mybir.dt.from_np(v.dtype), kind="ExternalInput").ap() for k, v in arrays.items()}
    y = nc.dram_tensor("y_out", (1, BATCH), F32, kind="ExternalOutput").ap()
    tower(nc, a, y)
    r = run_bass_kernel_spmd(nc, [arrays], core_ids=[0])
    return r.results[0]["y_out"].reshape(BATCH, 1)
```

```python
from contextlib import ExitStack

import concourse.bass as bass
from concourse import mybir

F32 = mybir.dt.float32
F32R = mybir.dt.float32r
I32 = mybir.dt.int32
U32 = mybir.dt.uint32
ALU = mybir.AluOpType
ACT = mybir.ActivationFunctionType
AX_X = mybir.AxisListType.X

P = 128
BATCH, IN, HID, D, N, OUT, HEADS, TOP2 = 1024, 2048, 2048, 512, 4, 512, 8, 256
HD = D // HEADS
CK = D // P
TILES = BATCH // P
EPS = 1e-5



def encoders(nc, sem, dram, w_stream, x_stream, enc_cols, x_hi, x_lo):
    KT = IN // P
    SLOTS = KT // 2
    HALVES, BH = 2, BATCH // 2
    CH = 4
    G_S1R, G_TOP, G_S1I, G_S2R, G_S2I, GROUPS = 0, 4, 5, 9, 13, 17
    PAIRS = GROUPS * SLOTS
    G_X, X_PARTS = 14, 4

    with ExitStack() as ctx:
        def sb(name, shape, dt=F32):
            return ctx.enter_context(nc.sbuf_tensor(name, shape, dt))

        h_hi, h_lo = sb("h_hi", [P, KT, BH], F32R), sb("h_lo", [P, KT, BH], F32R)
        z = sb("z", [P, KT, BH])
        w_raw = sb("w_raw", [P, 2, 2, 512])
        w_hi, w_lo = sb("w_hi", [P, 2, 2, 512], F32R), sb("w_lo", [P, 2, 2, 512], F32R)
        staged = sb("staged", [P, 2, 2, BH])
        squares = sb("squares", [P, 2, BH])
        colsum, rstd = sb("colsum", [P, BH]), sb("rstd", [P, BH])
        cols = sb("enc_columns", [P, 2, 4, KT])
        mean_w, eps = sb("mean_w", [P, P]), sb("eps", [P, 1])
        zeros = sb("zeros", [P, BH])
        acc = ctx.enter_context(nc.psum_tensor("acc", [P, CH, 512], F32))
        stat = ctx.enter_context(nc.psum_tensor("stat", [P, 512], F32))

        raw_landed = [sem("raw_landed0"), sem("raw_landed1")]
        x_landed = [sem(f"x_landed{i}") for i in range(X_PARTS)]
        cols_landed, consts = sem("cols_landed"), sem("p1_consts")
        hi_ready, lo_ready = sem("w_hi_ready"), sem("w_lo_ready")
        pairs_used = sem("pairs_used")
        xhi_ready, xlo_ready = sem("xhi_ready"), sem("xlo_ready")
        acc_done, drained = sem("acc_done"), sem("drained")
        summed, stats_made = sem("summed"), sem("stats_made")
        centred, squared = sem("centred"), sem("squared")
        std_made, rstd_made = sem("std_made"), sem("rstd_made")
        scaled, gelued = sem("scaled"), sem("gelued")
        hhi_ready, hlo_ready = sem("hhi_ready"), sem("hlo_ready")
        shi_ready = sem("shi_ready")
        sent = [sem(f"sent{b}") for b in range(3)]
        block = ctx.enter_context(nc.Block())

        SUMS = 4 * (1 + KT)

        def pair(half, g, s):
            return half * PAIRS + g * SLOTS + s

        def unit(half, g, c):
            return half * (GROUPS * CH) + g * CH + c

        def place(g, c):
            top = isinstance(g, int) and g == G_TOP
            return c % 2 if top else c % 3

        def stage_in(g, c):
            b = place(g, c)
            return squares[:, :, :] if b == 2 else staged[:, b, :, :]

        TOP_SENDS, OUT_SENDS = (2, 2, 0), (2, 1, 1)
        HALF_SENDS = [top + 2 * CH * each for top, each in zip(TOP_SENDS, OUT_SENDS)]

        def sends(half, g, c):
            b = place(g, c)
            if isinstance(g, int) and g == G_TOP:
                return half * HALF_SENDS[b] + c // 2
            return half * HALF_SENDS[b] + TOP_SENDS[b] + (g - G_S2R) * OUT_SENDS[b] + c // 3

        def schedule(run):
            for first, last in ((0, 0), (1, 3), (4, 4), (5, 5), (6, 6), (7, 8), (9, 9), (10, 11),
                                (12, 12), (13, 13), (14, 14), (15, 16)):
                run(first, last)

        def kind(g):
            return "top" if g == G_TOP else ("s1" if g < G_S2R else "s2")

        def norm1(g, s):
            if g not in (G_TOP, G_S2R) or s < 2:
                return 0, ()
            cut = (0, 3, 6, 9, 12, 14, 16)
            return int(g == G_S2R), range(cut[s - 2], cut[s - 1])

        def norm2(g, s):
            e = int(g in (G_S2R + 3, G_S2I))
            if g in (G_S1I, G_S2R + 3) and s >= 2:
                return e, range(2 * s - 4, 2 * s - 2)
            if g in (G_S1I + 1, G_S2I) and s < 2:
                return e, range(12 + 2 * s, 14 + 2 * s)
            return e, ()

        @block.sync
        def _(sp):
            for b in range(3):
                sp.sem_inc(sent[b], 16)
            def load_x(n, i):
                sp.dma_start(z[:, 4 * i:4 * i + 4, :], x_stream[bass.ds(n, 1), :, :, :].rearrange("n p k b -> p (n k) b")
                             ).then_inc(x_landed[i], 16)

            for i in range(X_PARTS):
                load_x(i, i)
            for u in range(2):
                sp.dma_start(w_raw[:, u, :, :], w_stream[u, :, :, :]).then_inc(raw_landed[u], 16)
            sp.dma_start(cols[:, :, :, :], enc_cols).then_inc(cols_landed, 16)

            def out(half, g):
                for c in range(CH):
                    sp.wait_ge(drained, unit(half, g, c) + 5)
                    src, done = stage_in(g, c), sent[place(g, c)]
                    if isinstance(g, int) and g == G_TOP:
                        sp.dma_start(dram["top_x"][c, :, bass.ts(half, BH)], src[:, 0, :]).then_inc(done, 16)
                    else:
                        dst = dram["s"][(g - G_S2R) * CH + c][:, :, bass.ts(half, BH)]
                        sp.dma_start(dst.rearrange("a p b -> p a b"), src).then_inc(done, 16)

            def group(half, g, before):
                for s in range(SLOTS):
                    sp.wait_ge(lo_ready, pair(half, g, s) + 3)
                    sp.dma_start(w_raw[:, s % 2, :, :], w_stream[g * SLOTS + s + 2, :, :, :]).then_inc(raw_landed[s % 2], 16)
                    if s == 0 and before in ("top", "s2"):
                        out(half, g - 1)
                    if isinstance(g, int) and g == G_X and s < X_PARTS:
                        sp.wait_ge(hlo_ready, half * 32 + 32)
                        load_x((half + 1) * X_PARTS + s, s)

            with nc.sync.Fori(0, HALVES) as half:
                def run(first, last):
                    before = kind(first - 1) if first else None
                    if first == last:
                        group(half, first, before)
                    else:
                        with nc.sync.Fori(first, last + 1) as g:
                            group(half, g, before)
                schedule(run)
                out(half, GROUPS - 1)
            for b in range(3):
                sp.wait_ge(sent[b], 16 * (HALF_SENDS[b] * HALVES + 1))
            for u in range(2):
                sp.wait_ge(raw_landed[u], 16 * (HALVES * PAIRS // 2 + 1))

        @block.scalar
        def _(act):
            def split_x(half, i):
                act.wait_ge(x_landed[i], 16 * (half + 1))
                nc.scalar.activation(x_hi[:, 4 * i:4 * i + 4, :], z[:, 4 * i:4 * i + 4, :], ACT.Copy).then_inc(xhi_ready, 1)

            for i in range(X_PARTS):
                split_x(0, i)
            act.wait_ge(cols_landed, 16)
            act.wait_ge(consts, 3)

            def drain(half, g, what):
                for c in range(CH):
                    if c < CH - 1:
                        act.wait_ge(acc_done, (half * GROUPS + g) * (CH - 1) + c + 1)
                    else:
                        act.wait_ge(pairs_used, pair(half, g, SLOTS - 1) + 3)
                    if what == "top":
                        act.wait_ge(sent[place(g, c)], 16 * (sends(half, g, c) + 1))
                        nc.scalar.activation(stage_in(g, c)[:, 0, :], acc[:, c, :], ACT.Copy).then_inc(drained, 1)
                    elif what == "s2r" or what == "s2i":
                        e = int(what == "s2i")
                        col = (g - (G_S2I if e else G_S2R)) * CH + c
                        act.wait_ge(sent[place(g, c)], 16 * (sends(half, g, c) + 1))
                        if c == 2:
                            act.wait_ge(summed, half * SUMS + SUMS)
                        nc.scalar.activation(stage_in(g, c)[:, 0, :].bitcast(F32R), acc[:, c, :], ACT.Identity,
                                             bias=cols[:, e, 3, bass.ds(col, 1)]).then_inc(shi_ready, 1)
                    else:
                        e = int(what == "s1i")
                        col = (g - (G_S1I if e else G_S1R)) * CH + c
                        if e:
                            act.wait_ge(hlo_ready, half * 32 + col + 1)
                        nc.scalar.activation(z[:, bass.ds(col, 1), :], acc[:, c:c + 1, :], ACT.Identity,
                                             bias=cols[:, e, 0, bass.ds(col, 1)]).then_inc(drained, 1)

            def group(half, g, before):
                for s in range(SLOTS):
                    u = s % 2
                    act.wait_ge(raw_landed[u], 16 * (half * (PAIRS // 2) + g * (SLOTS // 2) + s // 2 + 1))
                    act.wait_ge(pairs_used, pair(half, g, s) + 1)
                    nc.scalar.activation(w_hi[:, u, :, :], w_raw[:, u, :, :], ACT.Copy).then_inc(hi_ready, 1)
                    if s == 0 and before:
                        drain(half, g - 1, before)
                    if isinstance(g, int) and g == G_X and 2 <= s < 2 + X_PARTS:
                        split_x(half + 1, s - 2)
                    if not isinstance(g, int):
                        continue
                    e, chunks = norm1(g, s)
                    if chunks and s == 2:
                        act.wait_ge(sent[2], 16 * (half * HALF_SENDS[2] + 1))
                    for i in chunks:
                        act.wait_ge(centred, half * 32 + e * KT + i + 1)
                        if i >= 2:
                            act.wait_ge(summed, half * SUMS + (2 * e + 1) * (1 + KT) + i)
                        nc.scalar.activation(squares[:, i % 2, :], z[:, i, :], ACT.Square).then_inc(squared, 1)
                    if g in (G_S1I, G_S2R + 3) and s == 1:
                        e = int(g != G_S1I)
                        act.wait_ge(stats_made, half * 4 + 2 * e + 3)
                        nc.scalar.activation(rstd[:, :], stat[:, :], ACT.Sqrt, bias=eps[:, :]).then_inc(std_made, 1)
                    e, chunks = norm2(g, s)
                    for i in chunks:
                        act.wait_ge(scaled, half * 32 + e * KT + i + 1)
                        nc.scalar.activation(z[:, i, :], z[:, i, :], ACT.Gelu, bias=cols[:, e, 2, i:i + 1],
                                             scale=cols[:, e, 1, i:i + 1]).then_inc(gelued, 1)
                    for i in chunks:
                        act.wait_ge(gelued, half * 32 + e * KT + i + 1)
                        nc.scalar.activation(h_hi[:, i, :], z[:, i, :], ACT.Copy).then_inc(hhi_ready, 1)

            def what(g):
                return {0: "s1r", 4: "top", 5: "s1i", 9: "s2r", 13: "s2i"}[max(b for b in (0, 4, 5, 9, 13) if b <= g)]

            with nc.scalar.Fori(0, HALVES) as half:
                def run(first, last):
                    before = what(first - 1) if first else None
                    if first == last:
                        group(half, first, before)
                    else:
                        with nc.scalar.Fori(first, last + 1) as g:
                            group(half, g, before)
                schedule(run)
                drain(half, GROUPS - 1, "s2i")

        @block.vector
        def _(dve):
            dve.sem_inc(lo_ready, 2)
            dve.sem_inc(drained, CH)
            nc.vector.memset(mean_w[:, :], 1.0 / HID).then_inc(consts, 1)
            nc.vector.memset(eps[:, :], EPS).then_inc(consts, 1)
            nc.vector.memset(zeros[:, :], 0.0).then_inc(consts, 1)

            def split_x(half, i):
                dve.wait_ge(xhi_ready, half * X_PARTS + i + 1)
                nc.vector.tensor_tensor(x_lo[:, 4 * i:4 * i + 4, :], z[:, 4 * i:4 * i + 4, :],
                                        x_hi[:, 4 * i:4 * i + 4, :].bitcast(F32), ALU.subtract).then_inc(xlo_ready, 1)

            for i in range(X_PARTS):
                split_x(0, i)
            dve.wait_ge(cols_landed, 16)

            def group(half, g, before):
                for s in range(SLOTS):
                    u = s % 2
                    dve.wait_ge(hi_ready, pair(half, g, s) + 1)
                    nc.vector.tensor_tensor(w_lo[:, u, :, :], w_raw[:, u, :, :], w_hi[:, u, :, :].bitcast(F32),
                                            ALU.subtract).then_inc(lo_ready, 1)
                    if s == 0 and before:
                        drain(half, g - 1, before)
                    if isinstance(g, int) and g == G_X and 2 <= s < 2 + X_PARTS:
                        split_x(half + 1, s - 2)
                    if not isinstance(g, int):
                        continue
                    e, chunks = norm1(g, s)
                    if chunks and s == 2:
                        dve.wait_ge(stats_made, half * 4 + 2 * e + 2)
                    for i in chunks:
                        nc.vector.tensor_tensor(z[:, i, :], z[:, i, :], stat[:, :], ALU.subtract).then_inc(centred, 1)
                    if g in (G_S1I, G_S2R + 3) and s == 1:
                        e = int(g != G_S1I)
                        dve.wait_ge(std_made, half * 2 + e + 1)
                        nc.vector.reciprocal(rstd[:, :], rstd[:, :]).then_inc(rstd_made, 1)
                    e, chunks = norm2(g, s)
                    for i in chunks:
                        dve.wait_ge(hhi_ready, half * 32 + e * KT + i + 1)
                        nc.vector.tensor_tensor(h_lo[:, i, :], z[:, i, :], h_hi[:, i, :].bitcast(F32),
                                                ALU.subtract).then_inc(hlo_ready, 1)

            def drain(half, g, what):
                if what != "s2r" and what != "s2i":
                    return
                e = int(what == "s2i")
                for c in range(CH):
                    col = (g - (G_S2I if e else G_S2R)) * CH + c
                    dve.wait_ge(shi_ready, half * 32 + (g - G_S2R) * CH + c + 1)
                    nc.vector.scalar_tensor_tensor(
                        stage_in(g, c)[:, 1, :].bitcast(F32R), acc[:, c, :], cols[:, e, 3, bass.ds(col, 1)],
                        stage_in(g, c)[:, 0, :], ALU.add, ALU.subtract).then_inc(drained, 1)

            def what(g):
                return {0: "s1", 9: "s2r", 13: "s2i"}[max(b for b in (0, 9, 13) if b <= g)]

            with nc.vector.Fori(0, HALVES) as half:
                def run(first, last):
                    before = what(first - 1) if first else None
                    if first == last:
                        group(half, first, before)
                    else:
                        with nc.vector.Fori(first, last + 1) as g:
                            group(half, g, before)
                schedule(run)
                drain(half, GROUPS - 1, "s2i")

        @block.gpsimd
        def _(pool):
            def clear(half, n):
                pool.wait_ge(stats_made, half * 4 + n + 1)
                nc.gpsimd.tensor_tensor(colsum[:, :], zeros[:, :], zeros[:, :], ALU.add).then_inc(summed, 1)

            def add(half, n, i, src):
                pool.wait_ge(summed, half * SUMS + n * (1 + KT) + i + 1)
                nc.gpsimd.tensor_tensor(colsum[:, :], colsum[:, :], src, ALU.add).then_inc(summed, 1)

            pool.wait_ge(consts, 3)
            with nc.gpsimd.Fori(0, HALVES) as half:
                for e, g0 in ((0, G_S1R), (1, G_S1I)):
                    clear(half, 2 * e)
                    with nc.gpsimd.Fori(0, 4) as q:
                        for c in range(CH):
                            pool.wait_ge(drained, half * (GROUPS * CH) + g0 * CH + q * CH + c + 5)
                            add(half, 2 * e, q * CH + c, z[:, bass.ds(q * CH + c, 1), :])
                    clear(half, 2 * e + 1)
                    with nc.gpsimd.Fori(0, KT // 2) as q:
                        for u in range(2):
                            pool.wait_ge(squared, half * 32 + e * KT + q * 2 + u + 1)
                            add(half, 2 * e + 1, q * 2 + u, squares[:, u, :])
                    with nc.gpsimd.Fori(0, KT) as i:
                        pool.wait_ge(rstd_made, half * 2 + e + 1)
                        nc.gpsimd.tensor_tensor(z[:, bass.ds(i, 1), :], z[:, bass.ds(i, 1), :],
                                                rstd[:, :].unsqueeze(1), ALU.mult).then_inc(scaled, 1)

        @block.tensor
        def _(pe):
            pe.sem_inc(pairs_used, 2)
            pe.sem_inc(stats_made, 1)
            pe.wait_ge(consts, 3)

            def statistic(half, n):
                pe.wait_ge(summed, half * SUMS + (n + 1) * (1 + KT))
                nc.tensor.matmul(stat[:, :], mean_w[:, :], colsum[:, :], start=True, stop=True).then_inc(stats_made, 1)

            sums_at = {(G_TOP, 1): 0, (G_S1I, 0): 1, (G_S2R, 1): 2, (G_S2R + 3, 0): 3}

            def group(half, g, moving):
                a_hi, a_lo = moving
                for s in range(SLOTS):
                    pe.wait_ge(lo_ready, pair(half, g, s) + 3)
                    if isinstance(g, int) and g == G_S1R:
                        pe.wait_ge(xlo_ready, half * X_PARTS + s // 2 + 1)
                    if isinstance(g, int) and g == G_S2R and s == 0:
                        pe.wait_ge(hlo_ready, half * 32 + KT)
                    if isinstance(g, int) and g == G_S2I:
                        pe.wait_ge(hlo_ready, half * 32 + KT + 2 * s + 2)
                    for c in range(CH):
                        if s == 0:
                            pe.wait_ge(drained, unit(half, g, c) + 1)
                        for kk in range(2):
                            k = 2 * s + kk
                            for n, (a, b) in enumerate(((w_hi, a_hi), (w_hi, a_lo), (w_lo, a_hi))):
                                last = nc.tensor.matmul(acc[:, c, :], a[:, s % 2, kk, c * P:(c + 1) * P], b[:, k, :],
                                                        start=(k == 0 and n == 0), stop=(k == KT - 1 and n == 2))
                        if s == SLOTS - 1 and c < CH - 1:
                            last.then_inc(acc_done, 1)
                    last.then_inc(pairs_used, 1)
                    if isinstance(g, int) and (g, s) in sums_at:
                        statistic(half, sums_at[g, s])

            with nc.tensor.Fori(0, HALVES) as half:
                def run(first, last):
                    moving = (x_hi, x_lo) if first < G_S2R else (h_hi, h_lo)
                    if first == last:
                        group(half, first, moving)
                    else:
                        with nc.tensor.Fori(first, last + 1) as g:
                            group(half, g, moving)
                schedule(run)



def attention(nc, sem, dram, w_proj, bias_rows, out_cols, identity, w_hi, w_lo):
    with ExitStack() as ctx:
        w_soft = ctx.enter_context(nc.sbuf_tensor("w_soft", [P, TILES, N * N * HEADS], F32))
        scores(nc, sem, dram, w_proj, bias_rows, w_hi, w_lo, w_soft)
        attend(nc, sem, dram, bias_rows, out_cols, identity, w_hi, w_lo, w_soft)


def scores(nc, sem, dram, w_proj, bias_rows, w_hi, w_lo, w_soft):
    with ExitStack() as ctx:
        def sb(name, shape, dt=F32):
            return ctx.enter_context(nc.sbuf_tensor(name, shape, dt))

        MATS = 4
        UNITS = 2 * N * 2
        RING = 4
        bias = sb("qk_bias", [P, MATS, D])
        s_in = sb("qk_s", [P, RING, CK, 2, P], F32R)
        qk = sb("qk", [P, 2, 2, 2, N, D])
        mixed = sb("qk_mixed", [P, 2, N, D])
        prod = sb("qk_prod", [P, 3, N, D])
        dots = [w_soft] + [sb(f"qk_dots{i}", [P, TILES, N * N * HEADS]) for i in (1, 2)]
        tiny = sb("qk_tiny", [P, 1])
        ps = ctx.enter_context(nc.psum_tensor("qk_ps", [P, 8, D], F32))
        w_landed, bias_landed = [sem(f"qk_w_landed{i}") for i in range(MATS)], sem("qk_bias_landed")
        w_hi_made = sem("qk_w_hi_made")
        s_landed = [sem(f"qk_s_landed{i}") for i in range(RING)]
        s_used = sem("qk_s_used")
        made, evicted = sem("qk_made"), sem("qk_evicted")
        mixes, own_mix = sem("qk_mixes"), sem("qk_own_mix")
        pooled, reduced = sem("qk_pooled"), sem("qk_reduced")
        own_product, own_reduced = sem("qk_own_product"), sem("qk_own_reduced")
        soft, acted = sem("qk_soft"), sem("qk_acted")
        block = ctx.enter_context(nc.Block())

        def stages(fori, run):
            run(0, 0)
            run(1, 1)
            with fori(1, TILES // 2) as q:
                run(2 * q, 0)
                run(2 * q + 1, 1)
            run(TILES, 0)

        def mat(j, e):
            return 2 * j + e

        def raw(m):
            return qk[:, 0, m // 2, m % 2, :, :]

        @block.sync
        def _(sp):
            with nc.sync.Fori(0, TILES) as t:
                for n in range(N):
                    for e in range(2):
                        i = 2 * n + e
                        sp.wait_ge(s_used, t * 2 * N + i + 1)
                        src = dram["s"][(e * N + n) * CK:(e * N + n + 1) * CK, :, :, bass.ts(t, P)]
                        for c in range(CK):
                            sp.dma_start(s_in[:, i % RING, c, :, :].bitcast(F32),
                                         src[c].rearrange("a p b -> p a b")).then_inc(s_landed[i % RING], 16)
            sp.wait_ge(pooled, (TILES - 1) * 2 * N)
            for m in range(MATS):
                sp.dma_start(raw(m), w_proj[m, :, :, :].rearrange("c p o -> p c o")).then_inc(w_landed[m], 16)

        @block.scalar
        def _(act):
            act.wait_ge(s_landed[0], 16 * CK)
            act.dma_start(bias[:, :, :], bias_rows[0:MATS, :].unsqueeze(0).broadcast_to([P, MATS, D])).then_inc(bias_landed, 16)
            act.wait_ge(s_used, RING + TILES * 2 * N)
            for m in range(MATS):
                act.wait_ge(w_landed[m], 16)
                nc.scalar.activation(w_hi[:, m, :, :], raw(m), ACT.Copy).then_inc(w_hi_made, 1)
            act.wait_ge(soft, 7)
            nc.scalar.activation(w_soft[:, :, :], w_soft[:, :, :], ACT.Sqrt, bias=tiny[:, :],
                                 scale=1.0 / HD).then_inc(acted, 1)
            act.wait_ge(soft, 9)
            nc.scalar.activation(w_soft[:, :, :], w_soft[:, :, :], ACT.Exp).then_inc(acted, 1)

        @block.tensor
        def _(pe):
            pe.sem_inc(s_used, RING)
            with nc.tensor.Fori(0, TILES) as t:
                for n in range(N):
                    for e in range(2):
                        i = 2 * n + e
                        pe.wait_ge(s_landed[i % RING], 16 * CK * (t * 2 + i // RING + 1))
                        for j in range(2):
                            u = 2 * i + j
                            pe.wait_ge(evicted, t * UNITS + u + 1)
                            k = 0
                            for c in range(CK):
                                for a, b in ((0, w_hi), (1, w_hi), (0, w_lo)):
                                    last = nc.tensor.matmul(ps[:, u % 8, :], s_in[:, i % RING, c, a, :],
                                                            b[:, mat(j, e), c, :], start=(k == 0), stop=(k == 3 * CK - 1))
                                    k += 1
                            last.then_inc(s_used if j else made, 1)

        @block.vector
        def _(dve):
            dve.sem_inc(evicted, 8)
            dve.sem_inc(reduced, 2)
            dve.sem_inc(own_reduced, 1)
            nc.vector.memset(tiny[:, :], 1e-8 / HD)
            dve.wait_ge(bias_landed, 16)

            def evict(t, par, u):
                i, j = u // 2, u % 2
                n, e = i // 2, i % 2
                dve.wait_ge(s_used if j else made, t * 2 * N + i + 1 + (RING if j else 0))
                if u == 0 and not (isinstance(t, int) and t < 2):
                    dve.wait_ge(pooled, (t - 1) * 2 * N)
                nc.vector.tensor_tensor(qk[:, par, j, e, n, :], ps[:, u % 8, :], bias[:, mat(j, e), :],
                                        ALU.add).then_inc(evicted, 1)

            def dot(t, par, n, what):
                if what == 1:
                    if n == 0:
                        dve.wait_ge(own_mix, t + 1)
                        dve.wait_ge(mixes, t + 1)
                    dve.wait_ge(own_reduced, t * N + n + 1)
                    nc.vector.tensor_tensor(prod[:, 2, :, :], mixed[:, 0, n:n + 1, :].broadcast_to([P, N, D]),
                                            mixed[:, 1, :, :], ALU.mult).then_inc(own_product, 1)
                    return
                kind = {0: 0, 3: 1, 2: 2}[what]
                if what == 0 and n == 0:
                    dve.wait_ge(evicted, t * UNITS + UNITS + 8)
                    if not (isinstance(t, int) and t == 0):
                        dve.wait_ge(own_product, t * N)
                    nc.vector.tensor_tensor(mixed[:, 0, :, :], qk[:, par, 0, 0, :, :], qk[:, par, 0, 1, :, :],
                                            ALU.add).then_inc(own_mix, 1)
                if kind < 2:
                    dve.wait_ge(pooled, t * 2 * N + n * 2 + kind + 1)
                else:
                    dve.wait_ge(own_product, t * N + n + 1)
                W = N * HEADS
                nc.vector.tensor_reduce(
                    dots[kind][:, bass.ds(t, 1), n * W:(n + 1) * W].rearrange("p t w -> p (t w)"),
                    prod[:, kind, :, :].rearrange("p m (h d) -> p (m h) d", d=HD), AX_X,
                    ALU.add).then_inc(own_reduced if kind == 2 else reduced, 1)

            def stage(t, par):
                for u in range(UNITS):
                    if not (isinstance(t, int) and t == TILES):
                        evict(t, par, u)
                    if not (isinstance(t, int) and t == 0):
                        dot(t - 1, 1 - par, u // 4, u % 4)

            stages(nc.vector.Fori, stage)

            steps = [0]

            def link(ins):
                steps[0] += 1
                ins.then_inc(soft, 1)
                dve.wait_ge(soft, steps[0])

            a, b, c = (kind[:, :, :] for kind in dots)
            most = mixed[:, 0, 0, 0:TILES * N * HEADS]
            dve.wait_ge(own_reduced, TILES * N + 1)
            dve.wait_ge(reduced, TILES * 2 * N + 2)
            link(nc.vector.tensor_tensor(c, c, a, ALU.subtract))
            link(nc.vector.tensor_tensor(c, c, b, ALU.add))
            link(nc.vector.tensor_tensor(a, a, b, ALU.add))
            link(nc.vector.tensor_tensor(c, c, c, ALU.mult))
            link(nc.vector.tensor_tensor(a, a, a, ALU.mult))
            link(nc.vector.tensor_tensor(a, a, c, ALU.add))
            nc.vector.tensor_copy(tiny[:, :], tiny[:, :]).then_inc(soft, 1)
            steps[0] += 1
            dve.wait_ge(acted, 1)
            flat = a.rearrange("p t (n m h) -> p (t n) m h", m=N, h=HEADS)
            by_m = flat.rearrange("p x m h -> p x h m")
            m3 = most.rearrange("p (x h) -> p x h", h=HEADS)
            link(nc.vector.tensor_reduce(m3, by_m, AX_X, ALU.max))
            spread = m3.unsqueeze(2).broadcast_to([P, TILES * N, N, HEADS])
            nc.vector.tensor_tensor(flat, flat, spread, ALU.subtract).then_inc(soft, 1)
            steps[0] += 1
            dve.wait_ge(acted, 2)
            link(nc.vector.tensor_reduce(m3, by_m, AX_X, ALU.add))
            link(nc.vector.reciprocal(most, most))
            link(nc.vector.tensor_tensor(flat, flat, spread, ALU.mult))

        @block.gpsimd
        def _(pool):
            def work(t, par):
                def product(n, e):
                    pool.wait_ge(reduced, t * 2 * N + n * 2 + e + 1)
                    nc.gpsimd.tensor_tensor(prod[:, e, :, :],
                                            qk[:, par, 0, e, n:n + 1, :].broadcast_to([P, N, D]),
                                            qk[:, par, 1, e, :, :], ALU.mult).then_inc(pooled, 1)

                pool.wait_ge(evicted, t * UNITS + UNITS - 2 + 8)
                product(0, 0)
                pool.wait_ge(evicted, t * UNITS + UNITS + 8)
                if not (isinstance(t, int) and t == 0):
                    pool.wait_ge(own_product, t * N)
                nc.gpsimd.tensor_tensor(mixed[:, 1, :, :], qk[:, par, 1, 0, :, :], qk[:, par, 1, 1, :, :],
                                        ALU.subtract).then_inc(mixes, 1)
                product(0, 1)
                for n in range(1, N):
                    product(n, 0)
                    product(n, 1)

            work(0, 0)
            with nc.gpsimd.Fori(0, TILES // 2 - 1) as q:
                work(2 * q + 1, 1)
                work(2 * q + 2, 0)
            work(TILES - 1, 1)
            for m in range(MATS):
                pool.wait_ge(w_hi_made, m + 1)
                nc.gpsimd.tensor_tensor(w_lo[:, m, :, :], raw(m), w_hi[:, m, :, :].bitcast(F32), ALU.subtract)

def attend(nc, sem, dram, bias_rows, out_cols, identity, w_hi, w_lo, w_soft):
    with ExitStack() as ctx:
        def sb(name, shape, dt=F32):
            return ctx.enter_context(nc.sbuf_tensor(name, shape, dt))

        UNITS = 2 * N
        RING = 4
        bias = sb("v_bias", [P, 2, D])
        o_bias = sb("o_bias", [P, 2, CK])
        ident = sb("ident", [P, P])
        s_in = sb("v_s", [P, RING, CK, 2, P], F32R)
        v = sb("v", [P, 2, 2, N, D])
        w_tile = sb("w_tile", [P, 2, N * N * HEADS])
        prod = sb("v_prod", [P, 2, N, D])
        mixed = sb("v_mixed", [P, 2, D])
        m_hi = sb("m_hi", [P, 2, CK, N, P], F32R)
        m_lo = sb("m_lo", [P, 2, CK, N, P], F32R)
        staged = sb("attn_staged", [P, 2, 2, N, P])
        ps_v = ctx.enter_context(nc.psum_tensor("ps_v", [P, 4, D], F32))
        ps_t = ctx.enter_context(nc.psum_tensor("ps_t", [P, 2, CK, P], F32))
        ps_o = ctx.enter_context(nc.psum_tensor("ps_o", [P, 2, N, P], F32))
        consts_landed = sem("v_consts_landed")
        s_landed = [sem(f"v_s_landed{i}") for i in range(RING)]
        v_made, evicted = sem("v_made"), sem("v_evicted")
        pooled, halved, mixes = sem("v_pooled"), sem("v_halved"), sem("v_mixes")
        turned, t_hi, t_lo = sem("turned"), sem("t_hi"), sem("t_lo")
        w_picked = sem("w_picked")
        o_made, o_hi, o_lo = sem("o_made"), sem("o_hi"), sem("o_lo")
        sent = [sem("attn_sent0"), sem("attn_sent1")]
        block = ctx.enter_context(nc.Block())

        MIX, TURN, OUT, OUT_LO = UNITS, UNITS + 1, UNITS + N + 1, UNITS + N + 2

        def stages(fori, run):
            run(0, 0)
            run(1, 1)
            with fori(1, TILES // 2) as q:
                run(2 * q, 0)
                run(2 * q + 1, 1)
            run(TILES, 0)
            run(TILES + 1, 1)

        def live(t, u, lag):
            return not isinstance(t, int) or 0 <= t * UNITS + u - lag < TILES * UNITS

        def piece_of(t, u, lag):
            v = u + 2 * UNITS - lag
            w = v % UNITS
            return (t - 2) * UNITS + v, (t - 2) * N + v // 2, t - 2 + v // UNITS, w // N, w % N

        @block.sync
        def _(sp):
            for u in range(2):
                sp.sem_inc(sent[u], 16)
            sp.dma_start(bias[:, :, :], bias_rows[4:6, :].unsqueeze(0).broadcast_to([P, 2, D])).then_inc(consts_landed, 16)
            sp.dma_start(o_bias[:, :, :], out_cols).then_inc(consts_landed, 16)
            sp.dma_start(ident[:, :], identity).then_inc(consts_landed, 16)

            with nc.sync.Fori(0, TILES) as t:
                for u in range(UNITS):
                    sp.wait_ge(v_made, t * UNITS + u + 1)
                    for c in range(CK):
                        src = dram["s"][u * CK + c][:, :, bass.ts(t, P)]
                        sp.dma_start(s_in[:, u % RING, c, :, :].bitcast(F32),
                                     src.rearrange("a p b -> p a b")).then_inc(s_landed[u % RING], 16)

        @block.scalar
        def _(act):
            act.wait_ge(consts_landed, 48)

            def stage(t, par):
                for u in range(UNITS):
                    if live(t, u, OUT_LO):
                        piece, before, tile, e, c = piece_of(t, u, OUT_LO)
                        act.wait_ge(o_lo, piece + 3)
                        for a in range(2):
                            act.dma_start(dram["attn"][e, c, a][:, :, bass.ts(tile, P)],
                                          staged[:, c % 2, a, :, :]).then_inc(sent[c % 2], 16)
                    if live(t, u, TURN):
                        x, w = (t - 1) * UNITS + u - 1, (u - 1) % UNITS
                        act.wait_ge(turned, x + 3)
                        nc.scalar.activation(m_hi[:, w // N, :, w % N, :], ps_t[:, w % 2, :, :],
                                             ACT.Copy).then_inc(t_hi, 1)
                    if live(t, u, OUT):
                        piece, before, tile, e, c = piece_of(t, u, OUT)
                        act.wait_ge(o_made, piece + 1)
                        act.wait_ge(sent[c % 2], before * 32 + 16)
                        nc.scalar.activation(staged[:, c % 2, 0, :, :].bitcast(F32R), ps_o[:, c % 2, :, :], ACT.Identity,
                                             bias=o_bias[:, e, c:c + 1]).then_inc(o_hi, 1)

            stages(nc.scalar.Fori, stage)
            for u in range(2):
                act.wait_ge(sent[u], 16 + 32 * 4 * TILES)

        @block.tensor
        def _(pe):
            pe.sem_inc(v_made, RING)
            pe.sem_inc(turned, 2)
            pe.wait_ge(consts_landed, 48)

            def stage(t, par):
                for u in range(UNITS):
                    e, n = u // N, u % N
                    if live(t, u, 0):
                        pe.wait_ge(s_landed[u % RING], 16 * CK * (t * 2 + u // RING + 1))
                        pe.wait_ge(evicted, t * UNITS + u + 1)
                        k = 0
                        for c in range(CK):
                            for a, b in ((0, w_hi), (1, w_hi), (0, w_lo)):
                                last = nc.tensor.matmul(ps_v[:, u % 4, :], s_in[:, u % RING, c, a, :], b[:, e, c, :],
                                                        start=(k == 0), stop=(k == 3 * CK - 1))
                                k += 1
                        last.then_inc(v_made, 1)
                    if live(t, u, TURN):
                        x, w = (t - 1) * UNITS + u - 1, (u - 1) % UNITS
                        pe.wait_ge(mixes, x + 3)
                        pe.wait_ge(t_lo, x + 1)
                        for c in range(CK):
                            last = nc.tensor.transpose(ps_t[:, w % 2, c, :], mixed[:, w % 2, c * P:(c + 1) * P], ident[:, :])
                        last.then_inc(turned, 1)
                    if live(t, u, OUT):
                        piece, before, tile, e, c = piece_of(t, u, OUT)
                        pe.wait_ge(t_lo, tile * UNITS + (e + 1) * N + 2)
                        pe.wait_ge(o_lo, piece + 1)
                        k = 0
                        for j in range(CK):
                            for a, b in ((w_hi, m_hi), (w_hi, m_lo), (w_lo, m_hi)):
                                last = nc.tensor.matmul(ps_o[:, c % 2, :, :], a[:, 2 + e, j, c * P:(c + 1) * P], b[:, e, j, :, :],
                                                        start=(k == 0), stop=(k == 3 * CK - 1))
                                k += 1
                        last.then_inc(o_made, 1)

            stages(nc.tensor.Fori, stage)

        @block.vector
        def _(dve):
            dve.sem_inc(evicted, 4)
            dve.sem_inc(mixes, 2)
            dve.sem_inc(t_lo, 2)
            dve.sem_inc(o_lo, 2)
            dve.wait_ge(consts_landed, 48)

            def stage(t, par):
                for u in range(UNITS):
                    if live(t, u, OUT_LO):
                        piece, before, tile, e, c = piece_of(t, u, OUT_LO)
                        dve.wait_ge(o_hi, piece + 1)
                        nc.vector.scalar_tensor_tensor(
                            staged[:, c % 2, 1, :, :].bitcast(F32R), ps_o[:, c % 2, :, :], o_bias[:, e, c:c + 1],
                            staged[:, c % 2, 0, :, :], ALU.add, ALU.subtract).then_inc(o_lo, 1)
                    if live(t, u, 0) and u == 0:
                        nc.vector.tensor_copy(w_tile[:, par:par + 1, :], w_soft[:, bass.ds(t, 1), :]).then_inc(w_picked, 1)
                    if live(t, u, MIX):
                        x = (t - 1) * UNITS + u
                        dve.wait_ge(pooled, x + 1)
                        nc.vector.tensor_tensor(prod[:, u % 2, 0:2, :], prod[:, u % 2, 0:2, :], prod[:, u % 2, 2:4, :],
                                                ALU.add).then_inc(halved, 1)
                    if live(t, u, 0):
                        dve.wait_ge(v_made, t * UNITS + u + 1 + RING)
                        nc.vector.tensor_tensor(v[:, par, u // N, u % N, :], ps_v[:, u % 4, :], bias[:, u // N, :],
                                                ALU.add).then_inc(evicted, 1)
                    if live(t, u, MIX):
                        dve.wait_ge(turned, x + 1)
                        dve.wait_ge(halved, x + 1)
                        nc.vector.tensor_tensor(mixed[:, u % 2, :], prod[:, u % 2, 0, :], prod[:, u % 2, 1, :],
                                                ALU.add).then_inc(mixes, 1)
                    if live(t, u, TURN):
                        x, w = (t - 1) * UNITS + u - 1, (u - 1) % UNITS
                        dve.wait_ge(t_hi, x + 1)
                        nc.vector.tensor_tensor(m_lo[:, w // N, :, w % N, :], ps_t[:, w % 2, :, :],
                                                m_hi[:, w // N, :, w % N, :].bitcast(F32),
                                                ALU.subtract).then_inc(t_lo, 1)

            stages(nc.vector.Fori, stage)

        @block.gpsimd
        def _(pool):
            def work(t, par):
                pool.wait_ge(w_picked, t + 1)
                for u in range(UNITS):
                    e, n = u // N, u % N
                    if n == 0:
                        pool.wait_ge(evicted, t * UNITS + (e + 1) * N + 4)
                    pool.wait_ge(mixes, t * UNITS + u + 1)
                    w = w_tile[:, par, n * N * HEADS:(n + 1) * N * HEADS]
                    nc.gpsimd.tensor_tensor(prod[:, u % 2, :, :].rearrange("p m (h d) -> p (m h) d", d=HD),
                                            v[:, par, e, :, :].rearrange("p m (h d) -> p (m h) d", d=HD),
                                            w.unsqueeze(2).broadcast_to([P, N * HEADS, HD]), ALU.mult).then_inc(pooled, 1)

            with nc.gpsimd.Fori(0, TILES // 2) as q:
                work(2 * q, 0)
                work(2 * q + 1, 1)



def superpose(nc, sem, dram, w_int, ids_t, tables, identity):
    with ExitStack() as ctx:
        def sb(name, shape, dt=F32):
            return ctx.enter_context(nc.sbuf_tensor(name, shape, dt))

        MATS, RING, Q = 2 * N, 4, 4
        w_hi = sb("int_w_hi", [P, MATS, CK, D], F32R)
        w_lo = sb("int_w_lo", [P, MATS, CK, D], F32R)
        a_in = sb("a_in", [P, RING, 2, 2, P], F32R)
        ri = sb("ri", [P, 2, 2, N, D])
        raw = ri[:, :, :, :, :].rearrange("p x e n d -> p (x e) n d")
        sq = sb("sq", [P, 2, 2, N, P])
        unit = sb("unit", [P, 2, 2, N, P])
        there = sb("there", [P, N, P])
        d = sb("d", [P, 6, P])
        d_part = sb("d_part", [P, 6, P])
        d_there = sb("d_there", [P, 6, P])
        c_sum = sb("c_sum", [P, N, P])
        sup = sb("sup_rows", [P, 2, 2, D])
        strength = sb("strength", [P, TILES, N, N])
        st = sb("strength_tile", [P, N, N])
        st_sum = sb("strength_sum", [P, N])
        ids = sb("ids_sb", [P, TILES, N], I32)
        ident = sb("ident3", [P, P])
        tiny = sb("tiny3", [P, 1])
        norm = sb("norm", [P, 2])
        ps = ctx.enter_context(nc.psum_tensor("ri_ps", [P, 2, 3, D], F32))
        ps_t = ctx.enter_context(nc.psum_tensor("sup_ps", [P, 2, CK, P], F32))
        w_landed = [sem(f"int_w_landed{i}") for i in range(4)]
        w_hi_made, w_lo_made = sem("int_w_hi_made"), sem("int_w_lo_made")
        consts_landed, gathered = sem("p3_consts_landed"), sem("gathered")
        a_landed = [sem(f"a_landed{i}") for i in range(RING)]
        a_used = sem("a_used")
        copied, ri_ready = sem("ri_copied"), sem("ri_ready")
        squares, mags, present = sem("sup_squares"), sem("mags"), sem("present")
        roots, guarded, inverted = sem("roots"), sem("guarded"), sem("inverted")
        units = sem("units")
        paired, met, parts, d_steps = sem("paired"), sem("met"), sem("d_parts"), sem("d_steps")
        mixing, c_made, products = sem("mixing"), sem("c_made"), sem("sup_products")
        folded, quarters = sem("folded"), sem("quarters")
        power, normed, sup_ready = sem("power"), sem("normed"), sem("sup_ready")
        sup_turned, sent = sem("sup_turned"), [sem(f"sup_sent{u}") for u in range(2)]
        out_copied, started = sem("sup_copied"), sem("c_started")
        picked, inv_norm = sem("picked"), sem("inv_norm")
        RUNS = ((0, 0, 1, 3), (3, 0, 2, 2), (5, 0, 3, 1))
        PAIR = {}
        for at, i0, j0, count in RUNS:
            for x in range(count):
                PAIR[i0 + x, j0 + x] = PAIR[j0 + x, i0 + x] = at + x

        def others(j):
            return [n for n in range(N) if n != j]

        block = ctx.enter_context(nc.Block())

        INVERT, MIX, TOTAL = 1, 2, 3

        def stages(fori, run):
            run(0, 0)
            run(0, 1)
            with fori(1, TILES // 2) as half:
                run(half, 0)
                run(half, 1)
            run(TILES // 2, 0)
            run(TILES // 2, 1)

        def live(t, p, lag):
            return not isinstance(t, int) or 0 <= t * Q - 2 + p - lag < TILES * Q

        def quarter(t, par, p, lag):
            back, q = divmod(p - 2 - lag, Q)
            return (t + back) * Q + q, t + back, (par + back) % 2, q

        def is_tile(t, back):
            return not isinstance(t, int) or 0 <= t - back < TILES

        @block.sync
        def _(sp):
            for u in range(2):
                sp.sem_inc(sent[u], 16)
            for m in range(2):
                sp.dma_start(raw[:, m, :, :], w_int[m, :, :, :].rearrange("c p o -> p c o")).then_inc(w_landed[m], 16)
            with nc.sync.Fori(0, TILES) as t:
                for i in range(4 * N):
                    n, e, cp = i // 4, i // 2 % 2, i % 2
                    sp.wait_ge(a_used, t * 4 * N + i + 1)
                    for cc in range(2):
                        src = dram["attn"][e, 2 * cp + cc][:, :, n, bass.ts(t, P)]
                        sp.dma_start(a_in[:, i % RING, cc, :, :].bitcast(F32),
                                     src.rearrange("a p b -> p a b")).then_inc(a_landed[i % RING], 16)

        @block.gpsimd
        def _(pool):
            pool.sem_inc(units, 4)
            nc.gpsimd.dma_start(ids[:, :, :], ids_t).then_inc(gathered, 16)
            pool.wait_ge(gathered, 16)
            for t in range(TILES):
                for i in range(N):
                    nc.gpsimd.indirect_dma_start(
                        strength[:, t, i, :], None, tables[i],
                        bass.IndirectOffsetOnAxis(ap=ids[:, t, i:i + 1].bitcast(U32), axis=0)).then_inc(gathered, 16)

            def magnitude(t, par, p):
                k, tile, tp, q = quarter(t, par, p, 0)
                pool.wait_ge(squares, k + 1)
                nc.gpsimd.tensor_tensor(sq[:, q % 2, 0, :, :], sq[:, q % 2, 0, :, :], sq[:, q % 2, 1, :, :],
                                        ALU.add).then_inc(mags, 1)

            def units_of(t, par, p):
                k, tile, tp, q = quarter(t, par, p, INVERT)
                pool.wait_ge(inverted, k + 1)
                pool.wait_ge(quarters, k + 1)
                for e in range(2):
                    nc.gpsimd.tensor_tensor(unit[:, q % 2, e, :, :], ri[:, tp, e, :, q * P:(q + 1) * P],
                                            sq[:, q % 2, 1, :, :], ALU.mult).then_inc(units, 1)

            def multiply_pairs(out, x, done):
                for at, i0, j0, count in RUNS:
                    nc.gpsimd.tensor_tensor(out[:, at:at + count, :], x[:, i0:i0 + count, :], x[:, j0:j0 + count, :],
                                            ALU.mult).then_inc(done, 1)

            def both_there(t, par, p):
                k, tile, tp, q = quarter(t, par, p, INVERT)
                pool.wait_ge(present, k + 1)
                if not (isinstance(k, int) and k == 0):
                    pool.wait_ge(d_steps, 2 * k)
                multiply_pairs(d_there, there, met)

            def pairs(t, par, p):
                k, tile, tp, q = quarter(t, par, p, MIX)
                pool.wait_ge(units, 2 * k + 2 + 4)
                pool.wait_ge(c_made, k + 2)
                multiply_pairs(d, unit[:, q % 2, 0], paired)

            def product(t, par, p):
                k, tile, tp, q = quarter(t, par, p, TOTAL)
                pool.wait_ge(c_made, k + 3)
                for e in range(2):
                    nc.gpsimd.tensor_tensor(unit[:, q % 2, e, :, :], ri[:, tp, e, :, q * P:(q + 1) * P], c_sum[:, :, :],
                                            ALU.mult).then_inc(products, 1)

            def stage(half, par):
                t = 2 * half + par
                for p in range(Q):
                    at = 3 if p == 2 else 2
                    steps = [(pairs, MIX), (product, TOTAL), (units_of, INVERT), (both_there, INVERT)]
                    steps.insert(at, (magnitude, 0))
                    for step, lag in steps:
                        if live(t, p, lag):
                            step(t, par, p)

            stages(nc.gpsimd.Fori, stage)

        @block.scalar
        def _(act):
            for m in range(MATS):
                act.wait_ge(w_landed[m % 4], 16 * (m // 4 + 1))
                nc.scalar.activation(w_hi[:, m, :, :], raw[:, m % 4, :, :], ACT.Copy).then_inc(w_hi_made, 1)
                if m == 0:
                    for later in range(2, 4):
                        act.dma_start(raw[:, later, :, :], w_int[later, :, :, :].rearrange("c p o -> p c o")
                                      ).then_inc(w_landed[later], 16)
                    act.dma_start(ident[:, :], identity).then_inc(consts_landed, 16)
                if 1 <= m <= MATS - 4:
                    act.wait_ge(w_lo_made, m)
                    act.dma_start(raw[:, m - 1, :, :], w_int[m + 3, :, :, :].rearrange("c p o -> p c o")
                                  ).then_inc(w_landed[m - 1], 16)

            def copy(t, par, n):
                if n == 0:
                    if isinstance(t, int) and t < 2:
                        act.wait_ge(w_lo_made, MATS)
                    else:
                        act.wait_ge(products, (t - 1) * Q * 2 + 1)
                act.wait_ge(a_used, t * 4 * N + 4 * n + 4 + RING)
                for e in range(2):
                    nc.scalar.activation(ri[:, par, e, n, :], ps[:, n % 2, 2 * e, :], ACT.Copy).then_inc(copied, 1)

            def square(t, par, p):
                k, tile, tp, q = quarter(t, par, p, 0)
                act.wait_ge(ri_ready, tile * N + N + 2)
                act.wait_ge(units, 2 * k + 2)
                if not (isinstance(k, int) and k < 2):
                    act.wait_ge(present, k - 1)
                nc.scalar.activation(sq[:, q % 2, :, :, :].rearrange("p e n d -> p (e n) d"),
                                     ri[:, tp, :, :, q * P:(q + 1) * P].rearrange("p e n d -> p (e n) d"),
                                     ACT.Square).then_inc(squares, 1)

            def root(t, par, p):
                k, tile, tp, q = quarter(t, par, p, 0)
                act.wait_ge(mags, k + 1)
                nc.scalar.activation(sq[:, q % 2, 1, :, :], sq[:, q % 2, 0, :, :], ACT.Sqrt).then_inc(roots, 1)

            def start_mix(t, par, p):
                k, tile, tp, q = quarter(t, par, p, MIX)
                act.wait_ge(d_steps, k * 2 + 2)
                act.wait_ge(products, k * 2 + 1)
                for j in range(N):
                    i = others(j)[0]
                    nc.scalar.activation(c_sum[:, j, :], d[:, PAIR[i, j], :], ACT.Identity, bias=st_sum[:, j:j + 1],
                                         scale=st[:, i, j:j + 1]).then_inc(started, 1)

            def send(tile, par):
                act.wait_ge(sup_turned, tile + 3)
                nc.scalar.activation(sup[:, par, :, :].rearrange("p e d -> p (e d)"),
                                     ps_t[:, :, :, :].rearrange("p e c b -> p (e c b)"), ACT.Copy).then_inc(out_copied, 1)
                act.wait_ge(out_copied, tile + 1)
                act.dma_start(dram["sup"][:, :, bass.ts(tile, P)].rearrange("c p b -> p c b"),
                              sup[:, par, :, :].rearrange("p e (c b) -> p (e c) b", b=P)).then_inc(sent[par], 16)

            def stage(half, par):
                t = 2 * half + par
                for p in range(Q):
                    if p == 0:
                        if live(t, p, 0):
                            square(t, par, p)
                        if is_tile(t, 0):
                            copy(t, par, 0)
                            copy(t, par, 1)
                        if live(t, p, 0):
                            root(t, par, p)
                        if live(t, p, MIX):
                            start_mix(t, par, p)
                    elif p == 2:
                        if is_tile(t, 0):
                            copy(t, par, 3)
                        if live(t, p, MIX):
                            start_mix(t, par, p)
                        if live(t, p, 0):
                            square(t, par, p)
                            root(t, par, p)
                    else:
                        if live(t, p, 0):
                            square(t, par, p)
                            root(t, par, p)
                        if live(t, p, MIX):
                            start_mix(t, par, p)
                    if p == 1 and is_tile(t, 2):
                        act.wait_ge(power, 3 * (t - 1))
                        nc.scalar.activation(norm[:, 1:2], norm[:, 0:1], ACT.Sqrt, bias=tiny[:, :]).then_inc(normed, 1)
                    if p == 1 and is_tile(t, 0):
                        copy(t, par, 2)
                    if p == 3 and is_tile(t, 2):
                        send(t - 2, par)

            stages(nc.scalar.Fori, stage)
            for u in range(2):
                act.wait_ge(sent[u], 16 * (TILES // 2 + 1))

        @block.tensor
        def _(pe):
            pe.sem_inc(a_used, RING)
            pe.sem_inc(sup_turned, 2)

            def turn(t, par):
                pe.wait_ge(consts_landed, 16)
                pe.wait_ge(sup_ready, t + 1)
                for i in range(2 * CK):
                    last = nc.tensor.transpose(ps_t[:, i // CK, i % CK, :], sup[:, par, i // CK, i % CK * P:(i % CK + 1) * P],
                                               ident[:, :])
                last.then_inc(sup_turned, 1)

            def maps(t, par, before=None):
                for i in range(4 * N):
                    if i == 4 and before is not None:
                        turn(before, 1 - par)
                    n, e, cp = i // 4, i // 2 % 2, i % 2
                    pe.wait_ge(a_landed[i % RING], 32 * (t * N + i // RING + 1))
                    pe.wait_ge(w_lo_made, 2 * n + 2)
                    if e == 0 and cp == 0:
                        pe.wait_ge(ri_ready, t * N + n + 1)
                    for to, m in ((e, e), (2, 1 - e)):
                        k = 0
                        for cc in range(2):
                            for a, b in ((0, w_hi), (1, w_hi), (0, w_lo)):
                                first = cp == 0 and k == 0 and (to < 2 or e == 0)
                                final = cp == 1 and k == 5 and (to < 2 or e == 1)
                                last = nc.tensor.matmul(ps[:, n % 2, (0, 1, 2)[to], :], a_in[:, i % RING, cc, a, :],
                                                        b[:, 2 * n + m, 2 * cp + cc, :], start=first, stop=final)
                                k += 1
                    last.then_inc(a_used, 1)

            maps(0, 0)
            maps(1, 1)
            maps(2, 0)
            maps(3, 1, before=0)
            with nc.tensor.Fori(2, TILES // 2) as q:
                maps(2 * q, 0, before=2 * q - 3)
                maps(2 * q + 1, 1, before=2 * q - 2)
            for t in range(TILES - 3, TILES):
                turn(t, t % 2)

        @block.vector
        def _(dve):
            dve.sem_inc(ri_ready, 2)
            dve.sem_inc(quarters, 2)
            dve.sem_inc(c_made, 2)
            dve.sem_inc(products, 1)
            nc.vector.memset(tiny[:, :], 1e-8)
            for m in range(MATS):
                dve.wait_ge(w_hi_made, m + 1)
                nc.vector.tensor_tensor(w_lo[:, m, :, :], raw[:, m % 4, :, :], w_hi[:, m, :, :].bitcast(F32),
                                        ALU.subtract).then_inc(w_lo_made, 1)
            MIXING = N * (N - 2) - 1

            def finish(t, par, n):
                dve.wait_ge(copied, 2 * (t * N + n) + 2)
                nc.vector.tensor_tensor(ri[:, par, 0, n, :], ri[:, par, 0, n, :], ps[:, n % 2, 1, :],
                                        ALU.subtract).then_inc(ri_ready, 1)

            def invert(t, par, p):
                k, tile, tp, q = quarter(t, par, p, INVERT)
                b = q % 2
                dve.wait_ge(roots, k + 1)
                nc.vector.tensor_scalar(sq[:, b, 1, :, :], sq[:, b, 1, :, :], 1e-30, None, ALU.max).then_inc(guarded, 1)
                dve.wait_ge(guarded, k + 1)
                nc.vector.reciprocal(sq[:, b, 1, :, :], sq[:, b, 1, :, :]).then_inc(inverted, 1)
                if not (isinstance(k, int) and k == 0):
                    dve.wait_ge(met, 3 * k)
                nc.vector.tensor_scalar(there[:, :, :], sq[:, b, 0, :, :], 0.0, None, ALU.is_gt).then_inc(present, 1)

            def pick(tile):
                nc.vector.tensor_copy(st[:, :, :], strength[:, bass.ds(tile, 1), :, :].rearrange("p t i j -> p (t i) j")
                                      ).then_inc(picked, 1)
                dve.wait_ge(picked, 2 * tile + 1)
                nc.vector.tensor_reduce(st_sum[:, :], st[:, :, :].rearrange("p i j -> p j i"), AX_X,
                                        ALU.add).then_inc(picked, 1)
                dve.wait_ge(picked, 2 * tile + 2)

            def parts_of(t, par, p):
                k, tile, tp, q = quarter(t, par, p, MIX)
                dve.wait_ge(units, 2 * k + 2 + 4)
                if not (isinstance(k, int) and k == 0):
                    dve.wait_ge(d_steps, k * 2)
                for at, i0, j0, count in RUNS:
                    nc.vector.tensor_tensor(d_part[:, at:at + count, :], unit[:, q % 2, 1, i0:i0 + count, :],
                                            unit[:, q % 2, 1, j0:j0 + count, :], ALU.mult).then_inc(parts, 1)

            def join(t, par, p):
                k, tile, tp, q = quarter(t, par, p, MIX)
                dve.wait_ge(parts, k * 3 + 3)
                dve.wait_ge(paired, 3 * k + 3)
                dve.wait_ge(met, 3 * k + 3)
                nc.vector.tensor_tensor(d[:, :, :], d[:, :, :], d_part[:, :, :], ALU.add).then_inc(d_steps, 1)
                dve.wait_ge(d_steps, k * 2 + 1)
                nc.vector.tensor_tensor(d[:, :, :], d[:, :, :], d_there[:, :, :], ALU.subtract).then_inc(d_steps, 1)

            def mix(t, par, p):
                k, tile, tp, q = quarter(t, par, p, MIX)
                for x in range(1, N - 1):
                    for j in range(N):
                        i, out = others(j)[x], c_sum[:, j, :]
                        if x == 1:
                            dve.wait_ge(started, k * N + j + 1)
                        else:
                            dve.wait_ge(mixing, k * MIXING + (x - 2) * N + j + 1)
                        nc.vector.scalar_tensor_tensor(out, d[:, PAIR[i, j], :], st[:, i, j:j + 1], out, ALU.mult,
                                                       ALU.add).then_inc(c_made if x == N - 2 and j == N - 1 else mixing, 1)

            def fold(t, par, p):
                k, tile, tp, q = quarter(t, par, p, TOTAL)
                dve.wait_ge(products, 2 * k + 3)
                u = unit[:, q % 2, 0:2, :, :]
                nc.vector.tensor_tensor(u[:, :, 0:2, :], u[:, :, 0:2, :], u[:, :, 2:4, :], ALU.add).then_inc(folded, 1)

            def total(t, par, p, half):
                k, tile, tp, q = quarter(t, par, p, TOTAL)
                u = unit[:, q % 2, 0:2, :, :]
                if q == 0:
                    dve.wait_ge(sent[tp], 16 * (half + par))
                dve.wait_ge(folded, k + 1)
                nc.vector.tensor_tensor(sup[:, tp, :, q * P:(q + 1) * P], u[:, :, 0, :], u[:, :, 1, :],
                                        ALU.add).then_inc(quarters, 1)

            def sum_squares(tile, par):
                dve.wait_ge(quarters, tile * Q + Q + 2)
                if not isinstance(tile, int) or tile < TILES - 1:
                    dve.wait_ge(d_steps, (tile * Q + Q + 1) * 2 + 2)
                waste = d_part[:, 0:N, :].rearrange("p n d -> p (n d)")
                for e in range(2):
                    nc.vector.tensor_tensor_reduce(out=waste, in0=sup[:, par, e, :], in1=sup[:, par, e, :], scale=1.0,
                                                   scalar=0.0, op0=ALU.mult, op1=ALU.add,
                                                   accum_out=norm[:, e:e + 1]).then_inc(power, 1)
                    dve.wait_ge(power, 3 * tile + 1 + e)
                nc.vector.tensor_tensor(norm[:, 0:1], norm[:, 0:1], norm[:, 1:2], ALU.add).then_inc(power, 1)

            def normalize(tile, par):
                flat = sup[:, par, :, :].rearrange("p e d -> p (e d)")
                dve.wait_ge(normed, tile + 1)
                nc.vector.reciprocal(norm[:, 1:2], norm[:, 1:2]).then_inc(inv_norm, 1)
                dve.wait_ge(inv_norm, tile + 1)
                nc.vector.tensor_scalar(flat, flat, norm[:, 1:2], None, ALU.mult).then_inc(sup_ready, 1)

            def stage(half, par):
                t = 2 * half + par
                for p in range(Q):
                    if live(t, p, INVERT):
                        invert(t, par, p)
                    if p == 0 and is_tile(t, 1):
                        if isinstance(t, int) and t == 1:
                            dve.wait_ge(gathered, 16 * (1 + TILES * N))
                        pick(t - 1)
                    if live(t, p, MIX):
                        parts_of(t, par, p)
                        join(t, par, p)
                    if live(t, p, TOTAL):
                        fold(t, par, p)
                        total(t, par, p, half)
                    if p in (0, 2) and is_tile(t, 0):
                        finish(t, par, 3 if p else 0)
                    if p == 1 and is_tile(t, 2):
                        sum_squares(t - 2, par)
                    if live(t, p, MIX):
                        mix(t, par, p)
                    if p == 1 and is_tile(t, 2):
                        normalize(t - 2, par)
                    if p < 2 and is_tile(t, 0):
                        finish(t, par, 1 + p)

            stages(nc.vector.Fori, stage)



def towers(nc, sem, dram, w_tail, w_top2, w_top3, tail_cols, y):
    with ExitStack() as ctx:
        def sb(name, shape, dt=F32):
            return ctx.enter_context(nc.sbuf_tensor(name, shape, dt))

        HALVES, BH = 2, BATCH // 2
        UNITS = HALVES * CK
        PLACE = (0, 1, 2, 0, 1)
        w_raw = sb("tail_w_raw", [P, 2, CK, D])
        w_hi, w_lo = sb("tail_w_hi", [P, 3, CK, D], F32R), sb("tail_w_lo", [P, 3, CK, D], F32R)
        w3 = sb("w_top3", [P, 2])
        cols = sb("tail_columns", [P, 5, CK])
        rows = sb("rows", [P, 2 * CK, BH])
        x_hi = sb("tail_x_hi", [P, HALVES, 2 * CK, BH], F32R)
        x_lo = sb("tail_x_lo", [P, HALVES, 2 * CK, BH], F32R)
        amp_hi, amp_lo = sb("amp_hi", [P, HALVES, CK, BH], F32R), sb("amp_lo", [P, HALVES, CK, BH], F32R)
        real, imag = sb("real", [P, 2, BH]), sb("imag", [P, 2, BH])
        colsum = sb("tail_colsum", [P, HALVES, BH])
        mean_w, eps = sb("tail_mean_w", [P, P]), sb("tail_eps", [P, 1])
        y_sb = sb("y_row", [1, HALVES, BH])
        ps = ctx.enter_context(nc.psum_tensor("tail_ps", [P, 8, BH], F32))
        top_x = w_raw

        names = """wt_landed0 wt_landed1 wt_hi wt_lo tail_cols_landed tail_consts sup_landed0 sup_landed1 xs_hi xs_lo
            m_made m_copied m_real m_squared m_power m_amp m_hi m_lo
            p_made p_out p_sum stat1 p_centred p_squared p_sum2 stat2 p_std p_rstd p_scaled p_gelu z_hi z_lo
            top_x_landed t1_made t1_sum t1_relu t1_hi t1_lo t2_made t2_relu t3_made y_copied y_sent"""
        s = {n: sem("tail_" + n) for n in names.split()}
        wt_landed = [s["wt_landed0"], s["wt_landed1"]]
        sup_landed = [s["sup_landed0"], s["sup_landed1"]]
        block = ctx.enter_context(nc.Block())

        def unit(i):
            return i // CK, i % CK

        post_out = rows[:, :, :].rearrange("p (h c) b -> p h c b", h=HALVES)
        z_hi, z_lo = x_hi[:, :, 0:CK, :], x_lo[:, :, 0:CK, :]
        t1_hi, t1_lo = x_hi[:, :, CK:2 * CK, :], x_lo[:, :, CK:2 * CK, :]
        t2 = rows[:, 0:2 * HALVES, :].rearrange("p (h c) b -> p h c b", h=HALVES)

        def width(m):
            return TOP2 if m == 4 else D

        @block.sync
        def _(sp):
            def load_sup(h, e):
                sp.dma_start(rows[:, e * CK:(e + 1) * CK, :],
                             dram["sup"][e * CK:(e + 1) * CK, :, h * BH:(h + 1) * BH].rearrange("c p b -> p c b")
                             ).then_inc(sup_landed[e], 16)

            def load_w(m):
                src = w_top2 if m == 4 else w_tail[m]
                sp.dma_start(w_raw[:, m % 2, :, 0:width(m)], src.rearrange("c p o -> p c o")).then_inc(wt_landed[m % 2], 16)

            load_w(0), load_sup(0, 0), load_sup(0, 1), load_w(1)
            sp.dma_start(cols[:, :, :], tail_cols).then_inc(s["tail_cols_landed"], 16)
            sp.dma_start(w3[:, :], w_top3).then_inc(s["tail_cols_landed"], 16)
            for e in range(2):
                sp.wait_ge(s["xs_lo"], e + 1)
                load_sup(1, e)
            for m in range(2, 5):
                sp.wait_ge(s["wt_lo"], m - 1)
                load_w(m)
            sp.wait_ge(s["wt_lo"], 5)
            for h in range(HALVES):
                sp.dma_start(top_x[:, h, :, :], dram["top_x"][:, :, h * BH:(h + 1) * BH].rearrange("c p b -> p c b")
                             ).then_inc(s["top_x_landed"], 16)
            for h in range(HALVES):
                sp.wait_ge(s["y_copied"], h + 1)
                sp.dma_start(y[:, h * BH:(h + 1) * BH], y_sb[:, h, :]).then_inc(s["y_sent"], 16)
            sp.wait_ge(s["y_sent"], 16 * HALVES)

        @block.tensor
        def _(pe):
            def products(out, w_place, k_parts, moving, c, h, first=True, last=True):
                b_hi, b_lo = moving
                n = 0
                for k in range(CK):
                    for a, b in ((w_hi, b_hi), (w_hi, b_lo), (w_lo, b_hi)):
                        ins = nc.tensor.matmul(out, a[:, w_place, k, c * P:(c + 1) * P], b[:, h, k_parts + k, :],
                                               start=first and n == 0, stop=last and n == 3 * CK - 1)
                        n += 1
                return ins

            sup = (x_hi, x_lo)
            for i in range(UNITS):
                h, c = unit(i)
                pe.wait_ge(s["xs_lo"], 2 * h + 1)
                pe.wait_ge(s["wt_lo"], 1)
                b = 3 * (i % 2)
                if i >= 2:
                    pe.wait_ge(s["m_squared"], i - 1)
                products(ps[:, b, :], 0, 0, sup, c, h)
                pe.wait_ge(s["xs_lo"], 2 * h + 2)
                products(ps[:, b + 2, :], 0, CK, sup, c, h, last=False)
                pe.wait_ge(s["wt_lo"], 2)
                products(ps[:, b + 1, :], 1, CK, sup, c, h)
                products(ps[:, b + 2, :], 1, 0, sup, c, h, first=False).then_inc(s["m_made"], 1)
            for i in range(UNITS):
                h, c = unit(i)
                pe.wait_ge(s["m_lo"], h * CK + CK)
                pe.wait_ge(s["wt_lo"], 3)
                if i >= 2:
                    pe.wait_ge(s["p_out"], i - 1)
                products(ps[:, 6 + i % 2, :], 2, 0, (amp_hi, amp_lo), c, h).then_inc(s["p_made"], 1)
            pe.wait_ge(s["tail_consts"], 2)
            pe.wait_ge(s["m_squared"], UNITS)
            for name, bank, source in (("stat1", 0, "p_sum"), ("stat2", 2, "p_sum2")):
                for h in range(HALVES):
                    pe.wait_ge(s[source], (h + 1) * CK)
                    nc.tensor.matmul(ps[:, bank + h, :], mean_w[:, :], colsum[:, h, :], start=True, stop=True).then_inc(s[name], 1)
            for i in range(UNITS):
                h, c = unit(i)
                pe.wait_ge(s["z_lo"], h * CK + CK)
                pe.wait_ge(s["wt_lo"], 4)
                if i >= 2:
                    pe.wait_ge(s["t1_sum"], i - 1)
                products(ps[:, 4 + i % 2, :], 0, 0, (x_hi, x_lo), c, h).then_inc(s["t1_made"], 1)
            for i in range(2 * HALVES):
                h, c = i // 2, i % 2
                pe.wait_ge(s["t1_lo"], h * CK + CK)
                pe.wait_ge(s["wt_lo"], 5)
                pe.wait_ge(s["p_out"], UNITS)
                if i >= 2:
                    pe.wait_ge(s["t2_relu"], i - 1)
                products(ps[:, 6 + i % 2, :], 1, CK, (x_hi, x_lo), c, h).then_inc(s["t2_made"], 1)
            for h in range(HALVES):
                pe.wait_ge(s["t2_relu"], 2 * h + 2)
                pe.wait_ge(s["p_centred"], UNITS)
                for k in range(2):
                    ins = nc.tensor.matmul(ps[0:1, h, :], w3[:, k:k + 1], t2[:, h, k, :], start=(k == 0), stop=(k == 1))
                ins.then_inc(s["t3_made"], 1)

        def lagged(count, *steps):
            for i in range(count + len(steps) - 1):
                for lag, step in enumerate(steps):
                    if 0 <= i - lag < count:
                        step(i - lag)

        @block.scalar
        def _(act):
            def split_w(m):
                if m >= 3:
                    act.wait_ge(s["m_made"], UNITS)
                act.wait_ge(wt_landed[m % 2], 16 * (m // 2 + 1))
                w = width(m)
                nc.scalar.activation(w_hi[:, PLACE[m], :, 0:w], w_raw[:, m % 2, :, 0:w], ACT.Copy).then_inc(s["wt_hi"], 1)

            def split_x(h, e):
                act.wait_ge(sup_landed[e], 16 * (h + 1))
                part = slice(e * CK, (e + 1) * CK)
                nc.scalar.activation(x_hi[:, h, part, :], rows[:, part, :], ACT.Copy).then_inc(s["xs_hi"], 1)

            split_w(0), split_x(0, 0), split_x(0, 1), split_w(1), split_x(1, 0), split_x(1, 1), split_w(2)

            def copy(i):
                act.wait_ge(s["m_made"], i + 1)
                if i >= 2:
                    act.wait_ge(s["m_lo"], i - 1)
                nc.scalar.activation(real[:, i % 2, :], ps[:, 3 * (i % 2), :], ACT.Copy).then_inc(s["m_copied"], 1)

            def square(i):
                nc.scalar.activation(imag[:, i % 2, :], ps[:, 3 * (i % 2) + 2, :], ACT.Square)
                act.wait_ge(s["m_real"], i + 1)
                nc.scalar.activation(real[:, i % 2, :], real[:, i % 2, :], ACT.Square).then_inc(s["m_squared"], 1)

            def root(i):
                act.wait_ge(s["m_power"], i + 1)
                nc.scalar.activation(real[:, i % 2, :], real[:, i % 2, :], ACT.Sqrt).then_inc(s["m_amp"], 1)
                act.wait_ge(s["m_amp"], i + 1)
                nc.scalar.activation(amp_hi[:, i // CK, i % CK, :], real[:, i % 2, :], ACT.Copy).then_inc(s["m_hi"], 1)

            for i in range(UNITS):
                copy(i), square(i), root(i)
            split_w(3), split_w(4)
            act.wait_ge(s["tail_cols_landed"], 32)

            def bias(i):
                h, c = unit(i)
                act.wait_ge(s["p_made"], i + 1)
                nc.scalar.activation(post_out[:, h, c, :], ps[:, 6 + i % 2, :], ACT.Identity,
                                     bias=cols[:, 0, c:c + 1]).then_inc(s["p_out"], 1)

            for i in range(UNITS):
                bias(i)
            for i in range(UNITS):
                act.wait_ge(s["p_centred"], i + 1)
                if i >= 2:
                    act.wait_ge(s["p_sum2"], i - 1)
                nc.scalar.activation(real[:, i % 2, :], post_out[:, i // CK, i % CK, :], ACT.Square).then_inc(s["p_squared"], 1)
            act.wait_ge(s["p_sum2"], UNITS)
            for h in range(HALVES):
                act.wait_ge(s["stat2"], h + 1)
                nc.scalar.activation(imag[:, h, :], ps[:, 2 + h, :], ACT.Sqrt, bias=eps[:, :]).then_inc(s["p_std"], 1)

            def gelu(i):
                h, c = unit(i)
                act.wait_ge(s["p_scaled"], i + 1)
                nc.scalar.activation(post_out[:, h, c, :], post_out[:, h, c, :], ACT.Gelu, bias=cols[:, 2, c:c + 1],
                                     scale=cols[:, 1, c:c + 1]).then_inc(s["p_gelu"], 1)

            def split_z(i):
                h, c = unit(i)
                act.wait_ge(s["p_gelu"], i + 1)
                nc.scalar.activation(z_hi[:, h, c, :], post_out[:, h, c, :], ACT.Copy).then_inc(s["z_hi"], 1)

            lagged(UNITS, gelu, split_z)

            def relu(i):
                h, c = unit(i)
                act.wait_ge(s["t1_sum"], i + 1)
                nc.scalar.activation(top_x[:, h, c, :], top_x[:, h, c, :], ACT.Relu, bias=cols[:, 3, c:c + 1]).then_inc(s["t1_relu"], 1)

            def split_t(i):
                h, c = unit(i)
                act.wait_ge(s["t1_relu"], i + 1)
                nc.scalar.activation(t1_hi[:, h, c, :], top_x[:, h, c, :], ACT.Copy).then_inc(s["t1_hi"], 1)

            lagged(UNITS, relu, split_t)
            act.wait_ge(s["p_made"], UNITS)
            for i in range(2 * HALVES):
                act.wait_ge(s["t2_made"], i + 1)
                nc.scalar.activation(t2[:, i // 2, i % 2, :], ps[:, 6 + i % 2, :], ACT.Relu,
                                     bias=cols[:, 4, i % 2:i % 2 + 1]).then_inc(s["t2_relu"], 1)
            for h in range(HALVES):
                act.wait_ge(s["t3_made"], h + 1)
                nc.scalar.activation(y_sb[:, h, :], ps[0:1, h, :], ACT.Copy).then_inc(s["y_copied"], 1)

        @block.vector
        def _(dve):
            nc.vector.memset(mean_w[:, :], 1.0 / OUT).then_inc(s["tail_consts"], 1)
            nc.vector.memset(eps[:, :], EPS).then_inc(s["tail_consts"], 1)

            def minus(out, a, b, done):
                nc.vector.tensor_tensor(out, a, b.bitcast(F32), ALU.subtract).then_inc(s[done], 1)

            def split_w(m):
                dve.wait_ge(s["wt_hi"], m + 1)
                w = width(m)
                minus(w_lo[:, PLACE[m], :, 0:w], w_raw[:, m % 2, :, 0:w], w_hi[:, PLACE[m], :, 0:w], "wt_lo")

            def split_x(h, e):
                dve.wait_ge(s["xs_hi"], 2 * h + e + 1)
                part = slice(e * CK, (e + 1) * CK)
                minus(x_lo[:, h, part, :], rows[:, part, :], x_hi[:, h, part, :], "xs_lo")

            split_w(0), split_x(0, 0), split_x(0, 1), split_w(1), split_x(1, 0), split_x(1, 1), split_w(2)
            for i in range(UNITS):
                b = 3 * (i % 2)
                dve.wait_ge(s["m_copied"], i + 1)
                nc.vector.tensor_tensor(real[:, i % 2, :], real[:, i % 2, :], ps[:, b + 1, :], ALU.subtract).then_inc(s["m_real"], 1)
                dve.wait_ge(s["m_squared"], i + 1)
                nc.vector.tensor_tensor(real[:, i % 2, :], real[:, i % 2, :], imag[:, i % 2, :], ALU.add).then_inc(s["m_power"], 1)
                dve.wait_ge(s["m_hi"], i + 1)
                minus(amp_lo[:, i // CK, i % CK, :], real[:, i % 2, :], amp_hi[:, i // CK, i % CK, :], "m_lo")
            split_w(3), split_w(4)

            def summed(i, src, name):
                h, c = unit(i)
                if c == 0:
                    ins = nc.vector.tensor_copy(colsum[:, h, :], src)
                else:
                    dve.wait_ge(s[name], i)
                    ins = nc.vector.tensor_tensor(colsum[:, h, :], colsum[:, h, :], src, ALU.add)
                ins.then_inc(s[name], 1)

            for i in range(UNITS):
                dve.wait_ge(s["p_out"], i + 1)
                summed(i, post_out[:, i // CK, i % CK, :], "p_sum")
            for h in range(HALVES):
                dve.wait_ge(s["stat1"], h + 1)
                for c in range(CK):
                    nc.vector.tensor_tensor(post_out[:, h, c, :], post_out[:, h, c, :], ps[:, h, :],
                                            ALU.subtract).then_inc(s["p_centred"], 1)
            for i in range(UNITS):
                dve.wait_ge(s["p_squared"], i + 1)
                summed(i, real[:, i % 2, :], "p_sum2")
            for h in range(HALVES):
                dve.wait_ge(s["p_std"], h + 1)
                nc.vector.reciprocal(imag[:, h, :], imag[:, h, :]).then_inc(s["p_rstd"], 1)
                dve.wait_ge(s["p_rstd"], h + 1)
                for c in range(CK):
                    nc.vector.tensor_tensor(post_out[:, h, c, :], post_out[:, h, c, :], imag[:, h, :],
                                            ALU.mult).then_inc(s["p_scaled"], 1)
            for i in range(UNITS):
                h, c = unit(i)
                dve.wait_ge(s["z_hi"], i + 1)
                minus(z_lo[:, h, c, :], post_out[:, h, c, :], z_hi[:, h, c, :], "z_lo")
            dve.wait_ge(s["top_x_landed"], 16 * HALVES)

            def add_x(i):
                h, c = unit(i)
                dve.wait_ge(s["t1_made"], i + 1)
                nc.vector.tensor_tensor(top_x[:, h, c, :], top_x[:, h, c, :], ps[:, 4 + i % 2, :], ALU.add).then_inc(s["t1_sum"], 1)

            def split_t(i):
                h, c = unit(i)
                dve.wait_ge(s["t1_hi"], i + 1)
                minus(t1_lo[:, h, c, :], top_x[:, h, c, :], t1_hi[:, h, c, :], "t1_lo")

            lagged(UNITS, add_x, split_t)


def tower(nc, a, y):
    with ExitStack() as ctx:
        def sem(name):
            return ctx.enter_context(nc.semaphore(name))

        def scratch(name, shape):
            return nc.dram_tensor(name, shape, F32, kind="Internal").ap()

        dram = {
            "s": scratch("encoded", [2 * N * CK, 2, P, BATCH]),
            "top_x": scratch("top_x", [CK, P, BATCH]),
            "attn": scratch("attended", [2, CK, 2, P, N, BATCH]),
            "sup": scratch("superposed", [2 * CK, P, BATCH]),
        }
        with nc.sbuf_tensor("moving_hi", [P, IN // P, 512], F32R) as x_hi, \
                nc.sbuf_tensor("moving_lo", [P, IN // P, 512], F32R) as x_lo:
            encoders(nc, sem, dram, a["w_stream"], a["x_stream"], a["enc_cols"], x_hi, x_lo)
            w_hi, w_lo = (x[:, :, :].rearrange("p (m c) o -> p m c o", c=CK) for x in (x_hi, x_lo))
            attention(nc, sem, dram, a["w_proj"], a["bias_rows"], a["out_cols"], a["identity"], w_hi, w_lo)
        superpose(nc, sem, dram, a["w_int"], a["ids_t"], [a[f"tbl_{i}"] for i in range(N)], a["identity"])
        towers(nc, sem, dram, a["w_tail"], a["w_top2"], a["w_top3"], a["tail_cols"], y)


def lay_out(np, i):
    L = {k[len("L0_rec_"):]: np.asarray(v) for k, v in i.items() if k.startswith("L0_rec_")}
    top1, top2, top3 = (np.asarray(i[f"W_top{n}"]) for n in (1, 2, 3))

    def stream(w):
        return w.reshape(w.shape[0] // (2 * P), 2, P, w.shape[1] // 512, 512).transpose(3, 0, 2, 1, 4)

    def chunks(w):
        return w.reshape(w.shape[0] // P, P, w.shape[1])

    def columns(v):
        return v.reshape(-1, P).T

    w_stream = np.concatenate([stream(w) for w in (L["er_W1"].T, top1[OUT:], L["ei_W1"].T, L["er_W2"].T, L["ei_W2"].T)])
    proj = np.stack([chunks(L[f"W{n}_{e}"].T) for n in "qkvo" for e in "ri"])
    x_parts = np.asarray(i["r_x"]).T.reshape(IN // (4 * P), 4, P, 2, 512)
    b_top2 = np.concatenate([np.asarray(i["b_top2"]), np.zeros(D - TOP2, np.float32)])
    out = {
        "w_stream": np.concatenate([w_stream, w_stream[:1]]).reshape(-1, P, 2, 512)[:w_stream.size // (P * 1024) + 2],
        "x_stream": np.concatenate([x_parts.transpose(3, 0, 2, 1, 4).reshape(-1, P, 4, 512),
                                    proj[:4].transpose(0, 2, 1, 3)]),
        "enc_cols": np.stack([np.stack([columns(L[e + n]) for n in ("_b1", "_g1", "_be1", "_b2")], 1) for e in ("er", "ei")], 1),
        "w_proj": proj[4:],
        "bias_rows": np.stack([L[f"b{n}_{e}"] for n in "qkv" for e in "ri"]),
        "out_cols": np.stack([columns(L[f"bo_{e}"]) for e in "ri"], 1),
        "identity": np.eye(P, dtype=np.float32),
        "w_int": np.stack([chunks(L[f"int_W{e}"][n].T) for n in range(N) for e in "ri"]),
        "ids_t": np.asarray(i["ids"]).reshape(TILES, P, N).transpose(1, 0, 2),
        "w_tail": np.stack([chunks(w) for w in (L["meas_Mr"].T, L["meas_Mi"].T, L["post_W"].T, top1[:OUT])]),
        "w_top2": chunks(top2),
        "w_top3": columns(top3.reshape(-1)),
        "tail_cols": np.stack([columns(v) for v in (L["post_b"], L["post_g"], L["post_be"], np.asarray(i["b_top1"]), b_top2)], 1),
    }
    out.update({f"tbl_{n}": np.asarray(i[f"tbl_{n}"]) for n in range(N)})
    return {k: np.ascontiguousarray(v) for k, v in out.items()}


def kernel(**inputs):
    import numpy as np
    import concourse.bacc as bacc
    from concourse.bass_utils import run_bass_kernel_spmd

    nc = bacc.Bacc("TRN2", target_bir_lowering=False, num_devices=1)
    arrays = {f"in_{k}": v for k, v in lay_out(np, inputs).items()}
    a = {k[3:]: nc.dram_tensor(k, v.shape, mybir.dt.from_np(v.dtype), kind="ExternalInput").ap() for k, v in arrays.items()}
    y = nc.dram_tensor("y_out", (1, BATCH), F32, kind="ExternalOutput").ap()
    tower(nc, a, y)
    r = run_bass_kernel_spmd(nc, [arrays], core_ids=[0])
    return r.results[0]["y_out"].reshape(BATCH, 1)
```
